# Optimizing a Trainium2 kernel written in Bass

```python
import numpy as np
import jax
import jax.numpy as jnp

def _softmax(x, axis=-1):
    return jax.nn.softmax(x, axis=axis)

def _gelu(x):
    return jax.nn.gelu(x, approximate=True)

def _silu(x):
    return jax.nn.silu(x)

def _sigmoid(x):
    return jax.nn.sigmoid(x)

def _layernorm(x, axis=-1, eps=1e-05):
    m = jnp.mean(x, axis=axis, keepdims=True)
    v = jnp.var(x, axis=axis, keepdims=True)
    return (x - m) / jnp.sqrt(v + eps)

def _scatter_add(tgt, idx, src, axis=0):
    return tgt.at[idx].add(src)

def _segment_sum(src, seg, n):
    return jax.ops.segment_sum(src, seg, n)
kernel_name = 'mk_perceiver_d4_seqx_r4_293bdf'

def setup_inputs(seed: int=0):
    np.random.seed(seed)
    _w = jnp.asarray

    def _rec_inputs():
        import jax
        import jax.numpy as jnp
        _rk = jax.random.key(seed)
        x = -0.0002928 + 1 * jax.random.normal(jax.random.fold_in(_rk, 1), (1, 256, 256), jnp.float32)
        _lenS = 256 - jax.random.randint(jax.random.fold_in(_rk, 7), (1,), 0, max(1, 256 // 4) + 1, jnp.int32)
        _lenS2 = 4096 - jax.random.randint(jax.random.fold_in(_rk, 8), (1,), 0, max(1, 4096 // 4) + 1, jnp.int32)
        _ctx_1024P = jax.random.normal(jax.random.fold_in(_rk, 11), (1, 16, 256), jnp.float32)
        _ctx_1024c = jax.random.dirichlet(jax.random.fold_in(_rk, 511), 0.3 * jnp.ones((16,), jnp.float32), (1, 4096))
        _ctx_1024t = jnp.einsum('bsk,bkd->bsd', _ctx_1024c, _ctx_1024P)
        _ctx_1024t = _ctx_1024t * jax.lax.rsqrt(jnp.mean(jnp.square(_ctx_1024t)) + 1e-12) * 0.953939
        ctx_1024 = -1.39393e-06 + 0.999914 * (_ctx_1024t + 0.3 * jax.random.normal(jax.random.fold_in(_rk, 611), (1, 4096, 256), jnp.float32))
        fside_BxSxS2_0 = jax.random.uniform(jax.random.fold_in(_rk, 12), (1, 256, 4096), jnp.float32, 0.0, 1)
        _validS = jnp.arange(256)[None, :] < _lenS[:, None]
        _validS2 = jnp.arange(4096)[None, :] < _lenS2[:, None]
        _causal = jnp.tril(jnp.ones((256, 256), dtype=bool))
        mask_BxSxS2_ik1 = jnp.where(jnp.broadcast_to(_validS2[:, None, :], (1, 256, 4096)), 1, 0).astype(jnp.int32)
        mask_Bx1xS2_bf1 = jnp.ones((1, 1, 4096), dtype=bool)
        return (x, ctx_1024, fside_BxSxS2_0, mask_BxSxS2_ik1, mask_Bx1xS2_bf1)
    x, ctx_1024, fside_BxSxS2_0, mask_BxSxS2_ik1, mask_Bx1xS2_bf1 = _rec_inputs()

    def _L0_xattn_setup():
        import jax, jax.numpy as jnp
        import numpy as np
        NUM_HEADS = 16
        HIDDEN = 256
        B, S = (2, 512)

        def _split_heads(x, H):
            b, s, d = x.shape
            return x.reshape(b, s, H, d // H).transpose(0, 2, 1, 3)
        key = jax.random.key(seed)
        ks = jax.random.split(key, 14)
        D = HIDDEN
        scale = 1.0 / np.sqrt(D)
        inp = {'query': jax.random.normal(ks[0], (B, S, D), jnp.float32), 'key_in': jax.random.normal(ks[1], (B, S, D), jnp.float32), 'value': jax.random.normal(ks[2], (B, S, D), jnp.float32), 'group_prob': jax.random.uniform(ks[3], (B, S, S), jnp.float32), 'mask': jax.random.randint(ks[4], (B, S, S), 0, 2, jnp.int32), 'wq_k': jax.random.normal(ks[5], (D, D), jnp.float32) * scale, 'wq_b': jnp.zeros((D,), jnp.float32), 'wk_k': jax.random.normal(ks[6], (D, D), jnp.float32) * scale, 'wk_b': jnp.zeros((D,), jnp.float32), 'wv_k': jax.random.normal(ks[7], (D, D), jnp.float32) * scale, 'wv_b': jnp.zeros((D,), jnp.float32), 'wo_k': jax.random.normal(ks[8], (D, D), jnp.float32) * scale, 'wo_b': jnp.zeros((D,), jnp.float32)}
        return inp
    _L0_xattn_all = _L0_xattn_setup()
    _L0_xattn_in = {k: v for k, v in _L0_xattn_all.items() if k in ('wq_k', 'wq_b', 'wk_k', 'wk_b', 'wv_k', 'wv_b', 'wo_k', 'wo_b')}
    del _L0_xattn_all

    def _L0_attn_setup():
        import jax, jax.numpy as jnp
        import numpy as np
        import math
        B, L, D_MODEL = (2, 512, 256)
        NUM_HEADS = 16
        FEATURE_DIM = 16
        HEAD_DIM = D_MODEL // NUM_HEADS
        EPS = 1e-12

        def taylor_exp(x):
            d = x.shape[-1]
            r2 = math.sqrt(2.0)
            rd = math.sqrt(d)
            rrd = math.sqrt(rd)
            x2 = (x[..., :, None] * x[..., None, :]).reshape(*x.shape[:-1], d * d) / r2
            ones = jnp.ones_like(x[..., :1])
            return jnp.concatenate([ones, x / rrd, x2 / rd], axis=-1)
        key = jax.random.key(seed)
        k0, k1, k2, k3, k4 = jax.random.split(key, 5)
        hidden_states = jax.random.normal(k0, (B, L, D_MODEL), dtype=jnp.float32)
        s = 1.0 / math.sqrt(D_MODEL)
        Wq = jax.random.normal(k1, (FEATURE_DIM * NUM_HEADS, D_MODEL), dtype=jnp.float32) * s
        Wk = jax.random.normal(k2, (FEATURE_DIM * NUM_HEADS, D_MODEL), dtype=jnp.float32) * s
        Wv = jax.random.normal(k3, (NUM_HEADS * HEAD_DIM, D_MODEL), dtype=jnp.float32) * s
        Wo = jax.random.normal(k4, (D_MODEL, NUM_HEADS * HEAD_DIM), dtype=jnp.float32) * s
        return {'hidden_states': hidden_states, 'Wq': Wq, 'Wk': Wk, 'Wv': Wv, 'Wo': Wo}
    _L0_attn_all = _L0_attn_setup()
    _L0_attn_in = {k: v for k, v in _L0_attn_all.items() if k in ('Wq', 'Wk', 'Wv', 'Wo')}
    del _L0_attn_all

    def _L0_ffn_setup():
        import jax, jax.numpy as jnp
        import numpy as np
        B, S, H, E = (4, 512, 256, 8)
        key = jax.random.key(seed)
        k1, k2, k3 = jax.random.split(key, 3)
        scale_w = 1.0 / np.sqrt(H)
        return {'x': jax.random.normal(k1, (B, S, H), dtype=jnp.float32), 'router_w': jax.random.normal(k2, (H, E), dtype=jnp.float32) * scale_w, 'router_b': jnp.zeros((E,), dtype=jnp.float32), 'expert_w': jax.random.normal(k3, (E, H, H), dtype=jnp.float32) * scale_w, 'expert_b': jnp.zeros((E, H), dtype=jnp.float32)}
    _L0_ffn_all = _L0_ffn_setup()
    _L0_ffn_in = {k: v for k, v in _L0_ffn_all.items() if k in ('router_w', 'router_b', 'expert_w', 'expert_b')}
    del _L0_ffn_all

    def _L1_xattn_setup():
        import jax, jax.numpy as jnp
        import numpy as np
        B, S, D, H = (2, 512, 256, 16)
        HD = D // H
        key = jax.random.key(seed)
        ks = jax.random.split(key, 12)
        s = 1.0 / np.sqrt(D)
        return {'query': jax.random.normal(ks[0], (B, S, D), jnp.float32), 'key': jax.random.normal(ks[1], (B, S, D), jnp.float32), 'value': jax.random.normal(ks[2], (B, S, D), jnp.float32), 'mask': jax.random.randint(ks[3], (B, S, S), 0, 2, jnp.int32), 'wq_kernel': jax.random.normal(ks[4], (D, D), jnp.float32) * s, 'wq_bias': jnp.zeros((D,), jnp.float32), 'wk_kernel': jax.random.normal(ks[5], (D, D), jnp.float32) * s, 'wk_bias': jnp.zeros((D,), jnp.float32), 'wv_kernel': jax.random.normal(ks[6], (D, D), jnp.float32) * s, 'wv_bias': jnp.zeros((D,), jnp.float32), 'wo_kernel': jax.random.normal(ks[7], (D, D), jnp.float32) * s, 'wo_bias': jnp.zeros((D,), jnp.float32)}
    _L1_xattn_all = _L1_xattn_setup()
    _L1_xattn_in = {k: v for k, v in _L1_xattn_all.items() if k in ('wq_kernel', 'wq_bias', 'wk_kernel', 'wk_bias', 'wv_kernel', 'wv_bias', 'wo_kernel', 'wo_bias')}
    del _L1_xattn_all

    def _L1_attn_setup():
        import jax, jax.numpy as jnp
        import numpy as np
        DIM = 256
        HEADS = 16
        DIM_HEAD = 64
        NUM_FRAMES = 8
        PATCHES_PER_FRAME = 64
        BATCH = 2
        SEQ = NUM_FRAMES * PATCHES_PER_FRAME
        EPS = 1e-05

        def _block_causal_mask(seq_len: int) -> jnp.ndarray:
            frame = jnp.arange(seq_len) // PATCHES_PER_FRAME
            return frame[:, None] >= frame[None, :]
        key = jax.random.key(seed)
        k1, k2, k3 = jax.random.split(key, 3)
        inner = HEADS * DIM_HEAD
        x = jax.random.normal(k1, (BATCH, SEQ, DIM), dtype=jnp.float32)
        g = jnp.ones((1, 1, DIM), dtype=jnp.float32)
        b = jnp.zeros((1, 1, DIM), dtype=jnp.float32)
        w_qkv = jax.random.normal(k2, (DIM, 3 * inner), dtype=jnp.float32) * DIM ** (-0.5)
        w_out = jax.random.normal(k3, (inner, DIM), dtype=jnp.float32) * inner ** (-0.5)
        b_out = jnp.zeros((DIM,), dtype=jnp.float32)
        return {'x': x, 'g': g, 'b': b, 'w_qkv': w_qkv, 'w_out': w_out, 'b_out': b_out}
    _L1_attn_all = _L1_attn_setup()
    _L1_attn_in = {k: v for k, v in _L1_attn_all.items() if k in ('g', 'b', 'w_qkv', 'w_out', 'b_out')}
    del _L1_attn_all

    def _L1_ffn_setup():
        import jax, jax.numpy as jnp
        import numpy as np
        B, T, C, H, E = (4, 512, 256, 512, 8)
        CAPACITY_FACTOR = 1.0
        key = jax.random.key(seed)
        ks = jax.random.split(key, 5)
        scale = 0.02
        return {'x': jax.random.normal(ks[0], (B, T, C), dtype=jnp.float32), 'Wg': jax.random.normal(ks[1], (E, C), dtype=jnp.float32) * scale, 'W1': jax.random.normal(ks[2], (E, H, C), dtype=jnp.float32) * scale, 'W2': jax.random.normal(ks[3], (E, C, H), dtype=jnp.float32) * scale, 'W3': jax.random.normal(ks[4], (E, H, C), dtype=jnp.float32) * scale}
    _L1_ffn_all = _L1_ffn_setup()
    _L1_ffn_in = {k: v for k, v in _L1_ffn_all.items() if k in ('Wg', 'W1', 'W2', 'W3')}
    del _L1_ffn_all

    def _L2_xattn_setup():
        import jax, jax.numpy as jnp
        import numpy as np
        H = 16
        D = 256
        HD = D // H
        key = jax.random.key(seed)
        ks = jax.random.split(key, 12)
        B, S = (4, 512)
        scale = 1.0 / np.sqrt(D)
        inp = {'k': jax.random.normal(ks[0], (B, S, D), jnp.float32), 'v': jax.random.normal(ks[1], (B, S, D), jnp.float32), 'q': jax.random.normal(ks[2], (B, S, D), jnp.float32), 'mask': jnp.ones((B, 1, S), dtype=bool), 'Wk': jax.random.normal(ks[3], (D, D), jnp.float32) * scale, 'bk': jax.random.normal(ks[4], (D,), jnp.float32) * 0.01, 'Wv': jax.random.normal(ks[5], (D, D), jnp.float32) * scale, 'bv': jax.random.normal(ks[6], (D,), jnp.float32) * 0.01, 'Wq': jax.random.normal(ks[7], (D, D), jnp.float32) * scale, 'bq': jax.random.normal(ks[8], (D,), jnp.float32) * 0.01, 'Wo': jax.random.normal(ks[9], (D, D), jnp.float32) * scale, 'bo': jax.random.normal(ks[10], (D,), jnp.float32) * 0.01}
        return inp
    _L2_xattn_all = _L2_xattn_setup()
    _L2_xattn_in = {k: v for k, v in _L2_xattn_all.items() if k in ('Wk', 'bk', 'Wv', 'bv', 'Wq', 'bq', 'Wo', 'bo')}
    del _L2_xattn_all

    def _L2_attn_setup():
        import jax, jax.numpy as jnp
        import numpy as np
        import math
        D_MODEL = 256
        EMB = 256
        key = jax.random.key(seed)
        ks = jax.random.split(key, 9)
        s = 1.0 / math.sqrt(EMB)
        x = jax.random.normal(ks[0], (4, 512, EMB), dtype=jnp.float32)
        W1 = jax.random.uniform(ks[1], (EMB, EMB), minval=-s, maxval=s)
        b1 = jax.random.uniform(ks[2], (EMB,), minval=-s, maxval=s)
        W2 = jax.random.uniform(ks[3], (EMB, EMB), minval=-s, maxval=s)
        b2 = jax.random.uniform(ks[4], (EMB,), minval=-s, maxval=s)
        W3 = jax.random.uniform(ks[5], (EMB, EMB), minval=-s, maxval=s)
        b3 = jax.random.uniform(ks[6], (EMB,), minval=-s, maxval=s)
        W4 = jax.random.uniform(ks[7], (EMB, EMB), minval=-s, maxval=s)
        b4 = jax.random.uniform(ks[8], (EMB,), minval=-s, maxval=s)
        return {'x': x, 'W1': W1, 'b1': b1, 'W2': W2, 'b2': b2, 'W3': W3, 'b3': b3, 'W4': W4, 'b4': b4}
    _L2_attn_all = _L2_attn_setup()
    _L2_attn_in = {k: v for k, v in _L2_attn_all.items() if k in ('W1', 'b1', 'W2', 'b2', 'W3', 'b3', 'W4', 'b4')}
    del _L2_attn_all

    def _L2_ffn_setup():
        import jax, jax.numpy as jnp
        import numpy as np
        import math
        GOLDEN_CENTER = 1.0 / math.e
        GOLDEN_LOWER = 0.5 - math.log(4.0 / 3.0)
        GOLDEN_UPPER = 0.5
        B, T, D = (4, 512, 256)
        E = 8
        I = 1024 // (E // 2)

        def _routing_weights(x, Wr, temperature):
            inh = jax.nn.sigmoid(x @ Wr / temperature)
            in_zone = (inh >= GOLDEN_LOWER) & (inh <= GOLDEN_UPPER)
            dist = jnp.abs(inh - GOLDEN_CENTER)
            w = jnp.exp(-dist / 0.1) * in_zone.astype(x.dtype)
            wsum = w.sum(axis=-1, keepdims=True)
            no_expert = wsum < 1e-08
            fb = jnp.exp(-dist / 0.3)
            _, top2 = jax.lax.top_k(fb, 2)
            fb_mask = jax.nn.one_hot(top2, E, dtype=x.dtype).sum(axis=-2)
            fb_w = fb * fb_mask
            fb_w = fb_w / jnp.clip(fb_w.sum(axis=-1, keepdims=True), 1e-08)
            w = jnp.where(no_expert, fb_w, w)
            wsum = w.sum(axis=-1, keepdims=True)
            return w / jnp.clip(wsum, 1e-08)
        key = jax.random.key(seed)
        k = jax.random.split(key, 6)
        s_d = 1.0 / math.sqrt(D)
        s_i = 1.0 / math.sqrt(I)
        return {'x': jax.random.normal(k[0], (B, T, D), jnp.float32), 'Wg': jax.random.normal(k[1], (E, D, I), jnp.float32) * s_d, 'Wu': jax.random.normal(k[2], (E, D, I), jnp.float32) * s_d, 'Wd': jax.random.normal(k[3], (E, I, D), jnp.float32) * s_i, 'Wr': jax.random.normal(k[4], (D, E), jnp.float32) * s_d, 'temperature': jnp.ones((1,), jnp.float32)}
    _L2_ffn_all = _L2_ffn_setup()
    _L2_ffn_in = {k: v for k, v in _L2_ffn_all.items() if k in ('Wg', 'Wu', 'Wd', 'Wr', 'temperature')}
    del _L2_ffn_all

    def _L3_xattn_setup():
        import jax, jax.numpy as jnp
        import numpy as np
        EMBED_DIM = 256
        NUM_HEADS = 16
        HEAD_DIM = EMBED_DIM // NUM_HEADS
        SCALE = HEAD_DIM ** (-0.5)
        key = jax.random.key(seed)
        ks = jax.random.split(key, 12)
        B, S, D = (1, 1024, EMBED_DIM)
        w_std = D ** (-0.5)
        return {'query': jax.random.normal(ks[0], (B, S, D), dtype=jnp.float32), 'key': jax.random.normal(ks[1], (B, S, D), dtype=jnp.float32), 'value': jax.random.normal(ks[2], (B, S, D), dtype=jnp.float32), 'Wq': jax.random.normal(ks[3], (D, D), dtype=jnp.float32) * w_std, 'bq': jax.random.normal(ks[4], (D,), dtype=jnp.float32) * 0.01, 'Wk': jax.random.normal(ks[5], (D, D), dtype=jnp.float32) * w_std, 'bk': jax.random.normal(ks[6], (D,), dtype=jnp.float32) * 0.01, 'Wv': jax.random.normal(ks[7], (D, D), dtype=jnp.float32) * w_std, 'bv': jax.random.normal(ks[8], (D,), dtype=jnp.float32) * 0.01, 'Wo': jax.random.normal(ks[9], (D, D), dtype=jnp.float32) * w_std, 'bo': jax.random.normal(ks[10], (D,), dtype=jnp.float32) * 0.01}
    _L3_xattn_all = _L3_xattn_setup()
    _L3_xattn_in = {k: v for k, v in _L3_xattn_all.items() if k in ('Wq', 'bq', 'Wk', 'bk', 'Wv', 'bv', 'Wo', 'bo')}
    del _L3_xattn_all

    def _L3_attn_setup():
        import jax, jax.numpy as jnp
        import numpy as np
        EPS = 1e-05
        key = jax.random.key(seed)
        ks = jax.random.split(key, 7)
        B, T, H = (4, 1024, 256)
        x = jax.random.normal(ks[0], (B, T, H), dtype=jnp.float32)
        gamma = jnp.ones((H,), dtype=jnp.float32)
        beta = jnp.zeros((H,), dtype=jnp.float32)
        s = 1.0 / np.sqrt(H)
        Wg = jax.random.uniform(ks[1], (H, H), minval=-s, maxval=s, dtype=jnp.float32)
        bg = jax.random.uniform(ks[2], (H,), minval=-s, maxval=s, dtype=jnp.float32)
        Wc = jax.random.uniform(ks[3], (H, H), minval=-s, maxval=s, dtype=jnp.float32)
        bc = jax.random.uniform(ks[4], (H,), minval=-s, maxval=s, dtype=jnp.float32)
        return {'x': x, 'gamma': gamma, 'beta': beta, 'Wg': Wg, 'bg': bg, 'Wc': Wc, 'bc': bc}
    _L3_attn_all = _L3_attn_setup()
    _L3_attn_in = {k: v for k, v in _L3_attn_all.items() if k in ('gamma', 'beta', 'Wg', 'bg', 'Wc', 'bc')}
    del _L3_attn_all

    def _L3_ffn_setup():
        import jax, jax.numpy as jnp
        import numpy as np
        N_EMBD = 256
        N_STATE = 1024
        key = jax.random.key(seed)
        k_x, k_w1, k_b1, k_w2, k_b2 = jax.random.split(key, 5)
        x = jax.random.normal(k_x, (4, 512, N_EMBD), dtype=jnp.float32)
        w1 = jax.random.normal(k_w1, (N_EMBD, N_STATE), dtype=jnp.float32) * (1.0 / np.sqrt(N_EMBD))
        b1 = jax.random.normal(k_b1, (N_STATE,), dtype=jnp.float32) * 0.02
        w2 = jax.random.normal(k_w2, (N_STATE, N_EMBD), dtype=jnp.float32) * (1.0 / np.sqrt(N_STATE))
        b2 = jax.random.normal(k_b2, (N_EMBD,), dtype=jnp.float32) * 0.02
        return {'x': x, 'w1': w1, 'b1': b1, 'w2': w2, 'b2': b2}
    _L3_ffn_all = _L3_ffn_setup()
    _L3_ffn_in = {k: v for k, v in _L3_ffn_all.items() if k in ('w1', 'b1', 'w2', 'b2')}
    del _L3_ffn_all
    return {'x': x, 'ctx_1024': ctx_1024, 'fside_BxSxS2_0': fside_BxSxS2_0, 'mask_BxSxS2_ik1': mask_BxSxS2_ik1, 'mask_Bx1xS2_bf1': mask_Bx1xS2_bf1, 'L0_xattn_wq_k': _L0_xattn_in['wq_k'], 'L0_xattn_wq_b': _L0_xattn_in['wq_b'], 'L0_xattn_wk_k': _L0_xattn_in['wk_k'], 'L0_xattn_wk_b': _L0_xattn_in['wk_b'], 'L0_xattn_wv_k': _L0_xattn_in['wv_k'], 'L0_xattn_wv_b': _L0_xattn_in['wv_b'], 'L0_xattn_wo_k': _L0_xattn_in['wo_k'], 'L0_xattn_wo_b': _L0_xattn_in['wo_b'], 'L0_attn_Wq': _L0_attn_in['Wq'], 'L0_attn_Wk': _L0_attn_in['Wk'], 'L0_attn_Wv': _L0_attn_in['Wv'], 'L0_attn_Wo': _L0_attn_in['Wo'], 'L0_ffn_router_w': _L0_ffn_in['router_w'], 'L0_ffn_router_b': _L0_ffn_in['router_b'], 'L0_ffn_expert_w': _L0_ffn_in['expert_w'], 'L0_ffn_expert_b': _L0_ffn_in['expert_b'], 'L1_xattn_wq_kernel': _L1_xattn_in['wq_kernel'], 'L1_xattn_wq_bias': _L1_xattn_in['wq_bias'], 'L1_xattn_wk_kernel': _L1_xattn_in['wk_kernel'], 'L1_xattn_wk_bias': _L1_xattn_in['wk_bias'], 'L1_xattn_wv_kernel': _L1_xattn_in['wv_kernel'], 'L1_xattn_wv_bias': _L1_xattn_in['wv_bias'], 'L1_xattn_wo_kernel': _L1_xattn_in['wo_kernel'], 'L1_xattn_wo_bias': _L1_xattn_in['wo_bias'], 'L1_attn_g': _L1_attn_in['g'], 'L1_attn_b': _L1_attn_in['b'], 'L1_attn_w_qkv': _L1_attn_in['w_qkv'], 'L1_attn_w_out': _L1_attn_in['w_out'], 'L1_attn_b_out': _L1_attn_in['b_out'], 'L1_ffn_Wg': _L1_ffn_in['Wg'], 'L1_ffn_W1': _L1_ffn_in['W1'], 'L1_ffn_W2': _L1_ffn_in['W2'], 'L1_ffn_W3': _L1_ffn_in['W3'], 'L2_xattn_Wk': _L2_xattn_in['Wk'], 'L2_xattn_bk': _L2_xattn_in['bk'], 'L2_xattn_Wv': _L2_xattn_in['Wv'], 'L2_xattn_bv': _L2_xattn_in['bv'], 'L2_xattn_Wq': _L2_xattn_in['Wq'], 'L2_xattn_bq': _L2_xattn_in['bq'], 'L2_xattn_Wo': _L2_xattn_in['Wo'], 'L2_xattn_bo': _L2_xattn_in['bo'], 'L2_attn_W1': _L2_attn_in['W1'], 'L2_attn_b1': _L2_attn_in['b1'], 'L2_attn_W2': _L2_attn_in['W2'], 'L2_attn_b2': _L2_attn_in['b2'], 'L2_attn_W3': _L2_attn_in['W3'], 'L2_attn_b3': _L2_attn_in['b3'], 'L2_attn_W4': _L2_attn_in['W4'], 'L2_attn_b4': _L2_attn_in['b4'], 'L2_ffn_Wg': _L2_ffn_in['Wg'], 'L2_ffn_Wu': _L2_ffn_in['Wu'], 'L2_ffn_Wd': _L2_ffn_in['Wd'], 'L2_ffn_Wr': _L2_ffn_in['Wr'], 'L2_ffn_temperature': _L2_ffn_in['temperature'], 'L3_xattn_Wq': _L3_xattn_in['Wq'], 'L3_xattn_bq': _L3_xattn_in['bq'], 'L3_xattn_Wk': _L3_xattn_in['Wk'], 'L3_xattn_bk': _L3_xattn_in['bk'], 'L3_xattn_Wv': _L3_xattn_in['Wv'], 'L3_xattn_bv': _L3_xattn_in['bv'], 'L3_xattn_Wo': _L3_xattn_in['Wo'], 'L3_xattn_bo': _L3_xattn_in['bo'], 'L3_attn_gamma': _L3_attn_in['gamma'], 'L3_attn_beta': _L3_attn_in['beta'], 'L3_attn_Wg': _L3_attn_in['Wg'], 'L3_attn_bg': _L3_attn_in['bg'], 'L3_attn_Wc': _L3_attn_in['Wc'], 'L3_attn_bc': _L3_attn_in['bc'], 'L3_ffn_w1': _L3_ffn_in['w1'], 'L3_ffn_b1': _L3_ffn_in['b1'], 'L3_ffn_w2': _L3_ffn_in['w2'], 'L3_ffn_b2': _L3_ffn_in['b2']}

def reference(x, ctx_1024, fside_BxSxS2_0, mask_BxSxS2_ik1, mask_Bx1xS2_bf1, L0_xattn_wq_k, L0_xattn_wq_b, L0_xattn_wk_k, L0_xattn_wk_b, L0_xattn_wv_k, L0_xattn_wv_b, L0_xattn_wo_k, L0_xattn_wo_b, L0_attn_Wq, L0_attn_Wk, L0_attn_Wv, L0_attn_Wo, L0_ffn_router_w, L0_ffn_router_b, L0_ffn_expert_w, L0_ffn_expert_b, L1_xattn_wq_kernel, L1_xattn_wq_bias, L1_xattn_wk_kernel, L1_xattn_wk_bias, L1_xattn_wv_kernel, L1_xattn_wv_bias, L1_xattn_wo_kernel, L1_xattn_wo_bias, L1_attn_g, L1_attn_b, L1_attn_w_qkv, L1_attn_w_out, L1_attn_b_out, L1_ffn_Wg, L1_ffn_W1, L1_ffn_W2, L1_ffn_W3, L2_xattn_Wk, L2_xattn_bk, L2_xattn_Wv, L2_xattn_bv, L2_xattn_Wq, L2_xattn_bq, L2_xattn_Wo, L2_xattn_bo, L2_attn_W1, L2_attn_b1, L2_attn_W2, L2_attn_b2, L2_attn_W3, L2_attn_b3, L2_attn_W4, L2_attn_b4, L2_ffn_Wg, L2_ffn_Wu, L2_ffn_Wd, L2_ffn_Wr, L2_ffn_temperature, L3_xattn_Wq, L3_xattn_bq, L3_xattn_Wk, L3_xattn_bk, L3_xattn_Wv, L3_xattn_bv, L3_xattn_Wo, L3_xattn_bo, L3_attn_gamma, L3_attn_beta, L3_attn_Wg, L3_attn_bg, L3_attn_Wc, L3_attn_bc, L3_ffn_w1, L3_ffn_b1, L3_ffn_w2, L3_ffn_b2):
    import jax
    import jax.numpy as jnp

    def _L0_xattn_ref(query, key_in, value, group_prob, mask, wq_k, wq_b, wk_k, wk_b, wv_k, wv_b, wo_k, wo_b):
        import jax, jax.numpy as jnp
        import numpy as np
        NUM_HEADS = 16
        HIDDEN = 256
        B, S = (2, 512)

        def _split_heads(x, H):
            b, s, d = x.shape
            return x.reshape(b, s, H, d // H).transpose(0, 2, 1, 3)
        H = NUM_HEADS
        dh = query.shape[-1] // H
        q = _split_heads(query @ wq_k + wq_b, H)
        k = _split_heads(key_in @ wk_k + wk_b, H)
        v = _split_heads(value @ wv_k + wv_b, H)
        logits = jnp.einsum('bhqd,bhkd->bhqk', q, k) / jnp.sqrt(jnp.asarray(dh, q.dtype))
        neg = (1.0 - mask.astype(q.dtype)) * -1000000000.0
        logits = logits + neg[:, None, :, :]
        attn = jax.nn.softmax(logits, axis=-1)
        attn = attn * group_prob[:, None, :, :]
        out = jnp.einsum('bhqk,bhkd->bhqd', attn, v)
        out = out.transpose(0, 2, 1, 3).reshape(query.shape[0], -1, H * dh)
        return out @ wo_k + wo_b

    def _L0_attn_ref(hidden_states, Wq, Wk, Wv, Wo):
        import jax, jax.numpy as jnp
        import numpy as np
        import math
        B, L, D_MODEL = (2, 512, 256)
        NUM_HEADS = 16
        FEATURE_DIM = 16
        HEAD_DIM = D_MODEL // NUM_HEADS
        EPS = 1e-12

        def taylor_exp(x):
            d = x.shape[-1]
            r2 = math.sqrt(2.0)
            rd = math.sqrt(d)
            rrd = math.sqrt(rd)
            x2 = (x[..., :, None] * x[..., None, :]).reshape(*x.shape[:-1], d * d) / r2
            ones = jnp.ones_like(x[..., :1])
            return jnp.concatenate([ones, x / rrd, x2 / rd], axis=-1)
        b, l, _ = hidden_states.shape
        q = (hidden_states @ Wq.T).reshape(b, l, NUM_HEADS, FEATURE_DIM).transpose(0, 2, 1, 3)
        k = (hidden_states @ Wk.T).reshape(b, l, NUM_HEADS, FEATURE_DIM).transpose(0, 2, 1, 3)
        v = (hidden_states @ Wv.T).reshape(b, l, NUM_HEADS, HEAD_DIM).transpose(0, 2, 1, 3)
        qf = taylor_exp(q)
        kf = taylor_exp(k)
        A = jnp.einsum('bhnd,bhmd->bhnm', qf, kf)
        A = jnp.tril(A)
        y = jnp.einsum('bhnm,bhme->bhne', A, v)
        z = 1.0 / (jnp.einsum('bhld,bhld->bhl', qf, jnp.cumsum(kf, axis=2)) + EPS)
        y = y * z[..., None]
        y = y.transpose(0, 2, 1, 3).reshape(b, l, NUM_HEADS * HEAD_DIM)
        return y @ Wo.T

    def _L0_ffn_ref(x, router_w, router_b, expert_w, expert_b):
        import jax, jax.numpy as jnp
        import numpy as np
        B, S, H, E = (4, 512, 256, 8)
        b, s, h = x.shape
        xt = x.reshape(b * s, h)
        logits = xt @ router_w + router_b
        probs = jax.nn.softmax(logits, axis=-1)
        gate = jnp.max(probs, axis=-1)
        idx = jnp.argmax(probs, axis=-1)
        out_all = jnp.einsum('th,ehd->ted', xt, expert_w) + expert_b[None, :, :]
        e_out = jnp.take_along_axis(out_all, idx[:, None, None], axis=1)[:, 0, :]
        y = gate[:, None] * e_out
        return y.reshape(b, s, h)

    def _L1_xattn_ref(query, key, value, mask, wq_kernel, wq_bias, wk_kernel, wk_bias, wv_kernel, wv_bias, wo_kernel, wo_bias):
        import jax, jax.numpy as jnp
        import numpy as np
        B, S, D, H = (2, 512, 256, 16)
        HD = D // H
        b = query.shape[0]

        def split_heads(x):
            return x.reshape(b, -1, H, HD).transpose(0, 2, 1, 3)
        q = split_heads(query @ wq_kernel + wq_bias)
        k = split_heads(key @ wk_kernel + wk_bias)
        v = split_heads(value @ wv_kernel + wv_bias)
        scores = jnp.einsum('bhqd,bhkd->bhqk', q, k) / jnp.sqrt(jnp.float32(HD))
        m = mask[:, None, :, :]
        scores = jnp.where(m == 0, jnp.float32(-1000000000.0), scores)
        attn = jax.nn.softmax(scores, axis=-1)
        out = jnp.einsum('bhqk,bhkd->bhqd', attn, v)
        out = out.transpose(0, 2, 1, 3).reshape(b, -1, D)
        return out @ wo_kernel + wo_bias

    def _L1_attn_ref(x, g, b, w_qkv, w_out, b_out):
        import jax, jax.numpy as jnp
        import numpy as np
        DIM = 256
        HEADS = 16
        DIM_HEAD = 64
        NUM_FRAMES = 8
        PATCHES_PER_FRAME = 64
        BATCH = 2
        SEQ = NUM_FRAMES * PATCHES_PER_FRAME
        EPS = 1e-05

        def _block_causal_mask(seq_len: int) -> jnp.ndarray:
            frame = jnp.arange(seq_len) // PATCHES_PER_FRAME
            return frame[:, None] >= frame[None, :]
        mean = jnp.mean(x, axis=-1, keepdims=True)
        var = jnp.var(x, axis=-1, keepdims=True)
        xn = (x - mean) / jnp.sqrt(var + EPS) * g + b
        qkv = xn @ w_qkv
        q, k, v = jnp.split(qkv, 3, axis=-1)
        split_heads = lambda t: t.reshape(t.shape[0], t.shape[1], HEADS, DIM_HEAD).transpose(0, 2, 1, 3)
        q, k, v = (split_heads(q), split_heads(k), split_heads(v))
        scale = DIM_HEAD ** (-0.5)
        dots = jnp.einsum('bhqd,bhkd->bhqk', q, k) * scale
        mask = _block_causal_mask(x.shape[1])
        dots = jnp.where(mask[None, None], dots, -jnp.inf)
        attn = jax.nn.softmax(dots, axis=-1)
        out = jnp.einsum('bhqk,bhkd->bhqd', attn, v)
        out = out.transpose(0, 2, 1, 3).reshape(x.shape[0], x.shape[1], HEADS * DIM_HEAD)
        return out @ w_out + b_out

    def _L1_ffn_ref(x, Wg, W1, W2, W3):
        import jax, jax.numpy as jnp
        import numpy as np
        B, T, C, H, E = (4, 512, 256, 512, 8)
        CAPACITY_FACTOR = 1.0
        b, t, c = x.shape
        e = Wg.shape[0]
        n = b * t
        capacity = max(1, int(CAPACITY_FACTOR * n / e))
        x_flat = x.reshape(n, c)
        scores = (x_flat @ Wg.T).T
        top_vals, token_idx = jax.lax.top_k(scores, capacity)
        token_w = jax.nn.softmax(top_vals, axis=-1)
        xg = x_flat[token_idx]
        h = jax.nn.silu(jnp.einsum('eic,ehc->eih', xg, W1)) * jnp.einsum('eic,ehc->eih', xg, W3)
        y = jnp.einsum('eih,ech->eic', h, W2) * token_w[..., None]
        out = jnp.zeros_like(x_flat).at[token_idx.reshape(-1)].add(y.reshape(-1, c))
        return out.reshape(b, t, c)

    def _L2_xattn_ref(k, v, q, mask, Wk, bk, Wv, bv, Wq, bq, Wo, bo):
        import jax, jax.numpy as jnp
        import numpy as np
        H = 16
        D = 256
        HD = D // H
        B, Sq, _ = q.shape
        Sk = k.shape[1]
        kh = (k @ Wk.T + bk).reshape(B, Sk, H, HD).transpose(0, 2, 1, 3)
        vh = (v @ Wv.T + bv).reshape(B, Sk, H, HD).transpose(0, 2, 1, 3)
        qh = (q @ Wq.T + bq).reshape(B, Sq, H, HD).transpose(0, 2, 1, 3)
        qh = qh / jnp.sqrt(jnp.asarray(HD, qh.dtype))
        scores = jnp.einsum('bhqd,bhkd->bhqk', qh, kh)
        scores = jnp.where(mask[:, None, :, :], scores, jnp.asarray(-jnp.inf, scores.dtype))
        attn = jax.nn.softmax(scores, axis=-1)
        ctx = jnp.einsum('bhqk,bhkd->bhqd', attn, vh)
        ctx = ctx.transpose(0, 2, 1, 3).reshape(B, Sq, H * HD)
        out = ctx @ Wo.T + bo
        return out

    def _L2_attn_ref(x, W1, b1, W2, b2, W3, b3, W4, b4):
        import jax, jax.numpy as jnp
        import numpy as np
        import math
        D_MODEL = 256
        EMB = 256
        Q = x @ W1 + b1
        K = x @ W2 + b2
        V = x @ W3 + b3
        scale = 1.0 / math.sqrt(D_MODEL)
        scores = jnp.einsum('bse,bte->bst', Q, K) * scale
        attn = jax.nn.softmax(scores, axis=-1)
        out = jnp.einsum('bst,bte->bse', attn, V)
        return out @ W4 + b4

    def _L2_ffn_ref(x, Wg, Wu, Wd, Wr, temperature):
        import jax, jax.numpy as jnp
        import numpy as np
        import math
        GOLDEN_CENTER = 1.0 / math.e
        GOLDEN_LOWER = 0.5 - math.log(4.0 / 3.0)
        GOLDEN_UPPER = 0.5
        B, T, D = (4, 512, 256)
        E = 8
        I = 1024 // (E // 2)

        def _routing_weights(x, Wr, temperature):
            inh = jax.nn.sigmoid(x @ Wr / temperature)
            in_zone = (inh >= GOLDEN_LOWER) & (inh <= GOLDEN_UPPER)
            dist = jnp.abs(inh - GOLDEN_CENTER)
            w = jnp.exp(-dist / 0.1) * in_zone.astype(x.dtype)
            wsum = w.sum(axis=-1, keepdims=True)
            no_expert = wsum < 1e-08
            fb = jnp.exp(-dist / 0.3)
            _, top2 = jax.lax.top_k(fb, 2)
            fb_mask = jax.nn.one_hot(top2, E, dtype=x.dtype).sum(axis=-2)
            fb_w = fb * fb_mask
            fb_w = fb_w / jnp.clip(fb_w.sum(axis=-1, keepdims=True), 1e-08)
            w = jnp.where(no_expert, fb_w, w)
            wsum = w.sum(axis=-1, keepdims=True)
            return w / jnp.clip(wsum, 1e-08)
        weights = _routing_weights(x, Wr, temperature)
        gate = jnp.einsum('btd,edi->beti', x, Wg)
        up = jnp.einsum('btd,edi->beti', x, Wu)
        h = jax.nn.silu(gate) * up
        e_out = jnp.einsum('beti,eid->betd', h, Wd)
        out = jnp.einsum('bte,betd->btd', weights, e_out)
        return out

    def _L3_xattn_ref(query, key, value, Wq, bq, Wk, bk, Wv, bv, Wo, bo):
        import jax, jax.numpy as jnp
        import numpy as np
        EMBED_DIM = 256
        NUM_HEADS = 16
        HEAD_DIM = EMBED_DIM // NUM_HEADS
        SCALE = HEAD_DIM ** (-0.5)
        B, Sq, D = query.shape
        Skv = key.shape[1]
        H, Hd = (NUM_HEADS, HEAD_DIM)
        q = (query @ Wq.T + bq).reshape(B, Sq, H, Hd).transpose(0, 2, 1, 3)
        k = (key @ Wk.T + bk).reshape(B, Skv, H, Hd).transpose(0, 2, 1, 3)
        v = (value @ Wv.T + bv).reshape(B, Skv, H, Hd).transpose(0, 2, 1, 3)
        q = q * SCALE
        scores = jnp.einsum('bhqd,bhkd->bhqk', q, k)
        attn = jax.nn.softmax(scores, axis=-1)
        out = jnp.einsum('bhqk,bhkd->bhqd', attn, v)
        out = out.transpose(0, 2, 1, 3).reshape(B, Sq, D)
        return out @ Wo.T + bo

    def _L3_attn_ref(x, gamma, beta, Wg, bg, Wc, bc):
        import jax, jax.numpy as jnp
        import numpy as np
        EPS = 1e-05
        mu = jnp.mean(x, axis=-1, keepdims=True)
        var = jnp.mean((x - mu) ** 2, axis=-1, keepdims=True)
        normed = (x - mu) * jax.lax.rsqrt(var + EPS) * gamma + beta
        z = jax.nn.sigmoid(jnp.einsum('bth,oh->bto', normed, Wg) + bg)
        c = jnp.einsum('bth,oh->bto', normed, Wc) + bc
        B, T, H = x.shape

        def step(h, zc):
            z_t, c_t = zc
            h = (1.0 - z_t) * h + z_t * c_t
            return (h, h)
        h0 = jnp.zeros((B, H), dtype=x.dtype)
        _, hs = jax.lax.scan(step, h0, (jnp.swapaxes(z, 0, 1), jnp.swapaxes(c, 0, 1)))
        return jnp.swapaxes(hs, 0, 1) + x

    def _L3_ffn_ref(x, w1, b1, w2, b2):
        import jax, jax.numpy as jnp
        import numpy as np
        N_EMBD = 256
        N_STATE = 1024
        h = jax.nn.gelu(jnp.einsum('bse,eh->bsh', x, w1) + b1, approximate=False)
        return jnp.einsum('bsh,he->bse', h, w2) + b2
    x = x + _L0_xattn_ref(_layernorm(x, axis=-1), ctx_1024, ctx_1024, fside_BxSxS2_0, mask_BxSxS2_ik1, L0_xattn_wq_k, L0_xattn_wq_b, L0_xattn_wk_k, L0_xattn_wk_b, L0_xattn_wv_k, L0_xattn_wv_b, L0_xattn_wo_k, L0_xattn_wo_b)
    x = x + _L0_attn_ref(_layernorm(x, axis=-1), L0_attn_Wq, L0_attn_Wk, L0_attn_Wv, L0_attn_Wo)
    x = x + _L0_ffn_ref(_layernorm(x, axis=-1), L0_ffn_router_w, L0_ffn_router_b, L0_ffn_expert_w, L0_ffn_expert_b)
    x = x + _L1_xattn_ref(_layernorm(x, axis=-1), ctx_1024, ctx_1024, mask_BxSxS2_ik1, L1_xattn_wq_kernel, L1_xattn_wq_bias, L1_xattn_wk_kernel, L1_xattn_wk_bias, L1_xattn_wv_kernel, L1_xattn_wv_bias, L1_xattn_wo_kernel, L1_xattn_wo_bias)
    x = x + _L1_attn_ref(_layernorm(x, axis=-1), L1_attn_g, L1_attn_b, L1_attn_w_qkv, L1_attn_w_out, L1_attn_b_out)
    x = x + _L1_ffn_ref(_layernorm(x, axis=-1), L1_ffn_Wg, L1_ffn_W1, L1_ffn_W2, L1_ffn_W3)
    x = x + _L2_xattn_ref(ctx_1024, ctx_1024, _layernorm(x, axis=-1), mask_Bx1xS2_bf1, L2_xattn_Wk, L2_xattn_bk, L2_xattn_Wv, L2_xattn_bv, L2_xattn_Wq, L2_xattn_bq, L2_xattn_Wo, L2_xattn_bo)
    x = x + _L2_attn_ref(_layernorm(x, axis=-1), L2_attn_W1, L2_attn_b1, L2_attn_W2, L2_attn_b2, L2_attn_W3, L2_attn_b3, L2_attn_W4, L2_attn_b4)
    x = x + _L2_ffn_ref(_layernorm(x, axis=-1), L2_ffn_Wg, L2_ffn_Wu, L2_ffn_Wd, L2_ffn_Wr, L2_ffn_temperature)
    x = x + _L3_xattn_ref(_layernorm(x, axis=-1), ctx_1024, ctx_1024, L3_xattn_Wq, L3_xattn_bq, L3_xattn_Wk, L3_xattn_bk, L3_xattn_Wv, L3_xattn_bv, L3_xattn_Wo, L3_xattn_bo)
    x = x + _L3_attn_ref(_layernorm(x, axis=-1), L3_attn_gamma, L3_attn_beta, L3_attn_Wg, L3_attn_bg, L3_attn_Wc, L3_attn_bc)
    x = x + _L3_ffn_ref(_layernorm(x, axis=-1), L3_ffn_w1, L3_ffn_b1, L3_ffn_w2, L3_ffn_b2)
    return x

_drawn_inputs = setup_inputs


def setup_inputs(seed=0):
    import zlib

    import numpy as np

    out = dict(_drawn_inputs(seed))
    spreads = {'L0_xattn_wq_b': (0.0, 0.1),
     'L0_xattn_wk_b': (0.0, 2.0),
     'L0_xattn_wv_b': (0.0, 0.1),
     'L0_xattn_wo_b': (0.0, 0.1),
     'L0_ffn_router_b': (0.0, 0.1),
     'L0_ffn_expert_b': (0.0, 0.1),
     'L1_xattn_wq_bias': (0.0, 0.1),
     'L1_xattn_wk_bias': (0.0, 2.0),
     'L1_xattn_wv_bias': (0.0, 0.1),
     'L1_xattn_wo_bias': (0.0, 0.1),
     'L1_attn_g': (1.0, 0.2),
     'L1_attn_b': (0.0, 0.1),
     'L1_attn_b_out': (0.0, 0.1),
     'L3_attn_gamma': (1.0, 0.6),
     'L3_attn_beta': (0.0, 0.342)}
    factors = {'L1_ffn_Wg': 8.0,
     'L1_ffn_W1': 8.0,
     'L1_ffn_W2': 8.0,
     'L1_ffn_W3': 8.0,
     'L2_xattn_bk': 64.0,
     'L2_xattn_bv': 4.037,
     'L2_xattn_bq': 29.225,
     'L2_xattn_bo': 4.745,
     'L2_attn_W1': 4.701,
     'L2_attn_b1': 8.0,
     'L2_attn_W2': 4.793,
     'L2_attn_b2': 64.0,
     'L3_xattn_bq': 64.0,
     'L3_xattn_bk': 64.0,
     'L3_xattn_bv': 8.0,
     'L3_xattn_bo': 8.0,
     'L3_attn_bg': 52.117,
     'L3_attn_bc': 4.23,
     'L3_ffn_b1': 8.0,
     'L3_ffn_b2': 8.0,
     'L2_attn_b3': 3.095,
     'L3_attn_Wg': 2.746}
    for name, (base, spread) in spreads.items():
        noise = np.random.default_rng([zlib.crc32(name.encode()), seed]).standard_normal(out[name].shape)
        drawn = base * np.exp(spread * noise) if base else spread * noise
        out[name] = jnp.asarray(drawn.astype(out[name].dtype))
    for name, factor in factors.items():
        out[name] = (out[name] * factor).astype(out[name].dtype)
    return out
```

```python
import math
from contextlib import ExitStack

import concourse.bass as bass
from concourse import mybir

F32 = mybir.dt.float32
BF16 = mybir.dt.bfloat16
I32 = mybir.dt.int32
U32 = mybir.dt.uint32
U8 = mybir.dt.uint8
ALU = mybir.AluOpType
ACT = mybir.ActivationFunctionType
AX = mybir.AxisListType

P = 128
D = 256
NT = 256
QT = NT // P
CT = D // P
KEYS = 4096
KT = KEYS // P
H = 16
HD = D // H
LAYERS = 4
CHUNK = 512
NCHUNK = KEYS // CHUNK
GROUP = 4
NGROUP = KT // GROUP
UNROLL = 4
NP = 4
LAG = 2
Q_SCALE = float(HD) ** -0.5
KEYED = 2
PRIMED = 1
NEG = -(2.0 ** 100)
E = 8
EPS = 1e-5

PARTS_BESIDE = [3, 2, 2]
PAIRS = [(k, q) for k, n in enumerate(PARTS_BESIDE) for q in range(n)]
R_MASK = len(PAIRS) * HD
R_MAX = R_MASK + 1
R_ALL = R_MAX + 3


class Sems:

    def __init__(self, nc, ctx, prefix):
        self.nc, self.prefix, self.made = nc, prefix, {}
        ctx.callback(self.clear)

    def clear(self):
        for sem in self.made.values():
            self.nc.gpsimd.sem_clear(sem)
            self.nc.release_semaphore(sem)

    def __call__(self, name):
        if name not in self.made:
            self.made[name] = self.nc.alloc_semaphore(f"{self.prefix}_{name}")
        return self.made[name]


class Chain:

    def __init__(self, eng, sem):
        self.eng, self.sem, self.n = eng, sem, 0

    def __call__(self, ins):
        self.n += 1
        ins.then_inc(self.sem, 1)
        self.eng.wait_ge(self.sem, self.n)


def wait_apart(eng, sem, value, least):
    value = value if isinstance(value, int) else eng.to_reg(value)
    eng.wait_ge(sem, least)
    eng.wait_ge(sem, value)


class Core:
    pass


def norm_dve(c, dve, S, src, dst, n=0):
    for t in range(QT):
        dve.bn_stats(c.stats[:, t, :], src[:, t, :]).then_inc(S("norm_stats"), 1)
    dve.wait_ge(S("norm_stats"), QT * (n + 1))
    for t in range(QT):
        dve.bn_aggr(c.moments[:, t, :], c.stats[:, t, :]).then_inc(S("norm_moments"), 1)
    dve.wait_ge(S("norm_moments"), QT * (n + 1))
    dve.tensor_scalar(c.var[:, :], c.moments[:, :, 1], EPS, None, ALU.add).then_inc(S("norm_var"), 1)
    dve.wait_ge(S("norm_rstd"), n + 1)
    for t in range(QT):
        dve.tensor_scalar(dst[:, t, :], src[:, t, :], c.moments[:, t, 0:1], c.rstd[:, t:t + 1],
                          ALU.subtract, ALU.mult).then_inc(S("norm_done"), 1)


def norm_pool(c, pool, S, n=0):
    pool.wait_ge(S("norm_var"), n + 1)
    pool.tensor_tensor(c.rstd[:, :], c.var[:, :], c.minus_half[:, :], ALU.pow).then_inc(S("norm_rstd"), 1)


def turn_pe(c, pe, S, src, bank, name):
    for ct in range(CT):
        for t in range(QT):
            ins = pe.transpose(c.ps[:, bank, ct * NT + t * P:ct * NT + (t + 1) * P],
                               src[:, t, ct * P:(ct + 1) * P], c.ident[:, :])
    ins.then_inc(S(name), 1)


def by_tokens_pe(c, pe, out, srcT, w, bias, n_ct=CT):
    for t in range(QT):
        if bias is not None:
            pe.matmul(out[t], c.ones[0:1, 0:P], bias, start=True, stop=False)
        for ct in range(n_ct):
            ins = pe.matmul(out[t], srcT[:, ct, t * P:(t + 1) * P], w[:, ct, :],
                            start=(ct == 0 and bias is None), stop=(ct == n_ct - 1))
    return ins


def add_stream_dve(c, dve, S, bank):
    dve.tensor_tensor(c.x[:, :, :], c.ps[:, bank, :].rearrange("p (t d) -> p t d", t=QT), c.x[:, :, :],
                      ALU.add).then_inc(S("x_added"), 1)
    dve.wait_ge(S("x_added"), 1)


def constants(c):
    nc = c.nc
    with ExitStack() as ctx:
        S = Sems(nc, ctx, "const")
        block = ctx.enter_context(nc.Block())

        @block.sync
        def _(sp):
            sp.dma_start(c.x[:, :, :], c.a["x"].rearrange("(t p) d -> p t d", p=P)).then_inc(S("loaded"), 16)
            sp.dma_start(c.rows[:, :, :], c.a["rows"]).then_inc(S("loaded"), 16)
            sp.dma_start(c.wq[:, :, :], c.a["wq4"][0, :, :].rearrange("(t p) n -> p t n", p=P)).then_inc(S("loaded"), 16)
            sp.wait_ge(S("loaded"), 48)

        @block.gpsimd
        def _(pool):
            for k, (tile, value) in enumerate([(c.ident, 0.0), (c.identb, 0.0), (c.fold, 0.0), (c.ones, 1.0),
                                               (c.minus_half, -0.5), (c.tri, 0.5), (c.den16, 0.0)]):
                pool.memset(tile[:, :], value).then_inc(S("filled"), 1)
            pool.wait_ge(S("filled"), 7)
            for tile in (c.ident, c.identb):
                pool.affine_select(out=tile[:, :], in_=tile[:, :], compare_op=ALU.not_equal, fill=1.0, base=0,
                                   pattern=[[-1, P]], channel_multiplier=1).then_inc(S("placed"), 1)
            for g in range(4):
                pool.affine_select(out=c.fold[:, :], in_=c.fold[:, :], compare_op=ALU.not_equal, fill=1.0,
                                   base=-32 * g, pattern=[[-1, 32]], channel_multiplier=1).then_inc(S("placed"), 1)
                pool.wait_ge(S("placed"), 3 + g)
            for at in (0, 2 * P):
                pool.affine_select(out=c.tri[:, at:at + P], in_=c.tri[:, at:at + P], compare_op=ALU.is_ge, fill=0.0,
                                   base=0, pattern=[[1, P]], channel_multiplier=-1).then_inc(S("placed"), 1)
            pool.memset(c.den16[:, HD:HD + 1], 1.0).then_inc(S("placed"), 1)
            pool.iota(c.count8_i[:, :], pattern=[[1, E]], base=0, channel_multiplier=0).then_inc(S("placed"), 1)
            pool.wait_ge(S("placed"), 10)
            pool.tensor_copy(c.count8[:, :], c.count8_i[:, :]).then_inc(S("placed"), 1)
            pool.wait_ge(S("placed"), 11)


def project_context(c):
    nc = c.nc
    NK = CT * NCHUNK
    VB = 8
    NV = KT // VB
    PIECE = 1024
    with ExitStack() as ctx:
        S = Sems(nc, ctx, "kv")
        sb = lambda name, shape, dt: ctx.enter_context(nc.sbuf_tensor(name, shape, dt))
        ctxT = sb("ctxT", [P, CT, KEYS], F32)
        wk = sb("wk", [P, CT, D], F32)
        wv = sb("wv", [P, CT, D], F32)
        bk = sb("bk", [P, CT], F32)
        bv = sb("bv", [P, D], F32)
        kp = sb("kp", [P, 4, 3, CHUNK], BF16)
        rest = sb("rest", [P, 2, CHUNK], F32)
        vst = sb("vst", [P, 2, H, VB, HD], F32)
        raw = sb("raw", [P, 2, PIECE], I32)
        block = ctx.enter_context(nc.Block())
        ctx_v = c.a["ctxT"].rearrange("(t p) k -> p t k", p=P)
        vout = c.vals.rearrange("l p (h k e) -> l p h k e", h=H, k=KT)

        masks = []
        for t in range(QT):
            for j in range(KEYS // PIECE):
                masks.append((c.a["mask"][t * P:(t + 1) * P, j * PIECE:(j + 1) * PIECE],
                              c.neg_q[:, t, j * PIECE:(j + 1) * PIECE]))
        for j in range(KT * NT // PIECE):
            n = PIECE // NT
            masks.append((c.a["maskT"].rearrange("(k p) q -> p k q", p=P)[:, j * n:(j + 1) * n, :],
                          c.neg_k[:, j * n:(j + 1) * n, :]))

        @block.sync
        def _(sp):
            for j in range(NCHUNK):
                sp.dma_start(ctxT[:, :, j * CHUNK:(j + 1) * CHUNK], ctx_v[:, :, j * CHUNK:(j + 1) * CHUNK])\
                  .then_inc(S(f"ctx_loaded{j}"), 16)
            for j, (src, _) in enumerate(masks):
                if j >= 2:
                    sp.wait_ge(S("mask_made"), j - 1)
                dst = raw[:, j % 2, :]
                if len(src.shape) == 3:
                    dst = dst.rearrange("p (k q) -> p k q", q=NT)
                sp.dma_start(dst, src).then_inc(S(f"mask_loaded{j % 2}"), 16)
            sp.dma_start(c.gT[:, :, :], c.a["gT"].rearrange("(k p) q -> p k q", p=P)).then_inc(S("g_loaded"), 16)
            for n in range(4):
                sp.sem_inc(S(f"k_stored{n}"), 16)
            for n in range(2):
                sp.sem_inc(S(f"v_stored{n}"), 16)
            with sp.Fori(0, LAYERS) as l:
                for n in range(NK):
                    sp.wait_ge(S("k_split"), NK * l + n + 1 + PRIMED)
                    sp.dma_start(c.kparts[bass.ds(l, 1), :, (n // NCHUNK) * P:(n // NCHUNK + 1) * P,
                                          (n % NCHUNK) * CHUNK:(n % NCHUNK + 1) * CHUNK]
                                 .rearrange("o s p k -> p (o s) k"), kp[:, n % 4, :, :]).then_inc(S(f"k_stored{n % 4}"), 16)
                for n in range(NV):
                    sp.wait_ge(S("v_staged"), KT * l + VB * (n + 1) + PRIMED)
                    sp.dma_start(vout[bass.ds(l, 1), :, :, n * VB:(n + 1) * VB, :].rearrange("o p h k e -> (o p) h k e"),
                                 vst[:, n % 2, :, :, :]).then_inc(S(f"v_stored{n % 2}"), 16)
            for n in range(4):
                sp.wait_ge(S(f"k_stored{n}"), 16 * (NK // 4) * LAYERS + 16)
            for n in range(2):
                sp.wait_ge(S(f"v_stored{n}"), 16 * (NV // 2) * LAYERS + 16)
            sp.wait_ge(S("g_loaded"), 16)

        @block.tensor
        def _(pe):
            pe.sem_inc(S("k_psum"), PRIMED)
            with pe.Fori(0, LAYERS) as l:
                pe.wait_ge(S("wk_loaded"), 32 * l + 32)
                for n in range(NK):
                    mt, j = n // NCHUNK, n % NCHUNK
                    if mt == 0:
                        pe.wait_ge(S(f"ctx_loaded{j}"), 16)
                    pe.wait_ge(S("k_rest"), NK * l + n + 1)
                    for ct in range(CT):
                        ins = pe.matmul(c.ps[:, n % 2, :], wk[:, ct, mt * P:(mt + 1) * P],
                                        ctxT[:, ct, j * CHUNK:(j + 1) * CHUNK], start=(ct == 0), stop=(ct == CT - 1))
                    ins.then_inc(S("k_psum"), 1)
                pe.wait_ge(S("wv_loaded"), 32 * l + 32)
                for k in range(KT):
                    if k >= 2:
                        pe.wait_ge(S("v_staged"), KT * l + k - 1 + PRIMED)
                    for ct in range(CT):
                        ins = pe.matmul(c.ps[:, 2 + k % 2, 0:D], ctxT[:, ct, k * P:(k + 1) * P], wv[:, ct, :],
                                        start=(ct == 0), stop=(ct == CT - 1))
                    ins.then_inc(S("v_psum"), 1)

        @block.scalar
        def _(act):
            def second(l, n):
                act.wait_ge(S("k_rest"), NK * l + n + 3)
                act.activation(kp[:, n % 4, 1, :], rest[:, n % 2, :], ACT.Copy).then_inc(S("k_second"), 1)

            with act.Fori(0, LAYERS) as l:
                act.wait_ge(S("k_psum"), NK * l + PRIMED)
                act.wait_ge(S("k_rest"), NK * l + 2)
                act.dma_start(wk[:, :, :], c.a["wk4"][bass.ds(l, 1), :, :].rearrange("o (t p) n -> p (o t) n", p=P))\
                   .then_inc(S("wk_loaded"), 16)
                act.dma_start(bk[:, :], c.a["bk4"][bass.ds(l, 1), :, :].rearrange("o p t -> (o p) t"))\
                   .then_inc(S("wk_loaded"), 16)
                act.wait_ge(S("v_staged"), KT * l + PRIMED)
                act.dma_start(wv[:, :, :], c.a["wv4"][bass.ds(l, 1), :, :].rearrange("o (t p) n -> p (o t) n", p=P))\
                   .then_inc(S("wv_loaded"), 16)
                act.dma_start(bv[:, :], c.a["bv4"][bass.ds(l, 1), :].to_broadcast((P, D))).then_inc(S("wv_loaded"), 16)
                act.wait_ge(S("wk_loaded"), 32 * l + 32)
                for n in range(NK):
                    act.wait_ge(S("k_psum"), NK * l + n + 1 + PRIMED)
                    act.wait_ge(S(f"k_stored{n % 4}"), 16 * (NK // 4) * l + 16 * (n // 4) + 16)
                    act.activation(kp[:, n % 4, 0, :], c.ps[:, n % 2, :], ACT.Identity,
                                   bias=bk[:, n // NCHUNK:n // NCHUNK + 1]).then_inc(S("k_first"), 1)
                    if n > 0:
                        second(l, n - 1)
                second(l, NK - 1)

        @block.vector
        def _(dve):
            dve.sem_inc(S("k_rest"), 2)
            dve.sem_inc(S("v_staged"), PRIMED)
            dve.memset(c.ops.kop[96:P, :, :], 1.0).then_inc(S("kop_ones"), 1)
            for j, (_, dst) in enumerate(masks):
                dve.wait_ge(S(f"mask_loaded{j % 2}"), 16 * (j // 2 + 1))
                src = raw[:, j % 2, :]
                if len(dst.shape) == 3:
                    src = src.rearrange("p (k q) -> p k q", q=NT)
                dve.tensor_scalar(dst, src, -1.0, -NEG, ALU.add, ALU.mult).then_inc(S("mask_made"), 1)
            with dve.Fori(0, LAYERS) as l:
                dve.wait_ge(S("wk_loaded"), 32 * l + 32)
                for n in range(NK):
                    dve.wait_ge(S("k_first"), NK * l + n + 1)
                    dve.wait_ge(S("k_split"), NK * l + max(n - 1, 0) + PRIMED)
                    dve.scalar_tensor_tensor(out=rest[:, n % 2, :], in0=c.ps[:, n % 2, :],
                                             scalar=bk[:, n // NCHUNK:n // NCHUNK + 1], in1=kp[:, n % 4, 0, :],
                                             op0=ALU.add, op1=ALU.subtract).then_inc(S("k_rest"), 1)
                dve.wait_ge(S("wv_loaded"), 32 * l + 32)
                for k in range(KT):
                    dve.wait_ge(S("v_psum"), KT * l + k + 1)
                    if k % VB == 0:
                        dve.wait_ge(S(f"v_stored{(k // VB) % 2}"), 16 * (NV // 2) * l + 16 * (k // VB // 2) + 16)
                    dve.tensor_tensor(vst[:, (k // VB) % 2, :, k % VB, :],
                                      c.ps[:, 2 + k % 2, 0:D].rearrange("p (h e) -> p h e", h=H),
                                      bv[:, :].rearrange("p (h e) -> p h e", h=H), ALU.add).then_inc(S("v_staged"), 1)

        @block.gpsimd
        def _(pool):
            pool.sem_inc(S("k_split"), PRIMED)
            with pool.Fori(0, LAYERS) as l:
                for n in range(NK):
                    pool.wait_ge(S("k_second"), NK * l + n + 1)
                    pool.tensor_tensor(kp[:, n % 4, 2, :], rest[:, n % 2, :], kp[:, n % 4, 1, :], ALU.subtract)\
                        .then_inc(S("k_split"), 1)


class Operands:

    def __init__(self, c, ctx):
        self.c = c
        self.kop = ctx.enter_context(c.nc.sbuf_tensor("kop", [P, UNROLL, KEYS], BF16))
        self.vraw = ctx.enter_context(c.nc.sbuf_tensor("vraw", [P, UNROLL, KT * HD], F32))
        self.S = Sems(c.nc, ctx, "ops")

    def load(self, eng, l, h, u):
        at = 0
        for part, n in enumerate(PARTS_BESIDE):
            src = self.c.kparts[l, part, :, :].rearrange("(h x) k -> h x k", h=H)[bass.ds(h, 1), :, :]
            eng.dma_start(self.kop[at:at + n * HD, u, :], src.to_broadcast((n, HD, KEYS)))\
               .then_inc(self.S(f"k_loaded{u}"), 16)
            at += n * HD
        src = self.c.vals[l, :, :].rearrange("p (h n) -> p h n", h=H)[:, bass.ds(h, 1), :]
        eng.dma_start(self.vraw[:, u, :], src.rearrange("p o n -> p (o n)")).then_inc(self.S(f"v_loaded{u}"), 16)

    def load_first(self, eng, l):
        for u in range(UNROLL):
            self.load(eng, l, u, u)


def queries(c, l):
    nc = c.nc
    with ExitStack() as ctx:
        S = Sems(nc, ctx, f"q{l}")
        sb = lambda name, shape, dt: ctx.enter_context(nc.sbuf_tensor(f"{name}_q{l}", shape, dt))
        qf = sb("qf", [P, CT * NT], F32)
        rest = sb("qrest", [P, 2, CT * NT], F32)
        qp = sb("qp", [P, 3, CT * NT], BF16)
        raw8 = sb("raw8", [1, KEYS], U8) if l == KEYED else None
        neg_row = sb("neg_row", [1, KEYS], BF16) if l == KEYED else None
        block = ctx.enter_context(nc.Block())

        @block.vector
        def _(dve):
            norm_dve(c, dve, S, c.x, c.xn)
            link = Chain(dve, S("q_step"))
            dve.wait_ge(S("q_scaled"), 1)
            link(dve.tensor_copy(qp[:, 0, :], qf[:, :]))
            link(dve.tensor_tensor(rest[:, 0, :], qf[:, :], qp[:, 0, :], ALU.subtract))
            link(dve.tensor_copy(qp[:, 1, :], rest[:, 0, :]))
            dve.tensor_tensor(qp[:, 2, :], rest[:, 0, :], qp[:, 1, :], ALU.subtract).then_inc(S("q_split"), 1)

        @block.gpsimd
        def _(pool):
            norm_pool(c, pool, S)
            if l == KEYED:
                pool.wait_ge(S("keymask_loaded"), 16)
                pool.wait_ge(S("norm_rstd"), 1)
                pool.tensor_scalar(neg_row[:, :], raw8[:, :], -1.0, -NEG, ALU.add, ALU.mult).then_inc(S("neg_made"), 1)

        @block.tensor
        def _(pe):
            pe.wait_ge(S("norm_done"), QT)
            turn_pe(c, pe, S, c.xn, 0, "x_turned")
            pe.wait_ge(S("xT_ready"), 1)
            for mt in range(CT):
                out = c.ps[:, 1, mt * NT:(mt + 1) * NT]
                pe.matmul(out, c.row(f"bq{l}")[0:1, mt * P:(mt + 1) * P], c.ones[0:1, 0:NT], start=True, stop=False)
                for ct in range(CT):
                    ins = pe.matmul(out, c.wq[:, ct, mt * P:(mt + 1) * P], c.xT[:, ct, :],
                                    start=False, stop=(ct == CT - 1))
            ins.then_inc(S("q_psum"), 1)

        @block.scalar
        def _(act):
            act.wait_ge(S("x_turned"), 1)
            act.activation(c.xT[:, :, :], c.ps[:, 0, :].rearrange("p (t n) -> p t n", t=CT), ACT.Copy)\
               .then_inc(S("xT_ready"), 1)
            act.wait_ge(S("q_psum"), 1)
            act.mul(qf[:, :], c.ps[:, 1, :], Q_SCALE).then_inc(S("q_scaled"), 1)

        @block.sync
        def _(sp):
            if l == KEYED:
                sp.dma_start(raw8[:, :], c.a["mask_keys"]).then_inc(S("keymask_loaded"), 16)
            if l == 0:
                c.ops.load_first(sp, 0)
            sp.wait_ge(S("q_split"), 1)
            for part in range(3):
                sp.dma_start(c.qparts[part, :, :].rearrange("(t p) q -> p t q", p=P),
                             qp[:, part, :].rearrange("p (t q) -> p t q", t=CT)).then_inc(S("q_stored"), 16)
            if l == KEYED:
                sp.wait_ge(S("neg_made"), 1)
                sp.dma_start(c.ops.kop[R_MASK:R_MASK + 1, :, :],
                             neg_row[0:1, :].unsqueeze(1).to_broadcast((1, UNROLL, KEYS))).then_inc(S("mask_placed"), 16)
                sp.wait_ge(S("mask_placed"), 16)
            sp.wait_ge(S("q_stored"), 48)


def attend(c, l, by_query, weighted):
    nc = c.nc
    TURNS = H // UNROLL
    SC = QT * NCHUNK
    ops, kop, vraw = c.ops, c.ops.kop, c.ops.vraw
    with ExitStack() as ctx:
        S = Sems(nc, ctx, f"att{l}")
        sb = lambda name, shape, dt: ctx.enter_context(nc.sbuf_tensor(f"{name}_a{l}", shape, dt))
        qop = sb("qop", [P, UNROLL, NT], BF16)
        vop = sb("vop", [P, 2, KT, 32], F32)
        prob = sb("prob", [P, NP, GROUP * NT], F32)
        used = sb("used", [P, NP, GROUP * NT], F32) if weighted else prob
        best = sb("best", [P, 2, SC], F32)
        nmax = sb("nmax", [P, 2, QT], F32)
        mrow = sb("mrow", [1, 2, NT], F32)
        mrest = sb("mrest", [1, 2, NT], F32)
        mpart = sb("mpart", [1, 2, 3, NT], BF16)
        acc = sb("acc", [P, 2, NT], F32)
        rden = sb("rden", [P, QT], F32)
        dump = sb("dump", [P, 2, CHUNK], BF16) if by_query else None
        block = ctx.enter_context(nc.Block())

        s_bank = [c.ps[:, 0, :], c.ps[:, 1, :]]
        st_bank = [c.ps[:, 2:4, :].rearrange("p b n -> p (b n)"), c.ps[:, 4:6, :].rearrange("p b n -> p (b n)")]
        acc_bank = c.ps[:, 6, :]
        fold_out = c.ps[:, 7, 0:QT * 32]
        mrow_out = c.ps[0:1, 7, 256:256 + NT]
        qp = c.qparts.rearrange("s (h x) q -> s h x q", h=H)
        r_first = R_MASK + 1 if l == KEYED else R_MASK

        @block.sync
        def _(sp):
            def load_q(h, u):
                at = 0
                for n in PARTS_BESIDE:
                    sp.dma_start(qop[at:at + n * HD, u, :],
                                 qp[0:n, bass.ds(h, 1), :, :].rearrange("s o x q -> s (o x) q"))\
                      .then_inc(S(f"q_loaded{u}"), 16)
                    at += n * HD

            def maximum(h, u):
                sp.wait_ge(S("max_split"), h + 1 + PRIMED)
                sp.dma_start(qop[R_MAX:R_MAX + 3, u, :], mpart[0:1, u % 2, :, :]).then_inc(S(f"max_placed{u}"), 16)

            sp.wait_ge(S("qop_set"), 1)
            for u in range(UNROLL):
                load_q(u, u)
            maximum(0, 0)
            maximum(1, 1)
            with sp.Fori(0, TURNS - 1) as t:
                for u in range(UNROLL):
                    wait_apart(sp, S("st_psum"), NGROUP * UNROLL * t + NGROUP * (u + 1), 1)
                    load_q(UNROLL * t + u + UNROLL, u)
                    ops.load(sp, l, UNROLL * t + u + UNROLL, u)
                    maximum(UNROLL * t + u + 2, (u + 2) % UNROLL)
            maximum(H - 2, (H - 2) % UNROLL)
            maximum(H - 1, (H - 1) % UNROLL)
            sp.dma_start(c.wo[:, :, :], c.a["wo4"][l, :, :].rearrange("(t p) n -> p t n", p=P)).then_inc(S("weights"), 16)
            if l + 1 < LAYERS:
                sp.dma_start(c.wq[:, :, :], c.a["wq4"][l + 1, :, :].rearrange("(t p) n -> p t n", p=P))\
                  .then_inc(S("weights"), 16)
            sp.wait_ge(S("weights"), 32 if l + 1 < LAYERS else 16)
            for u in range(UNROLL):
                sp.wait_ge(S(f"max_placed{u}"), 16 * TURNS + 16 * (u == 3))

        @block.tensor
        def _(pe):
            def loaded(u, t):
                pe.wait_ge(ops.S(f"k_loaded{u}"), 48 * t + 48 * (TURNS * l + 1))
                pe.wait_ge(S(f"q_loaded{u}"), 48 * t + 48)

            def by_queries(n, u, chunk):
                pe.wait_ge(S("s_read"), n + 1)
                t, j = chunk // NCHUNK, chunk % NCHUNK
                pe.matmul(s_bank[chunk % 2], qop[0:r_first, u, t * P:(t + 1) * P],
                          kop[0:r_first, u, j * CHUNK:(j + 1) * CHUNK], start=True, stop=True).then_inc(S("s_psum"), 1)

            def by_keys(n, u, g):
                pe.wait_ge(S("exp_done"), n + 1)
                for j in range(GROUP):
                    k = g * GROUP + j
                    out = st_bank[g % 2][:, j * NT:(j + 1) * NT]
                    ins = pe.matmul(out, kop[0:R_ALL, u, k * P:(k + 1) * P], qop[0:R_ALL, u, :],
                                    start=(j % 2 == 0), stop=(not by_query and j % 2 == 1))
                    if by_query and j % 2 == 1:
                        ins = pe.matmul(st_bank[g % 2][:, (j - 1) * NT:(j + 1) * NT], c.identb[:, :],
                                        c.neg_k[:, k - 1:k + 1, :], start=False, stop=True)
                ins.then_inc(S("st_psum"), 1)

            def values(h, h2, g):
                n = NGROUP * h + g
                pe.wait_ge(S("exp_done"), n + 3)
                if g == 0:
                    pe.wait_ge(S("acc_read"), h + PRIMED)
                if weighted:
                    for j in range(GROUP):
                        pe.matmul(acc_bank[32 * j:32 * j + 32, h2 * NT:(h2 + 1) * NT], c.den16[:, :],
                                  prob[:, g % NP, j * NT:(j + 1) * NT], start=(g == 0), stop=False,
                                  skip_group_check=True)
                    pe.wait_ge(S("weighted"), n + 1)
                for j in range(GROUP):
                    ins = pe.matmul(acc_bank[32 * j:32 * j + 32, h2 * NT:(h2 + 1) * NT],
                                    vop[:, h2, g * GROUP + j, :], used[:, g % NP, j * NT:(j + 1) * NT],
                                    start=(g == 0 and not weighted), stop=(g == NGROUP - 1), skip_group_check=True)
                ins.then_inc(S("pv_psum"), 1)

            def turn_max(h, h2, folded):
                if not isinstance(folded, int) or folded > 0:
                    pe.wait_ge(S("head_done"), folded)
                pe.wait_ge(S("max_found"), h + 1)
                pe.wait_ge(S("max_row"), h)
                for t in range(QT):
                    ins = pe.matmul(mrow_out[:, t * P:(t + 1) * P], nmax[:, h2, t:t + 1], c.ident[:, :],
                                    start=True, stop=True)
                ins.then_inc(S("max_turned"), 1)

            def fold(h, h2, rows):
                pe.wait_ge(S("max_row"), rows)
                pe.wait_ge(S("acc_read"), h + 1 + PRIMED)
                if not isinstance(h, int) or h > 0:
                    pe.wait_ge(S("head_done"), h)
                for t in range(QT):
                    ins = pe.matmul(fold_out[:, t * 32:(t + 1) * 32], acc[:, h2, t * P:(t + 1) * P], c.fold[:, :],
                                    start=True, stop=True)
                ins.then_inc(S("folded"), 1)

            def turn(t, first=False, last=False):
                for u in range(UNROLL):
                    h = UNROLL * t + u
                    h2, u2 = u % 2, (u + 2) % UNROLL
                    ahead = not (last and u >= 2)
                    pe.wait_ge(S(f"max_placed{u}"), 16 * t + 16 + 16 * (u == 3))
                    if ahead:
                        loaded(u2, t + (u + 2) // UNROLL)
                    pe.wait_ge(S("v_filled"), h + 1)
                    for g in range(NGROUP):
                        by_keys(NGROUP * h + g, u, g)
                        if g < LAG and not (first and u == 0):
                            values(h - 1, 1 - h2, NGROUP - LAG + g)
                        if g > LAG:
                            values(h, h2, g - LAG)
                        if ahead:
                            for i in range(2):
                                by_queries(SC * (h + 2) + 2 * g + i, u2, 2 * g + i)
                        if g == LAG:
                            values(h, h2, 0)
                        if g == 1 and not (last and u == 3):
                            turn_max(h + 1, 1 - h2, h - 1)
                        if g == 4 and not (first and u == 0):
                            fold(h - 1, 1 - h2, H if last and u == 3 else h + 2)

            pe.wait_ge(S("values_cleared"), 1)
            for h in range(2):
                loaded(h, 0)
                for chunk in range(SC):
                    by_queries(SC * h + chunk, h, chunk)
                    if h == 1 and chunk == 3:
                        turn_max(0, 0, 0)
            turn(0, first=True)
            with pe.Fori(1, TURNS - 1) as t:
                turn(t)
            turn(TURNS - 1, last=True)
            for g in range(NGROUP - LAG, NGROUP):
                values(H - 1, 1, g)
            fold(H - 1, 1, H)

        @block.scalar
        def _(act):
            def row(h, h2):
                act.wait_ge(S("max_turned"), h + 1)
                act.wait_ge(S("max_split"), h - 1 + PRIMED)
                act.activation(mrow[:, h2, :], mrow_out, ACT.Copy).then_inc(S("max_row"), 1)

            def sums(h, h2):
                act.wait_ge(S("pv_psum"), NGROUP * h + NGROUP + NP)
                act.activation(acc[:, h2, :], acc_bank[:, h2 * NT:(h2 + 1) * NT], ACT.Copy).then_inc(S("acc_read"), 1)

            def turn(t, first=False, last=False):
                for u in range(UNROLL):
                    h = UNROLL * t + u
                    h2 = u % 2
                    for g in range(NGROUP):
                        n = NGROUP * h + g
                        act.wait_ge(S("st_psum"), n + 1)
                        act.wait_ge(S("pv_psum"), n + 1)
                        act.activation(prob[:, g % NP, :], st_bank[g % 2], ACT.Exp).then_inc(S("exp_done"), 1)
                        if g == LAG - 1 and not (first and u == 0):
                            sums(h - 1, 1 - h2)
                        if g == 2 and not (last and u == 3):
                            row(h + 1, 1 - h2)

            act.sem_inc(S("exp_done"), 2)
            act.sem_inc(S("acc_read"), PRIMED)
            act.wait_ge(S("max_turned"), 1)
            act.activation(mrow[:, 0, :], mrow_out, ACT.Copy).then_inc(S("max_row"), 1)
            turn(0, first=True)
            with act.Fori(1, TURNS - 1) as t:
                turn(t)
            turn(TURNS - 1, last=True)
            sums(H - 1, 1)

        @block.vector
        def _(dve):
            def chunk_max(n, h2, chunk):
                t, j = chunk // NCHUNK, chunk % NCHUNK
                if not by_query:
                    dve.wait_ge(S("s_psum"), n + 1)
                if by_query:
                    wait_apart(dve, S("s_psum"), n + 1, 1)
                    dve.wait_ge(S("s_read"), n + 1)
                    dve.tensor_tensor_reduce(out=dump[:, chunk % 2, :], in0=s_bank[chunk % 2],
                                             in1=c.neg_q[:, t, j * CHUNK:(j + 1) * CHUNK], scale=1.0, scalar=-3.0e38,
                                             op0=ALU.add, op1=ALU.max, accum_out=best[:, h2, chunk:chunk + 1])\
                       .then_inc(S("s_read"), 1)
                else:
                    dve.tensor_reduce(best[:, h2, chunk:chunk + 1], s_bank[chunk % 2], AX.X, ALU.max)\
                       .then_inc(S("s_read"), 1)

            def row_max(h, h2):
                dve.wait_ge(S("s_read"), SC * h + SC + 2)
                if not isinstance(h, int) or h >= 2:
                    dve.wait_ge(S("max_turned"), h - 1)
                dve.tensor_reduce(nmax[:, h2, :], best[:, h2, :].rearrange("p (t j) -> p t j", t=QT), AX.X, ALU.max,
                                  negate=True).then_inc(S("max_found"), 1)

            def weigh(n, g):
                dve.wait_ge(S("exp_done"), n + 3)
                dve.wait_ge(S("pv_psum"), n + 1)
                dve.tensor_tensor(used[:, g % NP, :], prob[:, g % NP, :],
                                  c.gT[:, g * GROUP:(g + 1) * GROUP, :].rearrange("p k q -> p (k q)"), ALU.mult)\
                   .then_inc(S("weighted"), 1)

            def normalise(h):
                folded = fold_out.rearrange("p (t e) -> p t e", t=QT)
                dve.wait_ge(S("folded"), h + 1)
                dve.reciprocal(rden[:, :], folded[:, :, HD]).then_inc(S("den_inverted"), 1)
                dve.wait_ge(S("den_inverted"), h + 1)
                dve.tensor_tensor(c.att[:, :, bass.ds(HD * h, HD)], folded[:, :, 0:HD],
                                  rden[:, :].unsqueeze(2).to_broadcast((P, QT, HD)), ALU.mult)\
                   .then_inc(S("head_done"), 1)

            def turn(t, first=False, last=False):
                for u in range(UNROLL):
                    h = UNROLL * t + u
                    h2 = u % 2
                    for g in range(NGROUP):
                        if not (last and u >= 2):
                            for i in range(2):
                                chunk_max(SC * (h + 2) + 2 * g + i, h2, 2 * g + i)
                            if g == NGROUP - 1:
                                row_max(h + 2, h2)
                        if weighted:
                            weigh(NGROUP * h + g, g)
                        if g == 5 and not (first and u == 0):
                            normalise(h - 1)

            dve.sem_inc(S("s_read"), 2)
            for h in range(2):
                for chunk in range(SC):
                    chunk_max(SC * h + chunk, h, chunk)
                row_max(h, h)
            turn(0, first=True)
            with dve.Fori(1, TURNS - 1) as t:
                turn(t)
            turn(TURNS - 1, last=True)
            normalise(H - 1)

        @block.gpsimd
        def _(pool):
            def split(h, h2):
                wait_apart(pool, S("max_row"), h + 1, 1)
                pool.tensor_copy(mpart[:, h2, 0, :], mrow[:, h2, :]).then_inc(S("max_step"), 1)
                pool.wait_ge(S("max_step"), 3 * h + 1)
                pool.tensor_tensor(mrest[:, h2, :], mrow[:, h2, :], mpart[:, h2, 0, :], ALU.subtract)\
                    .then_inc(S("max_step"), 1)
                wait_apart(pool, S("max_step"), 3 * h + 2, 1)
                pool.tensor_copy(mpart[:, h2, 1, :], mrest[:, h2, :]).then_inc(S("max_step"), 1)
                pool.wait_ge(S("max_step"), 3 * h + 3)
                pool.tensor_tensor(mpart[:, h2, 2, :], mrest[:, h2, :], mpart[:, h2, 1, :], ALU.subtract)\
                    .then_inc(S("max_split"), 1)

            def fill(h, h2, u, t):
                wait_apart(pool, ops.S(f"v_loaded{u}"), 16 * t + 16 * (TURNS * l + 1), 16)
                pool.tensor_copy(vop[:, h2, :, 0:HD], vraw[:, u, :].rearrange("p (k e) -> p k e", e=HD))\
                    .then_inc(S("v_filled"), 1)

            pool.memset(qop[96:P, :, :], 1.0 if l == KEYED else 0.0).then_inc(S("qop_set"), 1)
            pool.wait_ge(S("qop_set"), 1)
            pool.memset(vop[:, :, :, HD:32], 0.0).then_inc(S("vop_zero"), 1)
            pool.wait_ge(S("vop_zero"), 1)
            pool.memset(vop[:, :, :, HD:HD + 1], 0.0 if weighted else 1.0).then_inc(S("values_cleared"), 1)
            pool.wait_ge(S("values_cleared"), 1)
            pool.sem_inc(S("pv_psum"), NP)
            pool.sem_inc(S("max_split"), PRIMED)
            pool.sem_inc(S("max_placed3"), 16)
            fill(0, 0, 0, 0)
            fill(1, 1, 1, 0)
            split(0, 0)

            def turn(t, first=False, last=False):
                for u in range(UNROLL):
                    h = UNROLL * t + u
                    if not (last and u == 3):
                        if u == 0:
                            pool.wait_ge(S("max_placed3"), 16 * t + 16)
                        else:
                            pool.wait_ge(S(f"max_placed{u - 1}"), 16 * t + 16)
                        split(h + 1, 1 - u % 2)
                    if not (last and u >= 2):
                        wait_apart(pool, S("pv_psum"), NGROUP * h + NGROUP + NP, NP)
                        fill(h + 2, u % 2, (u + 2) % UNROLL, t + (u + 2) // UNROLL)

            turn(0, first=True)
            with pool.Fori(1, TURNS - 1) as t:
                turn(t)
            turn(TURNS - 1, last=True)


def project_out(c, l):
    nc = c.nc
    with ExitStack() as ctx:
        S = Sems(nc, ctx, f"o{l}")
        block = ctx.enter_context(nc.Block())

        @block.sync
        def _(sp):
            if l + 1 < LAYERS:
                c.ops.load_first(sp, l + 1)

        @block.tensor
        def _(pe):
            turn_pe(c, pe, S, c.att, 0, "att_turned")
            pe.wait_ge(S("attT_ready"), 1)
            by_tokens_pe(c, pe, [c.ps[:, 1, t * D:(t + 1) * D] for t in range(QT)], c.xT, c.wo[:, :, :],
                         c.row(f"bo{l}")).then_inc(S("out_psum"), 1)

        @block.scalar
        def _(act):
            act.wait_ge(S("att_turned"), 1)
            act.activation(c.xT[:, :, :], c.ps[:, 0, :].rearrange("p (t n) -> p t n", t=CT), ACT.Copy)\
               .then_inc(S("attT_ready"), 1)

        @block.vector
        def _(dve):
            dve.wait_ge(S("out_psum"), 1)
            add_stream_dve(c, dve, S, 1)


def turn_act(c, act, S, bank=0, n=0):
    act.wait_ge(S("turned"), n + 1)
    act.activation(c.xT[:, :, :], c.ps[:, bank, :].rearrange("p (t n) -> p t n", t=CT), ACT.Copy)\
       .then_inc(S("xT_ready"), 1)


def halves(c, bank):
    return [c.ps[:, bank, t * D:(t + 1) * D] for t in range(QT)]


def by_channels_pe(c, pe, out, w, srcT, bias=None, n_ct=CT):
    if bias is not None:
        pe.matmul(out, bias, c.ones[0:1, 0:NT], start=True, stop=False)
    for ct in range(n_ct):
        ins = pe.matmul(out, w(ct), srcT[:, ct, :], start=(ct == 0 and bias is None), stop=(ct == n_ct - 1))
    return ins


def tiles(a):
    return a.rearrange("(t p) n -> p t n", p=P)


def taylor(c):
    nc = c.nc
    G = H // 4
    with ExitStack() as ctx:
        S = Sems(nc, ctx, "taylor")
        sb = lambda name, shape, dt: ctx.enter_context(nc.sbuf_tensor(f"t_{name}", shape, dt))
        wq = sb("wq", [P, CT, 4 * P], F32)
        wk = sb("wk", [P, CT, 4 * P], F32)
        wv = sb("wv", [P, CT, D], F32)
        wo = sb("wo", [P, CT, D], F32)
        qT = sb("qT", [P, G, NT], F32)
        kT = sb("kT", [P, G, NT], F32)
        vop = sb("vop", [P, QT, H, 32], F32)
        square = sb("square", [P, 4, 3 * P], F32)
        weight = sb("weight", [P, 8, 3 * P], F32)
        acc = sb("acc", [P, 2, NT], F32)
        den = sb("den", [P, QT, 4], F32)
        block = ctx.enter_context(nc.Block())

        @block.sync
        def _(sp):
            for tile, name in ((wq, "t_wq"), (wk, "t_wk"), (wv, "t_wv"), (wo, "t_wo")):
                sp.dma_start(tile[:, :, :], tiles(c.a[name])).then_inc(S("weights"), 16)
            sp.wait_ge(S("weights"), 64)

        @block.gpsimd
        def _(pool):
            norm_pool(c, pool, S)
            pool.memset(vop[:, :, :, HD:32], 0.0).then_inc(S("vop_zero"), 1)
            pool.wait_ge(S("vop_zero"), 1)
            pool.memset(vop[:, :, :, HD:HD + 1], 1.0).then_inc(S("vop_ones"), 1)

        @block.tensor
        def _(pe):
            pe.wait_ge(S("norm_done"), QT)
            turn_pe(c, pe, S, c.xn, 0, "turned")
            pe.wait_ge(S("xT_ready"), 1)
            pe.wait_ge(S("weights"), 64)
            for w, bank, name in ((wq, 1, "q_psum"), (wk, 3, "k_psum")):
                for m in range(G):
                    ins = by_channels_pe(c, pe, c.ps[:, bank + m // 2, (m % 2) * NT:(m % 2 + 1) * NT],
                                         lambda ct: w[:, ct, m * P:(m + 1) * P], c.xT)
                ins.then_inc(S(name), 1)
            by_tokens_pe(c, pe, halves(c, 5), c.xT, wv, None).then_inc(S("v_psum"), 1)
            pe.wait_ge(S("q_ready"), 1)
            pe.wait_ge(S("k_ready"), 1)

            def scores(g):
                for j in range(4):
                    n = 4 * g + j
                    if n >= 4:
                        pe.wait_ge(S("squared"), n - 3)
                    rows = slice(32 * j, 32 * j + HD)
                    pe.matmul(c.ps[:, 1 + j, 0:NT], kT[rows, g, 0:P], qT[rows, g, :], start=True, stop=True)
                    pe.matmul(c.ps[:, 1 + j, NT:NT + P], kT[rows, g, P:NT], qT[rows, g, P:NT],
                              start=True, stop=True).then_inc(S("s_psum"), 1)

            def values(g):
                if g >= 2:
                    pe.wait_ge(S("acc_read"), g - 1)
                for j in range(4):
                    n = 4 * g + j
                    pe.wait_ge(S("weighted"), n + 1)
                    out = c.ps[32 * j:32 * j + 32, 6 + g % 2, :]
                    pe.matmul(out[:, 0:NT], vop[:, 0, n, :], weight[:, n % 8, 0:NT], start=True, stop=False)
                    ins = pe.matmul(out[:, P:NT], vop[:, 1, n, :], weight[:, n % 8, NT:NT + P], start=False, stop=True)
                ins.then_inc(S("pv_psum"), 1)

            def turn_back(g):
                pe.wait_ge(S("acc_read"), g + 1)
                if g >= 1:
                    pe.wait_ge(S("normalised"), g)
                for t in range(QT):
                    ins = pe.transpose(c.ps[:, 5, t * P:(t + 1) * P], acc[:, g % 2, t * P:(t + 1) * P], c.ident[:, :])
                ins.then_inc(S("turned_back"), 1)

            scores(0)
            pe.wait_ge(S("v_ready"), 1)
            pe.wait_ge(S("vop_ones"), 1)
            for g in range(G):
                if g + 1 < G:
                    scores(g + 1)
                values(g)
                if g >= 1:
                    turn_back(g - 1)
            turn_back(G - 1)
            pe.wait_ge(S("normalised"), G)
            turn_pe(c, pe, S, c.att, 0, "turned")
            pe.wait_ge(S("xT_ready"), 2)
            by_tokens_pe(c, pe, halves(c, 1), c.xT, wo, None).then_inc(S("out_psum"), 1)

        def sums(act, g):
            act.wait_ge(S("pv_psum"), g + 1)
            if g >= 2:
                act.wait_ge(S("turned_back"), g - 1)
            act.activation(acc[:, g % 2, :], c.ps[:, 6 + g % 2, 0:NT], ACT.Copy).then_inc(S("acc_read"), 1)

        @block.scalar
        def _(act):
            turn_act(c, act, S)
            act.wait_ge(S("q_psum"), 1)
            act.mul(qT[:, :, :], c.ps[:, 1:3, :].rearrange("p b (m n) -> p (b m) n", n=NT), 0.25).then_inc(S("q_ready"), 1)
            act.wait_ge(S("v_psum"), 1)
            act.activation(vop[:, :, :, 0:HD].rearrange("p t h e -> p (t h) e"),
                           c.ps[:, 5, :].rearrange("p (n e) -> p n e", e=HD), ACT.Copy).then_inc(S("v_ready"), 1)
            for g in range(G):
                for j in range(4):
                    n = 4 * g + j
                    act.wait_ge(S("s_psum"), n + 1)
                    if n >= 4:
                        act.wait_ge(S("weighted"), n - 3)
                    act.activation(square[:, j, :], c.ps[:, 1 + j, 0:3 * P], ACT.Square, bias=c.ones[:, 0:1])\
                       .then_inc(S("squared"), 1)
                if g >= 1:
                    sums(act, g - 1)
            sums(act, G - 1)
            turn_act(c, act, S, n=1)

        @block.vector
        def _(dve):
            norm_dve(c, dve, S, c.x, c.xn)
            dve.wait_ge(S("k_psum"), 1)
            dve.tensor_copy(kT[:, :, :], c.ps[:, 3:5, :].rearrange("p b (m n) -> p (b m) n", n=NT)).then_inc(S("k_ready"), 1)
            link = Chain(dve, S("den_step"))

            def normalise(g):
                dve.wait_ge(S("turned_back"), g + 1)
                folded = c.ps[:, 5, 0:QT * P].rearrange("p (t j e) -> p t j e", t=QT, j=4)
                link(dve.tensor_scalar(den[:, :, :], folded[:, :, :, HD], 1e-12, None, ALU.add))
                link(dve.reciprocal(den[:, :, :], den[:, :, :]))
                dve.tensor_tensor(c.att[:, :, 64 * g:64 * g + 64].rearrange("p t (j e) -> p t j e", j=4),
                                  folded[:, :, :, 0:HD], den[:, :, :].unsqueeze(3).to_broadcast((P, QT, 4, HD)),
                                  ALU.mult).then_inc(S("normalised"), 1)

            for g in range(G):
                for j in range(4):
                    n = 4 * g + j
                    dve.wait_ge(S("squared"), n + 1)
                    if n >= 8:
                        dve.wait_ge(S("pv_psum"), g - 1)
                    dve.scalar_tensor_tensor(out=weight[:, n % 8, :], in0=square[:, j, :], scalar=1.0,
                                             in1=c.tri[:, :], op0=ALU.add, op1=ALU.mult).then_inc(S("weighted"), 1)
                if g >= 2:
                    normalise(g - 2)
            normalise(G - 2)
            normalise(G - 1)
            dve.wait_ge(S("out_psum"), 1)
            add_stream_dve(c, dve, S, 1)


def first_expert(c):
    nc = c.nc
    with ExitStack() as ctx:
        S = Sems(nc, ctx, "first")
        sb = lambda name, shape, dt: ctx.enter_context(nc.sbuf_tensor(f"f_{name}", shape, dt))
        router = sb("router", [P, CT, E], F32)
        router_b = sb("router_b", [1, E], F32)
        bias = sb("bias", [1, E, D], F32)
        w = sb("w", [P, E, CT, D], F32)
        logits = sb("logits", [P, QT, E], F32)
        top = sb("top", [P, QT, 8], F32)
        where = sb("where", [P, QT, 8], U32)
        where_f = sb("where_f", [P, QT], F32)
        ntop = sb("ntop", [P, QT], F32)
        ex = sb("ex", [P, QT, E], F32)
        total = sb("total", [P, QT], F32)
        gate = sb("gate", [P, QT], F32)
        share = sb("share", [P, QT, E], F32)
        block = ctx.enter_context(nc.Block())

        @block.sync
        def _(sp):
            sp.dma_start(router[:, :, :], tiles(c.a["f_router"])).then_inc(S("router"), 16)
            sp.dma_start(router_b[:, :], c.a["f_router_b"]).then_inc(S("router"), 16)
            sp.dma_start(bias[:, :, :], c.a["f_bias"]).then_inc(S("router"), 16)
            for e in range(E):
                sp.dma_start(w[:, e, :, :], tiles(c.a["f_w"][e, :, :])).then_inc(S(f"expert{e}"), 16)

        @block.gpsimd
        def _(pool):
            norm_pool(c, pool, S)

        @block.tensor
        def _(pe):
            pe.wait_ge(S("norm_done"), QT)
            turn_pe(c, pe, S, c.xn, 0, "turned")
            pe.wait_ge(S("xT_ready"), 1)
            pe.wait_ge(S("router"), 48)
            by_tokens_pe(c, pe, [c.ps[:, 1, t * E:(t + 1) * E] for t in range(QT)], c.xT, router,
                         router_b[:, :]).then_inc(S("logits"), 1)
            for e in range(E):
                pe.wait_ge(S(f"expert{e}"), 16)
                if e >= 4:
                    pe.wait_ge(S("added"), QT * (e - 3))
                by_tokens_pe(c, pe, halves(c, 2 + e % 4), c.xT, w[:, e, :, :], bias[0:1, e, :]).then_inc(S("e_psum"), 1)

        @block.scalar
        def _(act):
            turn_act(c, act, S)
            act.wait_ge(S("top_found"), 1)
            for t in range(QT):
                act.activation(ex[:, t, :], logits[:, t, :], ACT.Exp, bias=ntop[:, t:t + 1],
                               accum_out=total[:, t:t + 1]).then_inc(S("exp_done"), 1)

        @block.vector
        def _(dve):
            norm_dve(c, dve, S, c.x, c.xn)
            link = Chain(dve, S("step"))
            dve.wait_ge(S("logits"), 1)
            link(dve.tensor_copy(logits[:, :, :], c.ps[:, 1, 0:QT * E].rearrange("p (t e) -> p t e", t=QT)))
            for t in range(QT):
                link(dve.max(top[:, t, :], logits[:, t, :]))
                link(dve.max_index(where[:, t, :], top[:, t, :], logits[:, t, :]))
            dve.tensor_scalar(ntop[:, :], top[:, :, 0], -1.0, None, ALU.mult).then_inc(S("top_found"), 1)
            link(dve.tensor_copy(where_f[:, :], where[:, :, 0]))
            dve.wait_ge(S("exp_done"), QT)
            link(dve.reciprocal(gate[:, :], total[:, :]))
            for t in range(QT):
                link(dve.tensor_scalar(share[:, t, :], c.count8[:, :], where_f[:, t:t + 1], gate[:, t:t + 1],
                                       ALU.is_equal, ALU.mult))
            add_experts_dve(c, dve, S, share, [2 + e % 4 for e in range(E)])


def add_experts_dve(c, dve, S, share, banks):
    for e in range(E):
        dve.wait_ge(S("e_psum"), e + 1)
        if e >= 1:
            dve.wait_ge(S("added"), QT * e)
        for t in range(QT):
            dve.scalar_tensor_tensor(out=c.x[:, t, :], in0=halves(c, banks[e])[t], scalar=share[:, t, e:e + 1],
                                     in1=c.x[:, t, :], op0=ALU.mult, op1=ALU.add).then_inc(S("added"), 1)
    dve.wait_ge(S("added"), QT * E)


def frames(c):
    nc = c.nc
    HN, DH, FR = 16, 64, 64
    INNER = HN * DH
    M = INNER // P
    with ExitStack() as ctx:
        S = Sems(nc, ctx, "frames")
        sb = lambda name, shape, dt: ctx.enter_context(nc.sbuf_tensor(f"m_{name}", shape, dt))
        w = sb("w", [P, 3, CT, INNER], F32)
        wo = sb("wo", [P, M, D], F32)
        gb = sb("gb", [P, 2, D], F32)
        bo = sb("bo", [1, D], F32)
        qT = sb("qT", [P, M, NT], F32)
        kT = sb("kT", [P, M, NT], F32)
        v = sb("v", [P, QT, INNER], F32)
        mask = sb("mask", [P, 3 * P], F32)
        s = sb("s", [P, 2, 3 * P], F32)
        top = sb("top", [P, 2, QT], F32)
        ntop = sb("ntop", [P, 2, QT], F32)
        p = sb("p", [P, 2, 3 * P], F32)
        total = sb("total", [P, 2, QT], F32)
        rden = sb("rden", [P, 2, QT], F32)
        pn = sb("pn", [P, 2, 3 * P], F32)
        pT = sb("pT", [P, 2, 3 * P], F32)
        oT = sb("oT", [P, M, NT], F32)
        block = ctx.enter_context(nc.Block())
        cols = [slice(0, P), slice(P, 3 * P)]

        @block.sync
        def _(sp):
            sp.dma_start(gb[:, 0, :], c.a["m_g"].to_broadcast((P, D))).then_inc(S("scales"), 16)
            sp.dma_start(gb[:, 1, :], c.a["m_b"].to_broadcast((P, D))).then_inc(S("scales"), 16)
            for k in range(3):
                sp.dma_start(w[:, k, :, :], tiles(c.a["m_w"])[:, :, k * INNER:(k + 1) * INNER]).then_inc(S(f"w{k}"), 16)
            sp.dma_start(wo[:, :, :], tiles(c.a["m_wo"])).then_inc(S("wo"), 16)
            sp.dma_start(bo[:, :], c.a["m_bo"]).then_inc(S("wo"), 16)

        @block.gpsimd
        def _(pool):
            norm_pool(c, pool, S)
            pool.memset(mask[:, :], 0.0).then_inc(S("mask"), 1)
            pool.wait_ge(S("mask"), 1)
            pool.memset(mask[0:FR, FR:2 * FR], NEG).then_inc(S("mask"), 1)
            pool.memset(mask[0:FR, P + 3 * FR:P + 4 * FR], NEG).then_inc(S("mask"), 1)
            norm_pool(c, pool, S, 1)

        @block.tensor
        def _(pe):
            pe.wait_ge(S("scaled"), 2 * QT)
            turn_pe(c, pe, S, c.att, 0, "turned")
            pe.wait_ge(S("xT_ready"), 1)
            n = 0
            for k in range(2):
                pe.wait_ge(S(f"w{k}"), 16)
                for m in range(0, M, 2):
                    if n >= 4:
                        pe.wait_ge(S("qk_read"), n - 3)
                    for i in range(2):
                        ins = by_channels_pe(c, pe, c.ps[:, 1 + n % 4, i * NT:(i + 1) * NT],
                                             lambda ct: w[:, k, ct, (m + i) * P:(m + i + 1) * P], c.xT)
                    ins.then_inc(S("qk_psum"), 1)
                    n += 1
            pe.wait_ge(S("w2"), 16)
            for i in range(4):
                t, j = i // 2, i % 2
                if i >= 2:
                    pe.wait_ge(S("v_read"), i - 1)
                for ct in range(CT):
                    ins = pe.matmul(c.ps[:, 5 + i % 2, :], c.xT[:, ct, t * P:(t + 1) * P],
                                    w[:, 2, ct, j * 512:(j + 1) * 512], start=(ct == 0), stop=(ct == CT - 1))
                ins.then_inc(S("v_psum"), 1)

            def scores(h):
                if h >= 2:
                    pe.wait_ge(S("s_read"), QT * (h - 1))
                r, m = slice(DH * (h % 2), DH * (h % 2) + DH), h // 2
                pe.matmul(c.ps[:, 1 + h % 2, cols[0]], qT[r, m, 0:P], kT[r, m, 0:P], start=True, stop=True)
                pe.matmul(c.ps[:, 1 + h % 2, cols[1]], qT[r, m, P:NT], kT[r, m, :], start=True, stop=True)\
                  .then_inc(S("s_psum"), 1)

            def turn_p(h):
                pe.wait_ge(S("p_scaled"), QT * (h + 1))
                if h >= 2:
                    pe.wait_ge(S("pT_ready"), h - 1)
                for i in range(3):
                    ins = pe.transpose(c.ps[:, 3 + h % 2, i * P:(i + 1) * P], pn[:, h % 2, i * P:(i + 1) * P],
                                       c.ident[:, :])
                ins.then_inc(S("p_turned"), 1)

            def values(h):
                pe.wait_ge(S("pT_ready"), h + 1)
                if h >= 4 and h % 2 == 0:
                    pe.wait_ge(S("o_read"), h // 2 - 1)
                if h == 0:
                    pe.wait_ge(S("v_read"), 4)
                out = c.ps[DH * (h % 2):DH * (h % 2) + DH, 5 + (h // 2) % 2, :]
                hs = slice(h * DH, (h + 1) * DH)
                pe.matmul(out[:, 0:NT], v[:, 0, hs], pT[:, h % 2, 0:NT], start=True, stop=False)
                pe.matmul(out[:, P:NT], v[:, 1, hs], pT[:, h % 2, NT:NT + P], start=False, stop=True)\
                  .then_inc(S("pv_psum"), 1)

            pe.wait_ge(S("qk_read"), M)
            for h in range(HN + 2):
                if h < HN:
                    scores(h)
                if 1 <= h <= HN:
                    turn_p(h - 1)
                if h >= 2:
                    values(h - 2)
            pe.wait_ge(S("wo"), 32)
            pe.wait_ge(S("o_read"), M)
            by_tokens_pe(c, pe, halves(c, 7), oT, wo, bo[:, :], M).then_inc(S("out_psum"), 1)

        def take_out(act, m):
            act.wait_ge(S("pv_psum"), 2 * m + 2)
            act.activation(oT[:, m, :], c.ps[:, 5 + m % 2, 0:NT], ACT.Copy).then_inc(S("o_read"), 1)

        @block.scalar
        def _(act):
            turn_act(c, act, S)
            for n in range(M):
                act.wait_ge(S("qk_psum"), n + 1)
                k, m = n // (M // 2), 2 * (n % (M // 2))
                act.activation((qT, kT)[k][:, m:m + 2, :], c.ps[:, 1 + n % 4, :].rearrange("p (m n) -> p m n", n=NT),
                               ACT.Copy, scale=(DH ** -0.5, 1.0)[k]).then_inc(S("qk_read"), 1)

            def weigh(h):
                act.wait_ge(S("top_negated"), h + 1)
                if h >= 2:
                    act.wait_ge(S("p_scaled"), QT * (h - 1))
                for t in range(QT):
                    act.activation(p[:, h % 2, cols[t]], s[:, h % 2, cols[t]], ACT.Exp, bias=ntop[:, h % 2, t:t + 1],
                                   accum_out=total[:, h % 2, t:t + 1]).then_inc(S("exp_done"), 1)

            def take_turned(h):
                act.wait_ge(S("p_turned"), h + 1)
                if h >= 2:
                    act.wait_ge(S("pv_psum"), h - 1)
                act.activation(pT[:, h % 2, :], c.ps[:, 3 + h % 2, 0:3 * P], ACT.Copy).then_inc(S("pT_ready"), 1)

            for h in range(HN + 1):
                if h < HN:
                    weigh(h)
                if h >= 1:
                    take_turned(h - 1)
                if h >= 3 and h % 2 == 1:
                    take_out(act, h // 2 - 1)
            take_out(act, M - 1)

        @block.vector
        def _(dve):
            norm_dve(c, dve, S, c.x, c.xn)
            dve.wait_ge(S("norm_done"), QT)
            norm_dve(c, dve, S, c.xn, c.att, 1)
            scale_norm_dve(c, dve, S, gb)
            for i in range(4):
                t, j = i // 2, i % 2
                dve.wait_ge(S("v_psum"), i + 1)
                dve.tensor_copy(v[:, t, j * 512:(j + 1) * 512], c.ps[:, 5 + i % 2, :]).then_inc(S("v_read"), 1)
            dve.wait_ge(S("mask"), 3)

            def tops(h):
                dve.wait_ge(S("s_psum"), h + 1)
                if h >= 2:
                    dve.wait_ge(S("exp_done"), QT * (h - 1))
                for t in range(QT):
                    dve.tensor_tensor_reduce(out=s[:, h % 2, cols[t]], in0=c.ps[:, 1 + h % 2, cols[t]],
                                             in1=mask[:, cols[t]], scale=1.0, scalar=-3.0e38, op0=ALU.add,
                                             op1=ALU.max, accum_out=top[:, h % 2, t:t + 1]).then_inc(S("s_read"), 1)
                dve.wait_ge(S("s_read"), QT * (h + 1))
                dve.tensor_scalar(ntop[:, h % 2, :], top[:, h % 2, :], -1.0, None, ALU.mult).then_inc(S("top_negated"), 1)

            def divide(h):
                dve.wait_ge(S("exp_done"), QT * (h + 1))
                dve.reciprocal(rden[:, h % 2, :], total[:, h % 2, :]).then_inc(S("inverted"), 1)
                dve.wait_ge(S("inverted"), h + 1)
                if h >= 2:
                    dve.wait_ge(S("p_turned"), h - 1)
                for t in range(QT):
                    dve.tensor_scalar(pn[:, h % 2, cols[t]], p[:, h % 2, cols[t]], rden[:, h % 2, t:t + 1], None,
                                      ALU.mult).then_inc(S("p_scaled"), 1)

            for h in range(HN + 1):
                if h < HN:
                    tops(h)
                if h >= 1:
                    divide(h - 1)
            dve.wait_ge(S("out_psum"), 1)
            add_stream_dve(c, dve, S, 7)


def scale_norm_dve(c, dve, S, gb):
    dve.wait_ge(S("norm_done"), 2 * QT)
    dve.wait_ge(S("scales"), 32)
    for t in range(QT):
        dve.tensor_tensor(c.att[:, t, :], c.att[:, t, :], gb[:, 0, :], ALU.mult).then_inc(S("scaled"), 1)
    dve.wait_ge(S("scaled"), QT)
    for t in range(QT):
        dve.tensor_tensor(c.att[:, t, :], c.att[:, t, :], gb[:, 1, :], ALU.add).then_inc(S("scaled"), 1)


def experts_pe(c, pe, S, w1, w3, w2, HT):
    HB = HT // 2

    def up(e):
        pe.wait_ge(S(f"up{e}"), 32)
        for b in range(HB):
            n = HB * e + b
            if n >= 2:
                pe.wait_ge(S("gated"), n - 1)
            for w, bank, name in ((w1, 1, "gate_psum"), (w3, 3, "up_psum")):
                for i in range(2):
                    m = 2 * b + i
                    ins = by_channels_pe(c, pe, c.ps[:, bank + n % 2, i * NT:(i + 1) * NT],
                                         lambda ct: w[:, e, ct, m * P:(m + 1) * P], c.xT)
                ins.then_inc(S(name), 1)

    def down(e):
        pe.wait_ge(S(f"down{e}"), 16)
        pe.wait_ge(S("gated"), HB * (e + 1))
        if e >= 2:
            pe.wait_ge(S("added"), QT * (e - 1))
        by_tokens_pe(c, pe, halves(c, 5 + e % 2), c.hT(e), w2[:, e, :, :], None, HT).then_inc(S("e_psum"), 1)

    for e in range(E + 1):
        if e < E:
            up(e)
        if e >= 1:
            down(e - 1)


def experts_act(c, act, S, HT, silu):
    HB = HT // 2
    for n in range(HB * E):
        act.wait_ge(S("gate_psum"), n + 1)
        if n >= 2:
            act.wait_ge(S("gated"), n - 1)
        act.activation(silu[:, n % 2, :], c.ps[:, 1 + n % 2, :], ACT.Silu).then_inc(S("silu_done"), 1)


def experts_dve(c, dve, S, HT, silu, share):
    HB = HT // 2

    def add(e):
        dve.wait_ge(S("e_psum"), e + 1)
        if e >= 1:
            dve.wait_ge(S("added"), QT * e)
        for t in range(QT):
            dve.scalar_tensor_tensor(out=c.x[:, t, :], in0=halves(c, 5 + e % 2)[t], scalar=share[:, t, e:e + 1],
                                     in1=c.x[:, t, :], op0=ALU.mult, op1=ALU.add).then_inc(S("added"), 1)

    for e in range(E):
        for b in range(HB):
            n = HB * e + b
            dve.wait_ge(S("silu_done"), n + 1)
            dve.wait_ge(S("up_psum"), n + 1)
            if b == 0 and e >= 2:
                dve.wait_ge(S("e_psum"), e - 1)
            dve.tensor_tensor(c.hT(e)[:, 2 * b:2 * b + 2, :], c.ps[:, 3 + n % 2, :].rearrange("p (m n) -> p m n", n=NT),
                              silu[:, n % 2, :].rearrange("p (m n) -> p m n", n=NT), ALU.mult).then_inc(S("gated"), 1)
        if e >= 1:
            add(e - 1)
    add(E - 1)
    dve.wait_ge(S("added"), QT * E)


def load_experts(c, sp, S, prefix, w1, w3, w2):
    for e in range(E):
        sp.dma_start(w1[:, e, :, :], tiles(c.a[f"{prefix}_w1"][e, :, :])).then_inc(S(f"up{e}"), 16)
        sp.dma_start(w3[:, e, :, :], tiles(c.a[f"{prefix}_w3"][e, :, :])).then_inc(S(f"up{e}"), 16)
        sp.dma_start(w2[:, e, :, :], tiles(c.a[f"{prefix}_w2"][e, :, :])).then_inc(S(f"down{e}"), 16)


def experts_choose(c):
    nc = c.nc
    HIDDEN = 512
    HT = HIDDEN // P
    ROUNDS = NT // E // 8
    TAKEN = -3.0e38
    with ExitStack() as ctx:
        S = Sems(nc, ctx, "choose")
        sb = lambda name, shape, dt: ctx.enter_context(nc.sbuf_tensor(f"e_{name}", shape, dt))
        router = sb("router", [P, CT, E], F32)
        w1 = sb("w1", [P, E, CT, HIDDEN], F32)
        w3 = sb("w3", [P, E, CT, HIDDEN], F32)
        w2 = sb("w2", [P, E, HT, D], F32)
        hidden = sb("hidden", [P, 2, HT, NT], F32)
        silu = sb("silu", [P, 2, 2 * NT], F32)
        score = sb("score", [E, NT], F32)
        left = sb("left", [E, ROUNDS + 1, NT], F32)
        top = sb("top", [E, ROUNDS, 8], F32)
        ntop = sb("ntop", [E, 1], F32)
        ex = sb("ex", [E, NT], F32)
        taken = sb("taken", [E, NT], F32)
        total = sb("total", [E, 1], F32)
        rden = sb("rden", [E, 1], F32)
        share_e = sb("share_e", [E, NT], F32)
        share = sb("share", [P, QT, E], F32)
        c.hT = lambda e: hidden[:, e % 2, :, :]
        block = ctx.enter_context(nc.Block())

        @block.sync
        def _(sp):
            sp.dma_start(router[:, :, :], tiles(c.a["e_router"])).then_inc(S("router"), 16)
            load_experts(c, sp, S, "e", w1, w3, w2)

        @block.gpsimd
        def _(pool):
            norm_pool(c, pool, S)

        @block.tensor
        def _(pe):
            pe.wait_ge(S("norm_done"), QT)
            turn_pe(c, pe, S, c.xn, 0, "turned")
            pe.wait_ge(S("xT_ready"), 1)
            pe.wait_ge(S("router"), 16)
            for ct in range(CT):
                ins = pe.matmul(c.ps[0:E, 7, 0:NT], router[:, ct, :], c.xT[:, ct, :], start=(ct == 0), stop=(ct == CT - 1))
            ins.then_inc(S("scores"), 1)
            pe.wait_ge(S("share_found"), 1)
            for t in range(QT):
                ins = pe.transpose(c.ps[:, 0, t * E:(t + 1) * E], share_e[:, t * P:(t + 1) * P], c.ident[0:E, 0:E])
            ins.then_inc(S("share_turned"), 1)
            experts_pe(c, pe, S, w1, w3, w2, HT)

        @block.scalar
        def _(act):
            turn_act(c, act, S)
            act.wait_ge(S("top_found"), 1)
            act.activation(ex[:, :], score[:, :], ACT.Exp, bias=ntop[:, :]).then_inc(S("exp_done"), 1)
            experts_act(c, act, S, HT, silu)

        @block.vector
        def _(dve):
            norm_dve(c, dve, S, c.x, c.xn)
            link = Chain(dve, S("step"))
            dve.wait_ge(S("scores"), 1)
            link(dve.tensor_copy(score[:, :], c.ps[0:E, 7, 0:NT]))
            link(dve.tensor_copy(left[:, 0, :], score[:, :]))
            for r in range(ROUNDS):
                link(dve.max(top[:, r, :], left[:, r, :]))
                if r == 0:
                    dve.tensor_scalar(ntop[:, :], top[:, 0, 0:1], -1.0, None, ALU.mult).then_inc(S("top_found"), 1)
                link(dve.match_replace(out=left[:, r + 1, :], in_to_replace=top[:, r, :], in_values=left[:, r, :],
                                       imm_value=TAKEN))
            link(dve.tensor_scalar(taken[:, :], left[:, ROUNDS, :], 0.9 * TAKEN, None, ALU.is_lt))
            dve.wait_ge(S("exp_done"), 1)
            link(dve.tensor_tensor(taken[:, :], taken[:, :], ex[:, :], ALU.mult))
            link(dve.tensor_reduce(total[:, :], taken[:, :], AX.X, ALU.add))
            link(dve.reciprocal(rden[:, :], total[:, :]))
            dve.tensor_scalar(share_e[:, :], taken[:, :], rden[:, :], None, ALU.mult).then_inc(S("share_found"), 1)
            dve.wait_ge(S("share_turned"), 1)
            link(dve.tensor_copy(share[:, :, :], c.ps[:, 0, 0:QT * E].rearrange("p (t e) -> p t e", t=QT)))
            experts_dve(c, dve, S, HT, silu, share)


def plain_attention(c):
    nc = c.nc
    with ExitStack() as ctx:
        S = Sems(nc, ctx, "plain")
        sb = lambda name, shape, dt: ctx.enter_context(nc.sbuf_tensor(f"s_{name}", shape, dt))
        w = sb("w", [P, 4, CT, D], F32)
        b = sb("b", [1, 4, D], F32)
        qT = sb("qT", [P, CT, NT], F32)
        kT = sb("kT", [P, CT, NT], F32)
        v = sb("v", [P, QT, D], F32)
        ntop = sb("ntop", [P, QT], F32)
        p = sb("p", [P, QT, NT], F32)
        total = sb("total", [P, QT], F32)
        pT = sb("pT", [P, QT, NT], F32)
        oT = sb("oT", [P, CT, NT], F32)
        block = ctx.enter_context(nc.Block())

        @block.sync
        def _(sp):
            sp.dma_start(b[:, :, :], c.a["s_b"]).then_inc(S("weights"), 16)
            for k in range(4):
                sp.dma_start(w[:, k, :, :], tiles(c.a["s_w"][k, :, :])).then_inc(S("weights"), 16)

        @block.gpsimd
        def _(pool):
            norm_pool(c, pool, S)

        @block.tensor
        def _(pe):
            pe.wait_ge(S("norm_done"), QT)
            turn_pe(c, pe, S, c.xn, 0, "turned")
            pe.wait_ge(S("xT_ready"), 1)
            pe.wait_ge(S("weights"), 80)
            for k, name in ((0, "q_psum"), (1, "k_psum")):
                for m in range(CT):
                    ins = by_channels_pe(c, pe, c.ps[:, 1 + k, m * NT:(m + 1) * NT],
                                         lambda ct: w[:, k, ct, m * P:(m + 1) * P], c.xT, b[0:1, k, m * P:(m + 1) * P])
                ins.then_inc(S(name), 1)
            by_tokens_pe(c, pe, halves(c, 3), c.xT, w[:, 2, :, :], b[0:1, 2, :]).then_inc(S("v_psum"), 1)
            pe.wait_ge(S("q_ready"), 1)
            pe.wait_ge(S("k_ready"), 1)
            for t in range(QT):
                for ct in range(CT):
                    ins = pe.matmul(c.ps[:, 4, t * NT:(t + 1) * NT], qT[:, ct, t * P:(t + 1) * P], kT[:, ct, :],
                                    start=(ct == 0), stop=(ct == CT - 1))
            ins.then_inc(S("s_psum"), 1)
            pe.wait_ge(S("p_scaled"), QT)
            turn_pe(c, pe, S, p, 5, "p_turned")
            pe.wait_ge(S("pT_ready"), 1)
            pe.wait_ge(S("v_ready"), 1)
            for m in range(CT):
                for k in range(QT):
                    ins = pe.matmul(c.ps[:, 6, m * NT:(m + 1) * NT], v[:, k, m * P:(m + 1) * P], pT[:, k, :],
                                    start=(k == 0), stop=(k == QT - 1))
            ins.then_inc(S("o_psum"), 1)
            pe.wait_ge(S("oT_ready"), 1)
            by_tokens_pe(c, pe, halves(c, 7), oT, w[:, 3, :, :], b[0:1, 3, :]).then_inc(S("out_psum"), 1)

        @block.scalar
        def _(act):
            turn_act(c, act, S)
            act.wait_ge(S("q_psum"), 1)
            act.mul(qT[:, :, :], c.ps[:, 1, :].rearrange("p (m n) -> p m n", n=NT), D ** -0.5).then_inc(S("q_ready"), 1)
            act.wait_ge(S("v_psum"), 1)
            act.activation(v[:, :, :], c.ps[:, 3, :].rearrange("p (m n) -> p m n", n=NT), ACT.Copy).then_inc(S("v_ready"), 1)
            act.wait_ge(S("top_found"), 1)
            for t in range(QT):
                act.activation(p[:, t, :], c.ps[:, 4, t * NT:(t + 1) * NT], ACT.Exp, bias=ntop[:, t:t + 1],
                               accum_out=total[:, t:t + 1]).then_inc(S("exp_done"), 1)
            act.wait_ge(S("p_turned"), 1)
            act.activation(pT[:, :, :], c.ps[:, 5, :].rearrange("p (m n) -> p m n", n=NT), ACT.Copy)\
               .then_inc(S("pT_ready"), 1)
            act.wait_ge(S("o_psum"), 1)
            act.activation(oT[:, :, :], c.ps[:, 6, :].rearrange("p (m n) -> p m n", n=NT), ACT.Copy)\
               .then_inc(S("oT_ready"), 1)

        @block.vector
        def _(dve):
            norm_dve(c, dve, S, c.x, c.xn)
            dve.wait_ge(S("k_psum"), 1)
            dve.tensor_copy(kT[:, :, :], c.ps[:, 2, :].rearrange("p (m n) -> p m n", n=NT)).then_inc(S("k_ready"), 1)
            dve.wait_ge(S("s_psum"), 1)
            dve.tensor_reduce(ntop[:, :], c.ps[:, 4, :].rearrange("p (t k) -> p t k", t=QT), AX.X, ALU.max, negate=True)\
               .then_inc(S("top_found"), 1)
            dve.wait_ge(S("exp_done"), QT)
            link = Chain(dve, S("step"))
            link(dve.reciprocal(total[:, :], total[:, :]))
            for t in range(QT):
                dve.tensor_scalar(p[:, t, :], p[:, t, :], total[:, t:t + 1], None, ALU.mult).then_inc(S("p_scaled"), 1)
            dve.wait_ge(S("out_psum"), 1)
            add_stream_dve(c, dve, S, 7)


def zone_experts(c):
    nc = c.nc
    CENTER, LOWER, UPPER = 1.0 / math.e, 0.5 - math.log(4.0 / 3.0), 0.5
    FLOOR = 1e-8
    HIDDEN = 256
    HT = HIDDEN // P
    with ExitStack() as ctx:
        S = Sems(nc, ctx, "zone")
        sb = lambda name, shape, dt: ctx.enter_context(nc.sbuf_tensor(f"z_{name}", shape, dt))
        router = sb("router", [P, CT, E], F32)
        temp = sb("temp", [P, 1], F32)
        w1 = sb("w1", [P, E, CT, HIDDEN], F32)
        w3 = sb("w3", [P, E, CT, HIDDEN], F32)
        w2 = sb("w2", [P, E, HT, D], F32)
        hidden = sb("hidden", [P, 2, HT, NT], F32)
        silu = sb("silu", [P, 2, 2 * NT], F32)
        te = lambda name: sb(name, [P, QT, E], F32)
        inh, zone, off, dist, near, fallback = (te(n) for n in ("inh", "zone", "off", "dist", "near", "fallback"))
        picked, second, share = te("picked"), te("second"), te("share")
        total = sb("total", [P, QT], F32)
        none = sb("none", [P, QT], F32)
        some = sb("some", [P, QT], F32)
        top = sb("top", [P, QT, 8], F32)
        where = sb("where", [P, QT, 8], U32)
        where_f = sb("where_f", [P, QT, 2], F32)
        c.hT = lambda e: hidden[:, e % 2, :, :]
        block = ctx.enter_context(nc.Block())

        @block.sync
        def _(sp):
            sp.dma_start(router[:, :, :], tiles(c.a["z_router"])).then_inc(S("router"), 16)
            sp.dma_start(temp[:, :], c.a["z_temp"].to_broadcast((P, 1))).then_inc(S("router"), 16)
            load_experts(c, sp, S, "z", w1, w3, w2)

        @block.gpsimd
        def _(pool):
            norm_pool(c, pool, S)

        @block.tensor
        def _(pe):
            pe.wait_ge(S("norm_done"), QT)
            turn_pe(c, pe, S, c.xn, 0, "turned")
            pe.wait_ge(S("xT_ready"), 1)
            pe.wait_ge(S("router"), 32)
            by_tokens_pe(c, pe, [c.ps[:, 7, t * E:(t + 1) * E] for t in range(QT)], c.xT, router, None)\
                .then_inc(S("logits"), 1)
            experts_pe(c, pe, S, w1, w3, w2, HT)

        @block.scalar
        def _(act):
            turn_act(c, act, S)
            act.wait_ge(S("logits"), 1)
            act.wait_ge(S("temp_inverted"), 1)
            act.activation(inh[:, :, :], c.ps[:, 7, 0:QT * E].rearrange("p (t e) -> p t e", t=QT), ACT.Sigmoid,
                           scale=temp[:, 0:1]).then_inc(S("inhibited"), 1)
            act.wait_ge(S("dist_found"), 1)
            act.activation(near[:, :, :], dist[:, :, :], ACT.Exp, scale=-1.0 / 0.1).then_inc(S("near_found"), 1)
            act.activation(fallback[:, :, :], dist[:, :, :], ACT.Exp, scale=-1.0 / 0.3).then_inc(S("near_found"), 1)
            experts_act(c, act, S, HT, silu)

        @block.vector
        def _(dve):
            dve.wait_ge(S("router"), 32)
            dve.reciprocal(temp[:, :], temp[:, :]).then_inc(S("temp_inverted"), 1)
            norm_dve(c, dve, S, c.x, c.xn)
            link = Chain(dve, S("step"))
            wide = lambda a: a.unsqueeze(2).to_broadcast((P, QT, E))
            dve.wait_ge(S("inhibited"), 1)
            link(dve.tensor_scalar(off[:, :, :], inh[:, :, :], CENTER, None, ALU.subtract))
            dve.scalar_tensor_tensor(out=dist[:, :, :], in0=off[:, :, :], scalar=-1.0, in1=off[:, :, :], op0=ALU.mult,
                                     op1=ALU.max).then_inc(S("dist_found"), 1)
            link(dve.tensor_scalar(zone[:, :, :], inh[:, :, :], LOWER, None, ALU.is_ge))
            link(dve.scalar_tensor_tensor(out=zone[:, :, :], in0=inh[:, :, :], scalar=UPPER, in1=zone[:, :, :],
                                          op0=ALU.is_le, op1=ALU.mult))
            dve.wait_ge(S("near_found"), 2)
            link(dve.tensor_tensor(near[:, :, :], near[:, :, :], zone[:, :, :], ALU.mult))
            link(dve.tensor_reduce(total[:, :], near[:, :, :], AX.X, ALU.add))
            link(dve.tensor_scalar(none[:, :], total[:, :], FLOOR, None, ALU.is_lt))
            link(dve.tensor_scalar(some[:, :], none[:, :], -1.0, 1.0, ALU.mult, ALU.add))
            for t in range(QT):
                link(dve.max(top[:, t, :], fallback[:, t, :]))
                link(dve.max_index(where[:, t, :], top[:, t, :], fallback[:, t, :]))
            link(dve.tensor_copy(where_f[:, :, :], where[:, :, 0:2]))
            for t in range(QT):
                link(dve.tensor_scalar(picked[:, t, :], c.count8[:, :], where_f[:, t, 0:1], None, ALU.is_equal))
                link(dve.scalar_tensor_tensor(out=second[:, t, :], in0=c.count8[:, :], scalar=where_f[:, t, 1:2],
                                              in1=picked[:, t, :], op0=ALU.is_equal, op1=ALU.add))
            link(dve.tensor_tensor(fallback[:, :, :], fallback[:, :, :], second[:, :, :], ALU.mult))
            link(dve.tensor_reduce(total[:, :], fallback[:, :, :], AX.X, ALU.add))
            link(dve.tensor_scalar(total[:, :], total[:, :], FLOOR, None, ALU.max))
            link(dve.reciprocal(total[:, :], total[:, :]))
            link(dve.tensor_tensor(total[:, :], total[:, :], none[:, :], ALU.mult))
            link(dve.tensor_tensor(fallback[:, :, :], fallback[:, :, :], wide(total[:, :]), ALU.mult))
            link(dve.tensor_tensor(near[:, :, :], near[:, :, :], wide(some[:, :]), ALU.mult))
            link(dve.tensor_tensor(near[:, :, :], near[:, :, :], fallback[:, :, :], ALU.add))
            link(dve.tensor_reduce(total[:, :], near[:, :, :], AX.X, ALU.add))
            link(dve.tensor_scalar(total[:, :], total[:, :], FLOOR, None, ALU.max))
            link(dve.reciprocal(total[:, :], total[:, :]))
            link(dve.tensor_tensor(share[:, :, :], near[:, :, :], wide(total[:, :]), ALU.mult))
            experts_dve(c, dve, S, HT, silu, share)


def recurrence(c):
    nc = c.nc
    with ExitStack() as ctx:
        S = Sems(nc, ctx, "gru")
        sb = lambda name, shape, dt: ctx.enter_context(nc.sbuf_tensor(f"r_{name}", shape, dt))
        w = sb("w", [P, 2, CT, D], F32)
        b = sb("b", [1, 2, D], F32)
        gb = sb("gb", [P, 2, D], F32)
        z = sb("z", [P, CT, NT], F32)
        keep = sb("keep", [P, CT, NT], F32)
        zc = sb("zc", [P, CT, NT], F32)
        hT = sb("hT", [P, CT, NT], F32)
        block = ctx.enter_context(nc.Block())

        @block.sync
        def _(sp):
            sp.dma_start(gb[:, 0, :], c.a["r_g"].to_broadcast((P, D))).then_inc(S("scales"), 16)
            sp.dma_start(gb[:, 1, :], c.a["r_b"].to_broadcast((P, D))).then_inc(S("scales"), 16)
            sp.dma_start(b[:, :, :], c.a["r_bias"]).then_inc(S("weights"), 16)
            for k in range(2):
                sp.dma_start(w[:, k, :, :], tiles(c.a["r_w"][k, :, :])).then_inc(S("weights"), 16)

        @block.gpsimd
        def _(pool):
            norm_pool(c, pool, S)
            norm_pool(c, pool, S, 1)

        @block.tensor
        def _(pe):
            pe.wait_ge(S("scaled"), 2 * QT)
            turn_pe(c, pe, S, c.att, 0, "turned")
            pe.wait_ge(S("xT_ready"), 1)
            pe.wait_ge(S("weights"), 48)
            for k, name in ((0, "z_psum"), (1, "c_psum")):
                for m in range(CT):
                    ins = by_channels_pe(c, pe, c.ps[:, 1 + k, m * NT:(m + 1) * NT],
                                         lambda ct: w[:, k, ct, m * P:(m + 1) * P], c.xT, b[0:1, k, m * P:(m + 1) * P])
                ins.then_inc(S(name), 1)
            pe.wait_ge(S("scanned"), CT)
            turn_pe(c, pe, S, hT, 3, "h_turned")

        @block.scalar
        def _(act):
            turn_act(c, act, S)
            act.wait_ge(S("z_psum"), 1)
            act.activation(z[:, :, :], c.ps[:, 1, :].rearrange("p (m n) -> p m n", n=NT), ACT.Sigmoid)\
               .then_inc(S("z_ready"), 1)

        @block.vector
        def _(dve):
            norm_dve(c, dve, S, c.x, c.xn)
            dve.wait_ge(S("norm_done"), QT)
            norm_dve(c, dve, S, c.xn, c.att, 1)
            scale_norm_dve(c, dve, S, gb)
            dve.tensor_tensor(c.x[:, :, :], c.x[:, :, :], c.xn[:, :, :], ALU.add).then_inc(S("norm_added"), 1)
            dve.wait_ge(S("z_ready"), 1)
            dve.tensor_scalar(keep[:, :, :], z[:, :, :], -1.0, 1.0, ALU.mult, ALU.add).then_inc(S("gates"), 1)
            dve.wait_ge(S("c_psum"), 1)
            dve.tensor_tensor(zc[:, :, :], c.ps[:, 2, :].rearrange("p (m n) -> p m n", n=NT), z[:, :, :], ALU.mult)\
               .then_inc(S("gates"), 1)
            dve.wait_ge(S("gates"), 2)
            for m in range(CT):
                dve.tensor_tensor_scan(hT[:, m, :], keep[:, m, :], zc[:, m, :], 0.0, ALU.mult, ALU.add)\
                   .then_inc(S("scanned"), 1)
            dve.wait_ge(S("h_turned"), 1)
            dve.wait_ge(S("norm_added"), 1)
            add_stream_dve(c, dve, S, 3)


def feed_forward(c):
    nc = c.nc
    HIDDEN = 1024
    HT = HIDDEN // P
    with ExitStack() as ctx:
        S = Sems(nc, ctx, "ffn")
        sb = lambda name, shape, dt: ctx.enter_context(nc.sbuf_tensor(f"g_{name}", shape, dt))
        w1 = sb("w1", [P, CT, HIDDEN], F32)
        w2 = sb("w2", [P, HT, D], F32)
        b1 = sb("b1", [P, HT], F32)
        b2 = sb("b2", [1, D], F32)
        hT = sb("hT", [P, HT, NT], F32)
        block = ctx.enter_context(nc.Block())

        @block.sync
        def _(sp):
            sp.dma_start(b1[:, :], c.a["g_b1"]).then_inc(S("w1"), 16)
            sp.dma_start(w1[:, :, :], tiles(c.a["g_w1"])).then_inc(S("w1"), 16)
            sp.dma_start(b2[:, :], c.a["g_b2"]).then_inc(S("w2"), 16)
            sp.dma_start(w2[:, :, :], tiles(c.a["g_w2"])).then_inc(S("w2"), 16)

        @block.gpsimd
        def _(pool):
            norm_pool(c, pool, S)

        @block.tensor
        def _(pe):
            pe.wait_ge(S("norm_done"), QT)
            turn_pe(c, pe, S, c.xn, 0, "turned")
            pe.wait_ge(S("xT_ready"), 1)
            pe.wait_ge(S("w1"), 32)
            for m in range(HT):
                if m >= 6:
                    pe.wait_ge(S("gelu_done"), m - 5)
                by_channels_pe(c, pe, c.ps[:, 1 + m % 6, 0:NT], lambda ct: w1[:, ct, m * P:(m + 1) * P], c.xT)\
                    .then_inc(S("h_psum"), 1)
            pe.wait_ge(S("w2"), 32)
            pe.wait_ge(S("gelu_done"), HT)
            by_tokens_pe(c, pe, halves(c, 7), hT, w2, b2[:, :], HT).then_inc(S("out_psum"), 1)

        @block.scalar
        def _(act):
            turn_act(c, act, S)
            for m in range(HT):
                act.wait_ge(S("h_psum"), m + 1)
                act.activation(hT[:, m, :], c.ps[:, 1 + m % 6, 0:NT], ACT.Gelu, bias=b1[:, m:m + 1])\
                   .then_inc(S("gelu_done"), 1)

        @block.vector
        def _(dve):
            norm_dve(c, dve, S, c.x, c.xn)
            dve.wait_ge(S("out_psum"), 1)
            add_stream_dve(c, dve, S, 7)


def program(nc, a, out, steps=None):
    ctx = ExitStack()
    with ctx:
        c = Core()
        c.nc, c.a = nc, a
        sb = lambda name, shape, dt: ctx.enter_context(nc.sbuf_tensor(name, shape, dt))
        c.ps = ctx.enter_context(nc.psum_tensor("ps", [P, 8, 512], F32))
        c.x = sb("x", [P, QT, D], F32)
        c.xn = sb("xn", [P, QT, D], F32)
        c.xT = sb("xT", [P, CT, NT], F32)
        c.att = sb("att", [P, QT, D], F32)
        c.rows = sb("rows", [1, len(ROWS), D], F32)
        c.row = lambda name: c.rows[0:1, ROWS.index(name), :]
        c.wq = sb("wq", [P, CT, D], F32)
        c.wo = sb("wo", [P, CT, D], F32)
        c.ident = sb("ident", [P, P], F32)
        c.identb = sb("identb", [P, P], BF16)
        c.fold = sb("fold", [P, 32], F32)
        c.ones = sb("ones", [P, NT], F32)
        c.minus_half = sb("minus_half", [P, QT], F32)
        c.tri = sb("tri", [P, 3 * P], F32)
        c.den16 = sb("den16", [P, 32], F32)
        c.count8 = sb("count8", [P, E], F32)
        c.count8_i = sb("count8_i", [P, E], I32)
        c.stats = sb("stats", [P, QT, 6], F32)
        c.moments = sb("moments", [P, QT, 2], F32)
        c.var = sb("var", [P, QT], F32)
        c.rstd = sb("rstd", [P, QT], F32)
        c.kparts = nc.dram_tensor("kparts", (LAYERS, 3, D, KEYS), BF16).ap()
        c.qparts = nc.dram_tensor("qparts", (3, D, NT), BF16).ap()
        c.vals = nc.dram_tensor("vals", (LAYERS, P, KT * D), F32).ap()

        c.ops = Operands(c, ctx)
        constants(c)
        steps = 12 if steps is None else steps
        with ExitStack() as masks:
            sb = lambda name, shape, dt: masks.enter_context(nc.sbuf_tensor(name, shape, dt))
            c.neg_q = sb("neg_q", [P, QT, KEYS], BF16)
            c.neg_k = sb("neg_k", [P, KT, NT], BF16)
            with nc.sbuf_tensor("gT", [P, KT, NT], F32) as c.gT:
                project_context(c)
                cross(c, 0, True, True)
            taylor(c)
            first_expert(c)
            cross(c, 1, True, False)
        frames(c)
        experts_choose(c)
        cross(c, 2, False, False)
        plain_attention(c)
        zone_experts(c)
        cross(c, 3, False, False)
        recurrence(c)
        feed_forward(c)
        store(c, out)


def cross(c, l, by_query, weighted):
    queries(c, l)
    attend(c, l, by_query, weighted)
    project_out(c, l)


def store(c, out):
    nc = c.nc
    with ExitStack() as ctx:
        S = Sems(nc, ctx, "end")
        block = ctx.enter_context(nc.Block())

        @block.sync
        def _(sp):
            sp.dma_start(out.rearrange("(t p) d -> p t d", p=P), c.x[:, :, :]).then_inc(S("stored"), 16)
            sp.wait_ge(S("stored"), 16)


ROWS = ["bq0", "bq1", "bq2", "bq3", "bo0", "bo1", "bo2", "bo3"]


def kernel(**inputs):
    import numpy as np
    import concourse.bacc as bacc
    from concourse.bass_utils import run_bass_kernel_spmd

    arrays = lay_out(inputs, np)
    nc = bacc.Bacc("TRN2", target_bir_lowering=False, num_devices=1)
    a = {name: nc.dram_tensor(f"in_{name}", v.shape, mybir.dt.from_np(v.dtype), kind="ExternalInput").ap()
         for name, v in arrays.items()}
    out = nc.dram_tensor("out", (NT, D), F32, kind="ExternalOutput").ap()
    program(nc, a, out)
    r = run_bass_kernel_spmd(nc, [{f"in_{name}": v for name, v in arrays.items()}], core_ids=[0])
    return r.results[0]["out"].reshape(1, NT, D)


def lay_out(inputs, np):
    i = {k: np.asarray(v) for k, v in inputs.items()}
    stack = lambda names, turn=(): np.ascontiguousarray(
        np.stack([i[n].T if n in turn else i[n] for n in names]))
    names = {"q": ["L0_xattn_wq_k", "L1_xattn_wq_kernel", "L2_xattn_Wq", "L3_xattn_Wq"],
             "k": ["L0_xattn_wk_k", "L1_xattn_wk_kernel", "L2_xattn_Wk", "L3_xattn_Wk"],
             "v": ["L0_xattn_wv_k", "L1_xattn_wv_kernel", "L2_xattn_Wv", "L3_xattn_Wv"],
             "o": ["L0_xattn_wo_k", "L1_xattn_wo_kernel", "L2_xattn_Wo", "L3_xattn_Wo"]}
    bias = {w: [f"L0_xattn_w{w}_b", f"L1_xattn_w{w}_bias", f"L2_xattn_b{w}", f"L3_xattn_b{w}"] for w in "qkvo"}
    out = {f"w{w}4": stack(n, turn=n[2:]) for w, n in names.items()}
    out["bk4"] = np.ascontiguousarray(stack(bias["k"]).reshape(LAYERS, CT, P).transpose(0, 2, 1))
    out["bv4"] = stack(bias["v"])
    out["x"] = i["x"][0]
    out["ctxT"] = np.ascontiguousarray(i["ctx_1024"][0].T)
    out["gT"] = np.ascontiguousarray(i["fside_BxSxS2_0"][0].T)
    out["mask"] = i["mask_BxSxS2_ik1"][0]
    out["maskT"] = np.ascontiguousarray(i["mask_BxSxS2_ik1"][0].T)
    out["mask_keys"] = np.ascontiguousarray(i["mask_Bx1xS2_bf1"][0]).view(np.uint8)
    for w in "qk":
        spaced = np.zeros((D, H, 32), np.float32)
        spaced[:, :, :HD] = i[f"L0_attn_W{w}"].T.reshape(D, H, HD)
        out[f"t_w{w}"] = spaced.reshape(D, H * 32)
    for w in "vo":
        out[f"t_w{w}"] = np.ascontiguousarray(i[f"L0_attn_W{w}"].T)
    out["f_router"] = i["L0_ffn_router_w"]
    out["f_router_b"] = i["L0_ffn_router_b"][None]
    out["f_bias"] = i["L0_ffn_expert_b"][None]
    out["f_w"] = i["L0_ffn_expert_w"]
    out["m_g"], out["m_b"] = i["L1_attn_g"][0], i["L1_attn_b"][0]
    out["m_w"], out["m_wo"], out["m_bo"] = i["L1_attn_w_qkv"], i["L1_attn_w_out"], i["L1_attn_b_out"][None]
    turned = lambda a: np.ascontiguousarray(a.transpose(0, 2, 1))
    out["e_router"] = np.ascontiguousarray(i["L1_ffn_Wg"].T)
    for n in "123":
        out[f"e_w{n}"] = turned(i[f"L1_ffn_W{n}"])
    out["s_w"] = np.stack([i[f"L2_attn_W{n}"] for n in "1234"])
    out["s_b"] = np.stack([i[f"L2_attn_b{n}"] for n in "1234"])[None]
    out["z_router"], out["z_temp"] = i["L2_ffn_Wr"], i["L2_ffn_temperature"][None]
    out["z_w1"], out["z_w3"], out["z_w2"] = i["L2_ffn_Wg"], i["L2_ffn_Wu"], i["L2_ffn_Wd"]
    out["r_g"], out["r_b"] = i["L3_attn_gamma"][None], i["L3_attn_beta"][None]
    out["r_w"] = np.stack([i["L3_attn_Wg"].T, i["L3_attn_Wc"].T])
    out["r_bias"] = np.stack([i["L3_attn_bg"], i["L3_attn_bc"]])[None]
    out["g_w1"], out["g_w2"], out["g_b2"] = i["L3_ffn_w1"], i["L3_ffn_w2"], i["L3_ffn_b2"][None]
    out["g_b1"] = np.ascontiguousarray(i["L3_ffn_b1"].reshape(-1, P).T)
    rows = [i[n] for n in bias["q"] + bias["o"]]
    out["rows"] = np.stack(rows)[None]
    return out
```

```python
import math
from contextlib import ExitStack

import concourse.bass as bass
from concourse import mybir

F32 = mybir.dt.float32
BF16 = mybir.dt.bfloat16
I32 = mybir.dt.int32
U32 = mybir.dt.uint32
U8 = mybir.dt.uint8
ALU = mybir.AluOpType
ACT = mybir.ActivationFunctionType
AX = mybir.AxisListType

P = 128
D = 256
NT = 256
QT = NT // P
CT = D // P
KEYS = 4096
KT = KEYS // P
H = 16
HD = D // H
LAYERS = 4
CHUNK = 512
NCHUNK = KEYS // CHUNK
GROUP = 4
NGROUP = KT // GROUP
UNROLL = 4
NP = 4
LAG = 2
Q_SCALE = float(HD) ** -0.5
KEYED = 2
PRIMED = 1
NORM_FILL, FOLD_FILL, TOP_FILL = 16, 6, 28
NEG = -(2.0 ** 100)
E = 8
EPS = 1e-5

PARTS_BESIDE = [3, 2, 2]
PAIRS = [(k, q) for k, n in enumerate(PARTS_BESIDE) for q in range(n)]
R_MASK = len(PAIRS) * HD
R_MAX = R_MASK + 1
R_ALL = R_MAX + 3


class Sems:

    def __init__(self, nc, ctx, prefix):
        self.nc, self.prefix, self.made = nc, prefix, {}
        ctx.callback(self.clear)

    def clear(self):
        for sem in self.made.values():
            self.nc.gpsimd.sem_clear(sem)
            self.nc.release_semaphore(sem)

    def __call__(self, name):
        if name not in self.made:
            self.made[name] = self.nc.alloc_semaphore(f"{self.prefix}_{name}")
        return self.made[name]


class Chain:

    def __init__(self, eng, sem):
        self.eng, self.sem, self.n = eng, sem, 0

    def __call__(self, ins):
        self.n += 1
        ins.then_inc(self.sem, 1)
        self.eng.wait_ge(self.sem, self.n)


def wait_apart(eng, sem, value, least):
    value = value if isinstance(value, int) else eng.to_reg(value)
    eng.wait_ge(sem, least)
    eng.wait_ge(sem, value)


class Core:
    pass


def norm_dve(c, dve, S, src, dst, n=0):
    for t in range(QT):
        dve.bn_stats(c.stats[:, t, :], src[:, t, :]).then_inc(S("norm_stats"), 1)
    dve.wait_ge(S("norm_stats"), QT * (n + 1))
    for t in range(QT):
        dve.bn_aggr(c.moments[:, t, :], c.stats[:, t, :]).then_inc(S("norm_moments"), 1)
    dve.wait_ge(S("norm_moments"), QT * (n + 1))
    dve.tensor_scalar(c.var[:, :], c.moments[:, :, 1], EPS, None, ALU.add).then_inc(S("norm_var"), 1)
    dve.wait_ge(S("norm_rstd"), n + 1)
    for t in range(QT):
        dve.tensor_scalar(dst[:, t, :], src[:, t, :], c.moments[:, t, 0:1], c.rstd[:, t:t + 1],
                          ALU.subtract, ALU.mult).then_inc(S("norm_done"), 1)


def norm_pool(c, pool, S, n=0):
    pool.wait_ge(S("norm_var"), n + 1)
    pool.tensor_tensor(c.rstd[:, :], c.var[:, :], c.minus_half[:, :], ALU.pow).then_inc(S("norm_rstd"), 1)


def turn_pe(c, pe, S, src, bank, name):
    for ct in range(CT):
        for t in range(QT):
            ins = pe.transpose(c.ps[:, bank, ct * NT + t * P:ct * NT + (t + 1) * P],
                               src[:, t, ct * P:(ct + 1) * P], c.ident[:, :])
    ins.then_inc(S(name), 1)


def keep_warm(c, pe, n, bank=7):
    for _ in range(n):
        pe.matmul(c.ps[:, bank, :], c.identb[:, :], c.idle[:, :], start=True, stop=True)


def by_tokens_pe(c, pe, out, srcT, w, bias, n_ct=CT):
    for t in range(QT):
        if bias is not None:
            pe.matmul(out[t], c.ones[0:1, 0:P], bias, start=True, stop=False)
        for ct in range(n_ct):
            ins = pe.matmul(out[t], srcT[:, ct, t * P:(t + 1) * P], w[:, ct, :],
                            start=(ct == 0 and bias is None), stop=(ct == n_ct - 1))
    return ins


def add_stream_dve(c, dve, S, bank):
    dve.tensor_tensor(c.x[:, :, :], c.ps[:, bank, :].rearrange("p (t d) -> p t d", t=QT), c.x[:, :, :],
                      ALU.add).then_inc(S("x_added"), 1)
    dve.wait_ge(S("x_added"), 1)


def constants(c):
    nc = c.nc
    with ExitStack() as ctx:
        S = Sems(nc, ctx, "const")
        block = ctx.enter_context(nc.Block())

        @block.sync
        def _(sp):
            sp.dma_start(c.x[:, :, :], c.a["x"].rearrange("(t p) d -> p t d", p=P)).then_inc(S("loaded"), 16)
            sp.dma_start(c.rows[:, :, :], c.a["rows"]).then_inc(S("loaded"), 16)
            sp.dma_start(c.wq[:, :, :], c.a["wq4"][0, :, :].rearrange("(t p) n -> p t n", p=P)).then_inc(S("loaded"), 16)
            sp.wait_ge(S("loaded"), 48)

        @block.gpsimd
        def _(pool):
            for k, (tile, value) in enumerate([(c.ident, 0.0), (c.identb, 0.0), (c.idle, 0.0), (c.fold, 0.0), (c.ones, 1.0),
                                               (c.minus_half, -0.5), (c.tri, 0.5), (c.den16, 0.0)]):
                pool.memset(tile[:, :], value).then_inc(S("filled"), 1)
            pool.wait_ge(S("filled"), 8)
            for tile in (c.ident, c.identb):
                pool.affine_select(out=tile[:, :], in_=tile[:, :], compare_op=ALU.not_equal, fill=1.0, base=0,
                                   pattern=[[-1, P]], channel_multiplier=1).then_inc(S("placed"), 1)
            for g in range(4):
                pool.affine_select(out=c.fold[:, :], in_=c.fold[:, :], compare_op=ALU.not_equal, fill=1.0,
                                   base=-32 * g, pattern=[[-1, 32]], channel_multiplier=1).then_inc(S("placed"), 1)
                pool.wait_ge(S("placed"), 3 + g)
            for at in (0, 2 * P):
                pool.affine_select(out=c.tri[:, at:at + P], in_=c.tri[:, at:at + P], compare_op=ALU.is_ge, fill=0.0,
                                   base=0, pattern=[[1, P]], channel_multiplier=-1).then_inc(S("placed"), 1)
            pool.memset(c.den16[:, HD:HD + 1], 1.0).then_inc(S("placed"), 1)
            pool.iota(c.count8_i[:, :], pattern=[[1, E]], base=0, channel_multiplier=0).then_inc(S("placed"), 1)
            pool.wait_ge(S("placed"), 10)
            pool.tensor_copy(c.count8[:, :], c.count8_i[:, :]).then_inc(S("placed"), 1)
            pool.wait_ge(S("placed"), 11)


def project_context(c):
    nc = c.nc
    NK = CT * NCHUNK
    VB = 8
    NV = KT // VB
    PIECE = KEYS // LAYERS
    PIECES = 2 * QT
    with ExitStack() as ctx:
        S = Sems(nc, ctx, "kv")
        sb = lambda name, shape, dt: ctx.enter_context(nc.sbuf_tensor(name, shape, dt))
        ctxT = sb("ctxT", [P, CT, KEYS], F32)
        wk = sb("wk", [P, CT, D], F32)
        wv = sb("wv", [P, CT, D], F32)
        bk = sb("bk", [P, CT], F32)
        bv = sb("bv", [P, D], F32)
        kp = sb("kp", [P, 4, 3, CHUNK], BF16)
        rest = sb("rest", [P, 2, CHUNK], F32)
        vst = sb("vst", [P, 2, H, VB, HD], F32)
        raw = sb("raw", [P, 2, PIECE], I32)
        block = ctx.enter_context(nc.Block())
        ctx_v = c.a["ctxT"].rearrange("(t p) k -> p t k", p=P)
        vout = c.vals.rearrange("l p (h k e) -> l p h k e", h=H, k=KT)

        def mask_piece(l, i):
            raw_i = raw[:, i % 2, :]
            if i < QT:
                cols = bass.ds(PIECE * l, PIECE)
                return c.a["mask"][i * P:(i + 1) * P, cols], raw_i, c.neg_q[:, i, cols]
            n = PIECE // NT
            tiles_k = bass.ds(QT * n * l + n * (i - QT), n)
            return (c.a["maskT"].rearrange("(k p) q -> p k q", p=P)[:, tiles_k, :],
                    raw_i.rearrange("p (k q) -> p k q", q=NT), c.neg_k[:, tiles_k, :])

        @block.sync
        def _(sp):
            for j in range(NCHUNK):
                sp.dma_start(ctxT[:, :, j * CHUNK:(j + 1) * CHUNK], ctx_v[:, :, j * CHUNK:(j + 1) * CHUNK])\
                  .then_inc(S(f"ctx_loaded{j}"), 16)
            for n in range(4):
                sp.sem_inc(S(f"k_stored{n}"), 16)
            for n in range(2):
                sp.sem_inc(S(f"v_stored{n}"), 16)
            def load_mask(l, i):
                wait_apart(sp, S("mask_made"), PIECES * l + i + 1, 1)
                src, dst, _ = mask_piece(l, i)
                sp.dma_start(dst, src).then_inc(S(f"mask_loaded{i % 2}"), 16)

            with sp.Fori(0, LAYERS) as l:
                for n in range(NK):
                    if n in (NK // 2, NK // 2 + 1):
                        load_mask(l, n - NK // 2)
                    sp.wait_ge(S("k_split"), NK * l + n + 1 + PRIMED)
                    sp.dma_start(c.kparts[bass.ds(l, 1), :, (n // NCHUNK) * P:(n // NCHUNK + 1) * P,
                                          (n % NCHUNK) * CHUNK:(n % NCHUNK + 1) * CHUNK]
                                 .rearrange("o s p k -> p (o s) k"), kp[:, n % 4, :, :]).then_inc(S(f"k_stored{n % 4}"), 16)
                for n in range(NV):
                    wait_apart(sp, S("v_staged"), KT * l + VB * (n + 1) + PRIMED, PRIMED)
                    if n < PIECES - 2:
                        load_mask(l, n + 2)
                    sp.dma_start(vout[bass.ds(l, 1), :, :, n * VB:(n + 1) * VB, :].rearrange("o p h k e -> (o p) h k e"),
                                 vst[:, n % 2, :, :, :]).then_inc(S(f"v_stored{n % 2}"), 16)
                g_share = bass.ds(KT // LAYERS * l, KT // LAYERS)
                sp.dma_start(c.gT[:, g_share, :], c.a["gT"].rearrange("(k p) q -> p k q", p=P)[:, g_share, :])\
                  .then_inc(S("g_loaded"), 16)
            for n in range(4):
                sp.wait_ge(S(f"k_stored{n}"), 16 * (NK // 4) * LAYERS + 16)
            for n in range(2):
                sp.wait_ge(S(f"v_stored{n}"), 16 * (NV // 2) * LAYERS + 16)
            sp.wait_ge(S("g_loaded"), 16 * LAYERS)

        @block.tensor
        def _(pe):
            pe.sem_inc(S("k_psum"), PRIMED)
            with pe.Fori(0, LAYERS) as l:
                pe.wait_ge(S("wk_loaded"), 32 * l + 32)
                for n in range(NK):
                    mt, j = n // NCHUNK, n % NCHUNK
                    if mt == 0:
                        pe.wait_ge(S(f"ctx_loaded{j}"), 16)
                    pe.wait_ge(S("k_rest"), NK * l + n + 1)
                    for ct in range(CT):
                        ins = pe.matmul(c.ps[:, n % 2, :], wk[:, ct, mt * P:(mt + 1) * P],
                                        ctxT[:, ct, j * CHUNK:(j + 1) * CHUNK], start=(ct == 0), stop=(ct == CT - 1))
                    ins.then_inc(S("k_psum"), 1)
                pe.wait_ge(S("wv_loaded"), 32 * l + 32)
                for k in range(KT):
                    if k >= 2:
                        pe.wait_ge(S("v_staged"), KT * l + k - 1 + PRIMED)
                    for ct in range(CT):
                        ins = pe.matmul(c.ps[:, 2 + k % 2, 0:D], ctxT[:, ct, k * P:(k + 1) * P], wv[:, ct, :],
                                        start=(ct == 0), stop=(ct == CT - 1))
                    ins.then_inc(S("v_psum"), 1)

        @block.scalar
        def _(act):
            def second(l, n):
                act.wait_ge(S("k_rest"), NK * l + n + 3)
                act.activation(kp[:, n % 4, 1, :], rest[:, n % 2, :], ACT.Copy).then_inc(S("k_second"), 1)

            with act.Fori(0, LAYERS) as l:
                act.wait_ge(S("k_psum"), NK * l + PRIMED)
                act.wait_ge(S("k_rest"), NK * l + 2)
                act.dma_start(wk[:, :, :], c.a["wk4"][bass.ds(l, 1), :, :].rearrange("o (t p) n -> p (o t) n", p=P))\
                   .then_inc(S("wk_loaded"), 16)
                act.dma_start(bk[:, :], c.a["bk4"][bass.ds(l, 1), :, :].rearrange("o p t -> (o p) t"))\
                   .then_inc(S("wk_loaded"), 16)
                act.wait_ge(S("v_staged"), KT * l + PRIMED)
                act.dma_start(wv[:, :, :], c.a["wv4"][bass.ds(l, 1), :, :].rearrange("o (t p) n -> p (o t) n", p=P))\
                   .then_inc(S("wv_loaded"), 16)
                act.dma_start(bv[:, :], c.a["bv4"][bass.ds(l, 1), :].to_broadcast((P, D))).then_inc(S("wv_loaded"), 16)
                act.wait_ge(S("wk_loaded"), 32 * l + 32)
                for n in range(NK):
                    act.wait_ge(S("k_psum"), NK * l + n + 1 + PRIMED)
                    act.wait_ge(S(f"k_stored{n % 4}"), 16 * (NK // 4) * l + 16 * (n // 4) + 16)
                    act.activation(kp[:, n % 4, 0, :], c.ps[:, n % 2, :], ACT.Identity,
                                   bias=bk[:, n // NCHUNK:n // NCHUNK + 1]).then_inc(S("k_first"), 1)
                    if n > 0:
                        second(l, n - 1)
                second(l, NK - 1)

        @block.vector
        def _(dve):
            dve.sem_inc(S("k_rest"), 2)
            dve.sem_inc(S("v_staged"), PRIMED)
            dve.sem_inc(S("mask_made"), 2)
            with dve.Fori(0, LAYERS) as l:
                dve.wait_ge(S("wk_loaded"), 32 * l + 32)
                for n in range(NK):
                    dve.wait_ge(S("k_first"), NK * l + n + 1)
                    dve.wait_ge(S("k_split"), NK * l + max(n - 1, 0) + PRIMED)
                    dve.scalar_tensor_tensor(out=rest[:, n % 2, :], in0=c.ps[:, n % 2, :],
                                             scalar=bk[:, n // NCHUNK:n // NCHUNK + 1], in1=kp[:, n % 4, 0, :],
                                             op0=ALU.add, op1=ALU.subtract).then_inc(S("k_rest"), 1)
                dve.wait_ge(S("wv_loaded"), 32 * l + 32)
                for k in range(KT):
                    dve.wait_ge(S("v_psum"), KT * l + k + 1)
                    if k % VB == 0:
                        dve.wait_ge(S(f"v_stored{(k // VB) % 2}"), 16 * (NV // 2) * l + 16 * (k // VB // 2) + 16)
                    dve.tensor_tensor(vst[:, (k // VB) % 2, :, k % VB, :],
                                      c.ps[:, 2 + k % 2, 0:D].rearrange("p (h e) -> p h e", h=H),
                                      bv[:, :].rearrange("p (h e) -> p h e", h=H), ALU.add).then_inc(S("v_staged"), 1)
                    if k % VB == VB - 1:
                        i = k // VB
                        dve.wait_ge(S(f"mask_loaded{i % 2}"), 16 * (PIECES // 2) * l + 16 * (i // 2 + 1))
                        _, src, dst = mask_piece(l, i)
                        dve.tensor_scalar(dst, src, -1.0, -NEG, ALU.add, ALU.mult).then_inc(S("mask_made"), 1)

        @block.gpsimd
        def _(pool):
            pool.sem_inc(S("k_split"), PRIMED)
            with pool.Fori(0, LAYERS) as l:
                for n in range(NK):
                    pool.wait_ge(S("k_second"), NK * l + n + 1)
                    pool.tensor_tensor(kp[:, n % 4, 2, :], rest[:, n % 2, :], kp[:, n % 4, 1, :], ALU.subtract)\
                        .then_inc(S("k_split"), 1)
            pool.wait_ge(S("k_split"), NK * LAYERS + PRIMED)
            pool.memset(c.ops.kop[96:P, :, :], 1.0).then_inc(S("kop_ones"), 1)


class Operands:

    def __init__(self, c, ctx):
        self.c = c
        self.kop = ctx.enter_context(c.nc.sbuf_tensor("kop", [P, UNROLL, KEYS], BF16))
        self.qop = ctx.enter_context(c.nc.sbuf_tensor("qop", [P, UNROLL, NT], BF16))
        self.vraw = ctx.enter_context(c.nc.sbuf_tensor("vraw", [P, UNROLL, KT * HD], F32))
        self.S = Sems(c.nc, ctx, "ops")

    def load(self, eng, l, h, u):
        at = 0
        for part, n in enumerate(PARTS_BESIDE):
            src = self.c.kparts[l, part, :, :].rearrange("(h x) k -> h x k", h=H)[bass.ds(h, 1), :, :]
            eng.dma_start(self.kop[at:at + n * HD, u, :], src.to_broadcast((n, HD, KEYS)))\
               .then_inc(self.S(f"k_loaded{u}"), 16)
            at += n * HD
        src = self.c.vals[l, :, :].rearrange("p (h n) -> p h n", h=H)[:, bass.ds(h, 1), :]
        eng.dma_start(self.vraw[:, u, :], src.rearrange("p o n -> p (o n)")).then_inc(self.S(f"v_loaded{u}"), 16)

    def load_first(self, eng, l):
        for u in range(UNROLL):
            self.load(eng, l, u, u)

    def load_q(self, eng, sem, heads, buffers):
        at = 0
        for n in PARTS_BESIDE:
            eng.dma_start(self.qop[at:at + n * HD, buffers, :], self.c.qparts[0:n * HD, heads, :]).then_inc(sem, 16)
            at += n * HD


def queries(c, l):
    nc = c.nc
    with ExitStack() as ctx:
        S = Sems(nc, ctx, f"q{l}")
        sb = lambda name, shape, dt: ctx.enter_context(nc.sbuf_tensor(f"{name}_q{l}", shape, dt))
        qf = sb("qf", [P, CT * NT], F32)
        rest = sb("qrest", [P, 2, CT * NT], F32)
        qp = sb("qp", [P, 3, CT * NT], BF16)
        raw8 = sb("raw8", [1, KEYS], U8) if l == KEYED else None
        neg_row = sb("neg_row", [1, KEYS], BF16) if l == KEYED else None
        block = ctx.enter_context(nc.Block())

        @block.vector
        def _(dve):
            norm_dve(c, dve, S, c.x, c.xn)
            link = Chain(dve, S("q_step"))
            dve.wait_ge(S("q_scaled"), 1)
            link(dve.tensor_copy(qp[:, 0, :], qf[:, :]))
            link(dve.tensor_tensor(rest[:, 0, :], qf[:, :], qp[:, 0, :], ALU.subtract))
            link(dve.tensor_copy(qp[:, 1, :], rest[:, 0, :]))
            dve.tensor_tensor(qp[:, 2, :], rest[:, 0, :], qp[:, 1, :], ALU.subtract).then_inc(S("q_split"), 1)

        @block.gpsimd
        def _(pool):
            pool.memset(c.ops.qop[96:P, :, :], 1.0 if l == KEYED else 0.0).then_inc(S("qop_set"), 1)
            pool.wait_ge(S("qop_set"), 1)
            norm_pool(c, pool, S)
            if l == KEYED:
                pool.wait_ge(S("keymask_loaded"), 16)
                pool.wait_ge(S("norm_rstd"), 1)
                pool.tensor_scalar(neg_row[:, :], raw8[:, :], -1.0, -NEG, ALU.add, ALU.mult).then_inc(S("neg_made"), 1)

        @block.tensor
        def _(pe):
            keep_warm(c, pe, NORM_FILL)
            pe.wait_ge(S("norm_done"), QT)
            turn_pe(c, pe, S, c.xn, 0, "x_turned")
            pe.wait_ge(S("xT_ready"), 1)
            for mt in range(CT):
                out = c.ps[:, 1, mt * NT:(mt + 1) * NT]
                pe.matmul(out, c.row(f"bq{l}")[0:1, mt * P:(mt + 1) * P], c.ones[0:1, 0:NT], start=True, stop=False)
                for ct in range(CT):
                    ins = pe.matmul(out, c.wq[:, ct, mt * P:(mt + 1) * P], c.xT[:, ct, :],
                                    start=False, stop=(ct == CT - 1))
            ins.then_inc(S("q_psum"), 1)

        @block.scalar
        def _(act):
            act.wait_ge(S("x_turned"), 1)
            act.activation(c.xT[:, :, :], c.ps[:, 0, :].rearrange("p (t n) -> p t n", t=CT), ACT.Copy)\
               .then_inc(S("xT_ready"), 1)
            act.wait_ge(S("q_psum"), 1)
            act.mul(qf[:, :], c.ps[:, 1, :], Q_SCALE).then_inc(S("q_scaled"), 1)

        @block.sync
        def _(sp):
            if l == KEYED:
                sp.dma_start(raw8[:, :], c.a["mask_keys"]).then_inc(S("keymask_loaded"), 16)
            if l == 0:
                c.ops.load_first(sp, 0)
            sp.wait_ge(S("q_split"), 1)
            for part in range(3):
                sp.dma_start(c.qparts.rearrange("(s t e) h q -> s (e h) t q", s=3, t=CT)[part, :, :, :],
                             qp[:, part, :].rearrange("p (t q) -> p t q", t=CT)).then_inc(S("q_stored"), 16)
            sp.wait_ge(S("q_stored"), 48)
            sp.wait_ge(S("qop_set"), 1)
            c.ops.load_q(sp, c.ops.S("q_first"), slice(0, UNROLL), slice(0, UNROLL))
            if l == KEYED:
                sp.wait_ge(S("neg_made"), 1)
                sp.dma_start(c.ops.kop[R_MASK:R_MASK + 1, :, :],
                             neg_row[0:1, :].unsqueeze(1).to_broadcast((1, UNROLL, KEYS))).then_inc(S("mask_placed"), 16)
                sp.wait_ge(S("mask_placed"), 16)


def attend(c, l, by_query, weighted):
    nc = c.nc
    TURNS = H // UNROLL
    SC = QT * NCHUNK
    ops, kop, qop, vraw = c.ops, c.ops.kop, c.ops.qop, c.ops.vraw
    SHARED = 6
    FIRST = 2 * SC
    with ExitStack() as ctx:
        S = Sems(nc, ctx, f"att{l}")
        sb = lambda name, shape, dt: ctx.enter_context(nc.sbuf_tensor(f"{name}_a{l}", shape, dt))
        vop = sb("vop", [P, 2, KT, 32], F32)
        prob = sb("prob", [P, NP, GROUP * NT], F32)
        used = sb("used", [P, NP, GROUP * NT], F32) if weighted else prob
        best = sb("best", [P, 2, SC], F32)
        nmax = sb("nmax", [P, 2, QT], F32)
        mrow = sb("mrow", [1, 2, NT], F32)
        mrest = sb("mrest", [1, 2, NT], F32)
        mpart = sb("mpart", [1, 2, 3, NT], BF16)
        acc = sb("acc", [P, 2, NT], F32)
        rden = sb("rden", [P, QT], F32)
        dump = sb("dump", [P, 4, CHUNK], BF16) if by_query else None
        block = ctx.enter_context(nc.Block())

        s_bank = [c.ps[:, 0, :], c.ps[:, 1, :]]
        st_bank = [c.ps[:, 2:4, :].rearrange("p b n -> p (b n)"), c.ps[:, 4:6, :].rearrange("p b n -> p (b n)")]
        acc_bank = c.ps[:, 6, :]
        fold_out = c.ps[:, 7, 0:QT * 32]
        mrow_out = c.ps[0:1, 7, 256:256 + NT]

        first_bank = lambda n: c.ps[:, 2 * (n % 3):2 * (n % 3) + 2, :].rearrange("p b n -> p (b n)")
        r_first = R_MASK + 1 if l == KEYED else R_MASK

        @block.sync
        def _(sp):
            def maximum(h, u):
                sp.wait_ge(S("max_split"), h + 1 + PRIMED)
                sp.dma_start(qop[R_MAX:R_MAX + 3, u, :], mpart[0:1, u % 2, :, :]).then_inc(S(f"max_placed{u}"), 16)

            maximum(0, 0)
            maximum(1, 1)
            with sp.Fori(0, TURNS - 1) as t:
                for u in range(UNROLL):
                    wait_apart(sp, S("st_psum"), NGROUP * UNROLL * t + NGROUP * (u + 1), 1)
                    ops.load_q(sp, S(f"q_loaded{u}"), bass.ds(UNROLL * t + u + UNROLL, 1), slice(u, u + 1))
                    ops.load(sp, l, UNROLL * t + u + UNROLL, u)
                    maximum(UNROLL * t + u + 2, (u + 2) % UNROLL)
            maximum(H - 2, (H - 2) % UNROLL)
            maximum(H - 1, (H - 1) % UNROLL)
            sp.dma_start(c.wo[:, :, :], c.a["wo4"][l, :, :].rearrange("(t p) n -> p t n", p=P)).then_inc(S("weights"), 16)
            if l + 1 < LAYERS:
                sp.dma_start(c.wq[:, :, :], c.a["wq4"][l + 1, :, :].rearrange("(t p) n -> p t n", p=P))\
                  .then_inc(S("weights"), 16)
            sp.wait_ge(S("weights"), 32 if l + 1 < LAYERS else 16)
            for u in range(UNROLL):
                sp.wait_ge(S(f"max_placed{u}"), 16 * TURNS + 16 * (u == 3))

        @block.tensor
        def _(pe):
            def loaded(u, t):
                pe.wait_ge(ops.S(f"k_loaded{u}"), 48 * t + 48 * (TURNS * l + 1))
                if isinstance(t, int) and t == 0:
                    pe.wait_ge(ops.S("q_first"), 48 * (l + 1))
                else:
                    pe.wait_ge(S(f"q_loaded{u}"), 48 * t)

            def by_queries(n, u, chunk):
                pe.wait_ge(S("s_read"), n + 1)
                t, j = chunk // NCHUNK, chunk % NCHUNK
                pe.matmul(s_bank[chunk % 2], qop[0:r_first, u, t * P:(t + 1) * P],
                          kop[0:r_first, u, j * CHUNK:(j + 1) * CHUNK], start=True, stop=True).then_inc(S("s_psum"), 1)

            def by_keys(n, u, g):
                pe.wait_ge(S("exp_done"), n + 1)
                for j in range(GROUP):
                    k = g * GROUP + j
                    out = st_bank[g % 2][:, j * NT:(j + 1) * NT]
                    ins = pe.matmul(out, kop[0:R_ALL, u, k * P:(k + 1) * P], qop[0:R_ALL, u, :],
                                    start=(j % 2 == 0), stop=(not by_query and j % 2 == 1))
                    if by_query and j % 2 == 1:
                        ins = pe.matmul(st_bank[g % 2][:, (j - 1) * NT:(j + 1) * NT], c.identb[:, :],
                                        c.neg_k[:, k - 1:k + 1, :], start=False, stop=True)
                ins.then_inc(S("st_psum"), 1)

            def values(h, h2, g):
                n = NGROUP * h + g
                pe.wait_ge(S("exp_done"), n + 3)
                if g == 0:
                    pe.wait_ge(S("acc_read"), h + PRIMED)
                if weighted:
                    for j in range(GROUP):
                        pe.matmul(acc_bank[32 * j:32 * j + 32, h2 * NT:(h2 + 1) * NT], c.den16[:, :],
                                  prob[:, g % NP, j * NT:(j + 1) * NT], start=(g == 0), stop=False,
                                  skip_group_check=True)
                    if g == SHARED:
                        pe.wait_ge(S("weighted_pool"), h + 1)
                    else:
                        pe.wait_ge(S("weighted"), (NGROUP - 1) * h + g + (g < SHARED))
                for j in range(GROUP):
                    ins = pe.matmul(acc_bank[32 * j:32 * j + 32, h2 * NT:(h2 + 1) * NT],
                                    vop[:, h2, g * GROUP + j, :], used[:, g % NP, j * NT:(j + 1) * NT],
                                    start=(g == 0 and not weighted), stop=(g == NGROUP - 1), skip_group_check=True)
                ins.then_inc(S("pv_psum"), 1)

            def turn_max(h, h2, folded):
                if not isinstance(folded, int) or folded > 0:
                    pe.wait_ge(S("head_done"), folded)
                pe.wait_ge(S("max_found"), h + 1)
                pe.wait_ge(S("max_row"), h)
                for t in range(QT):
                    ins = pe.matmul(mrow_out[:, t * P:(t + 1) * P], nmax[:, h2, t:t + 1], c.ident[:, :],
                                    start=True, stop=True)
                ins.then_inc(S("max_turned"), 1)

            def fold(h, h2, rows):
                pe.wait_ge(S("max_row"), rows)
                pe.wait_ge(S("acc_read"), h + 1 + PRIMED)
                if not isinstance(h, int) or h > 0:
                    pe.wait_ge(S("head_done"), h)
                for t in range(QT):
                    ins = pe.matmul(fold_out[:, t * 32:(t + 1) * 32], acc[:, h2, t * P:(t + 1) * P], c.fold[:, :],
                                    start=True, stop=True)
                ins.then_inc(S("folded"), 1)

            def turn(t, first=False, last=False):
                for u in range(UNROLL):
                    h = UNROLL * t + u
                    h2, u2 = u % 2, (u + 2) % UNROLL
                    pe.wait_ge(S(f"max_placed{u}"), 16 * t + 16 + 16 * (u == 3))
                    ahead = not (last and u >= 2)
                    if ahead:
                        loaded(u2, t + (u + 2) // UNROLL)
                    pe.wait_ge(S("v_filled"), h + 1)
                    for g in range(NGROUP):
                        by_keys(NGROUP * h + g, u, g)
                        if g < LAG and not (first and u == 0):
                            values(h - 1, 1 - h2, NGROUP - LAG + g)
                        if g > LAG:
                            values(h, h2, g - LAG)
                        if ahead:
                            for i in range(2):
                                by_queries(SC * (h + 2) + 2 * g + i, u2, 2 * g + i)
                        if g == LAG:
                            values(h, h2, 0)
                        if g == 1 and not (last and u == 3):
                            turn_max(h + 1, 1 - h2, h - 1)
                        if g == 4 and not (first and u == 0):
                            fold(h - 1, 1 - h2, H if last and u == 3 else h + 2)

            pe.wait_ge(S("values_cleared"), 1)
            for n in range(FIRST // 2):
                h, pair = n // (SC // 2), n % (SC // 2)
                if pair == 0:
                    loaded(h, 0)
                if n >= 3:
                    pe.wait_ge(S("first_read"), n - 2)
                for i in range(2):
                    t, j = 2 * pair // NCHUNK, 2 * pair % NCHUNK + i
                    ins = pe.matmul(first_bank(n)[:, i * CHUNK:(i + 1) * CHUNK], qop[0:r_first, h, t * P:(t + 1) * P],
                                    kop[0:r_first, h, j * CHUNK:(j + 1) * CHUNK], start=True, stop=True)
                ins.then_inc(S("first_psum"), 1)
                if h == 1 and pair == 2:
                    turn_max(0, 0, 0)
            pe.wait_ge(S("first_read"), FIRST // 2)
            pe.sem_inc(S("s_psum"), FIRST)
            turn(0, first=True)
            with pe.Fori(1, TURNS - 1) as t:
                turn(t)
            turn(TURNS - 1, last=True)
            for g in range(NGROUP - LAG, NGROUP):
                values(H - 1, 1, g)
            fold(H - 1, 1, H)
            keep_warm(c, pe, FOLD_FILL, 0)

        @block.scalar
        def _(act):
            def row(h, h2):
                act.wait_ge(S("max_turned"), h + 1)
                act.wait_ge(S("max_split"), h - 1 + PRIMED)
                act.activation(mrow[:, h2, :], mrow_out, ACT.Copy).then_inc(S("max_row"), 1)

            def sums(h, h2):
                act.wait_ge(S("pv_psum"), NGROUP * h + NGROUP + NP)
                act.activation(acc[:, h2, :], acc_bank[:, h2 * NT:(h2 + 1) * NT], ACT.Copy).then_inc(S("acc_read"), 1)

            def turn(t, first=False, last=False):
                for u in range(UNROLL):
                    h = UNROLL * t + u
                    h2 = u % 2
                    for g in range(NGROUP):
                        n = NGROUP * h + g
                        act.wait_ge(S("st_psum"), n + 1)
                        act.wait_ge(S("pv_psum"), n + 1)
                        act.activation(prob[:, g % NP, :], st_bank[g % 2], ACT.Exp).then_inc(S("exp_done"), 1)
                        if g == LAG - 1 and not (first and u == 0):
                            sums(h - 1, 1 - h2)
                        if g == 2 and not (last and u == 3):
                            row(h + 1, 1 - h2)

            act.sem_inc(S("exp_done"), 2)
            act.sem_inc(S("acc_read"), PRIMED)
            act.wait_ge(S("max_turned"), 1)
            act.activation(mrow[:, 0, :], mrow_out, ACT.Copy).then_inc(S("max_row"), 1)
            turn(0, first=True)
            with act.Fori(1, TURNS - 1) as t:
                turn(t)
            turn(TURNS - 1, last=True)
            sums(H - 1, 1)

        @block.vector
        def _(dve):
            def chunk_max(n, h2, chunk):
                t, j = chunk // NCHUNK, chunk % NCHUNK
                if not by_query:
                    dve.wait_ge(S("s_psum"), n + 1)
                if by_query:
                    wait_apart(dve, S("s_psum"), n + 1, 1)
                    dve.wait_ge(S("s_read"), n + 1)
                    dve.tensor_tensor_reduce(out=dump[:, chunk % 2, :], in0=s_bank[chunk % 2],
                                             in1=c.neg_q[:, t, j * CHUNK:(j + 1) * CHUNK], scale=1.0, scalar=-3.0e38,
                                             op0=ALU.add, op1=ALU.max, accum_out=best[:, h2, chunk:chunk + 1])\
                       .then_inc(S("s_read"), 1)
                else:
                    dve.tensor_reduce(best[:, h2, chunk:chunk + 1], s_bank[chunk % 2], AX.X, ALU.max)\
                       .then_inc(S("s_read"), 1)

            def row_max(h, h2):
                dve.wait_ge(S("s_read"), SC * h + SC + 2)
                dve.wait_ge(S("max_turned"), h - 1)
                dve.tensor_reduce(nmax[:, h2, :], best[:, h2, :].rearrange("p (t j) -> p t j", t=QT), AX.X, ALU.max,
                                  negate=True).then_inc(S("max_found"), 1)

            def weigh(n, g):
                dve.wait_ge(S("exp_done"), n + 3)
                dve.wait_ge(S("pv_psum"), n + 1)
                dve.tensor_tensor(used[:, g % NP, :], prob[:, g % NP, :],
                                  c.gT[:, g * GROUP:(g + 1) * GROUP, :].rearrange("p k q -> p (k q)"), ALU.mult)\
                   .then_inc(S("weighted"), 1)

            def normalise(h):
                folded = fold_out.rearrange("p (t e) -> p t e", t=QT)
                dve.wait_ge(S("folded"), h + 1)
                dve.reciprocal(rden[:, :], folded[:, :, HD]).then_inc(S("den_inverted"), 1)
                dve.wait_ge(S("den_inverted"), h + 1)
                dve.tensor_tensor(c.att[:, :, bass.ds(HD * h, HD)], folded[:, :, 0:HD],
                                  rden[:, :].unsqueeze(2).to_broadcast((P, QT, HD)), ALU.mult)\
                   .then_inc(S("head_done"), 1)

            def turn(t, first=False, last=False):
                for u in range(UNROLL):
                    h = UNROLL * t + u
                    h2 = u % 2
                    for g in range(NGROUP):
                        if not (last and u >= 2):
                            for i in range(2):
                                chunk_max(SC * (h + 2) + 2 * g + i, h2, 2 * g + i)
                            if g == NGROUP - 1:
                                row_max(h + 2, h2)
                        if weighted and g != SHARED:
                            weigh(NGROUP * h + g, g)
                        if g == 5 and not (first and u == 0):
                            normalise(h - 1)

            for n in range(FIRST // 2):
                h, pair = n // (SC // 2), n % (SC // 2)
                t, j = 2 * pair // NCHUNK, 2 * pair % NCHUNK
                dve.wait_ge(S("first_psum"), n + 1)
                if by_query:
                    if n >= 2:
                        dve.wait_ge(S("first_read"), n - 1)
                    dve.tensor_tensor_reduce(out=dump[:, 2 * (n % 2):2 * (n % 2) + 2, :].rearrange("p b n -> p (b n)"),
                                             in0=first_bank(n), in1=c.neg_q[:, t, j * CHUNK:(j + 2) * CHUNK],
                                             scale=1.0, scalar=-3.0e38, op0=ALU.add, op1=ALU.max,
                                             accum_out=best[:, h, pair:pair + 1]).then_inc(S("first_read"), 1)
                else:
                    dve.tensor_reduce(best[:, h, pair:pair + 1], first_bank(n), AX.X, ALU.max)\
                       .then_inc(S("first_read"), 1)
                if pair == SC // 2 - 1:
                    dve.wait_ge(S("first_read"), n + 1)
                    dve.tensor_reduce(nmax[:, h, :], best[:, h, 0:SC // 2].rearrange("p (t j) -> p t j", t=QT), AX.X,
                                      ALU.max, negate=True).then_inc(S("max_found"), 1)
            dve.wait_ge(S("max_found"), 2)
            dve.sem_inc(S("s_read"), FIRST + 2)
            turn(0, first=True)
            with dve.Fori(1, TURNS - 1) as t:
                turn(t)
            turn(TURNS - 1, last=True)
            normalise(H - 1)

        @block.gpsimd
        def _(pool):
            def split(h, h2):
                wait_apart(pool, S("max_row"), h + 1, 1)
                pool.tensor_copy(mpart[:, h2, 0, :], mrow[:, h2, :]).then_inc(S("max_step"), 1)
                pool.wait_ge(S("max_step"), 3 * h + 1)
                pool.tensor_tensor(mrest[:, h2, :], mrow[:, h2, :], mpart[:, h2, 0, :], ALU.subtract)\
                    .then_inc(S("max_step"), 1)
                wait_apart(pool, S("max_step"), 3 * h + 2, 1)
                pool.tensor_copy(mpart[:, h2, 1, :], mrest[:, h2, :]).then_inc(S("max_step"), 1)
                pool.wait_ge(S("max_step"), 3 * h + 3)
                pool.tensor_tensor(mpart[:, h2, 2, :], mrest[:, h2, :], mpart[:, h2, 1, :], ALU.subtract)\
                    .then_inc(S("max_split"), 1)

            def fill(h, h2, u, t):
                wait_apart(pool, ops.S(f"v_loaded{u}"), 16 * t + 16 * (TURNS * l + 1), 16)
                pool.tensor_copy(vop[:, h2, :, 0:HD], vraw[:, u, :].rearrange("p (k e) -> p k e", e=HD))\
                    .then_inc(S("v_filled"), 1)

            pool.memset(vop[:, :, :, HD:32], 0.0).then_inc(S("vop_zero"), 1)
            pool.wait_ge(S("vop_zero"), 1)
            pool.memset(vop[:, :, :, HD:HD + 1], 0.0 if weighted else 1.0).then_inc(S("values_cleared"), 1)
            pool.wait_ge(S("values_cleared"), 1)
            pool.sem_inc(S("pv_psum"), NP)
            pool.sem_inc(S("max_split"), PRIMED)
            pool.sem_inc(S("max_placed3"), 16)
            fill(0, 0, 0, 0)
            fill(1, 1, 1, 0)
            split(0, 0)

            def turn(t, first=False, last=False):
                for u in range(UNROLL):
                    h = UNROLL * t + u
                    if not (last and u == 3):
                        if u == 0:
                            pool.wait_ge(S("max_placed3"), 16 * t + 16)
                        else:
                            pool.wait_ge(S(f"max_placed{u - 1}"), 16 * t + 16)
                        split(h + 1, 1 - u % 2)
                    if weighted:
                        n = NGROUP * h + SHARED
                        wait_apart(pool, S("exp_done"), n + 3, 2)
                        pool.wait_ge(S("pv_psum"), n + 1)
                        pool.tensor_tensor(used[:, SHARED % NP, :], prob[:, SHARED % NP, :],
                                           c.gT[:, SHARED * GROUP:(SHARED + 1) * GROUP, :].rearrange("p k q -> p (k q)"),
                                           ALU.mult).then_inc(S("weighted_pool"), 1)
                        pool.wait_ge(S("weighted_pool"), h + 1)
                    if not (last and u >= 2):
                        wait_apart(pool, S("pv_psum"), NGROUP * h + NGROUP + NP, NP)
                        fill(h + 2, u % 2, (u + 2) % UNROLL, t + (u + 2) // UNROLL)

            turn(0, first=True)
            with pool.Fori(1, TURNS - 1) as t:
                turn(t)
            turn(TURNS - 1, last=True)


def project_out(c, l):
    nc = c.nc
    with ExitStack() as ctx:
        S = Sems(nc, ctx, f"o{l}")
        block = ctx.enter_context(nc.Block())

        @block.tensor
        def _(pe):
            turn_pe(c, pe, S, c.att, 0, "att_turned")
            pe.wait_ge(S("attT_ready"), 1)
            by_tokens_pe(c, pe, [c.ps[:, 1, t * D:(t + 1) * D] for t in range(QT)], c.xT, c.wo[:, :, :],
                         c.row(f"bo{l}")).then_inc(S("out_psum"), 1)

        @block.scalar
        def _(act):
            act.wait_ge(S("att_turned"), 1)
            act.activation(c.xT[:, :, :], c.ps[:, 0, :].rearrange("p (t n) -> p t n", t=CT), ACT.Copy)\
               .then_inc(S("attT_ready"), 1)

        @block.vector
        def _(dve):
            dve.wait_ge(S("out_psum"), 1)
            add_stream_dve(c, dve, S, 1)


def turn_act(c, act, S, bank=0, n=0):
    act.wait_ge(S("turned"), n + 1)
    act.activation(c.xT[:, :, :], c.ps[:, bank, :].rearrange("p (t n) -> p t n", t=CT), ACT.Copy)\
       .then_inc(S("xT_ready"), 1)


def halves(c, bank):
    return [c.ps[:, bank, t * D:(t + 1) * D] for t in range(QT)]


def by_channels_pe(c, pe, out, w, srcT, bias=None, n_ct=CT):
    if bias is not None:
        pe.matmul(out, bias, c.ones[0:1, 0:NT], start=True, stop=False)
    for ct in range(n_ct):
        ins = pe.matmul(out, w(ct), srcT[:, ct, :], start=(ct == 0 and bias is None), stop=(ct == n_ct - 1))
    return ins


def tiles(a):
    return a.rearrange("(t p) n -> p t n", p=P)


def taylor(c):
    nc = c.nc
    G = H // 4
    with ExitStack() as ctx:
        S = Sems(nc, ctx, "taylor")
        sb = lambda name, shape, dt: ctx.enter_context(nc.sbuf_tensor(f"t_{name}", shape, dt))
        wq = sb("wq", [P, CT, 4 * P], F32)
        wk = sb("wk", [P, CT, 4 * P], F32)
        wv = sb("wv", [P, CT, D], F32)
        wo = sb("wo", [P, CT, D], F32)
        qT = sb("qT", [P, G, NT], F32)
        kT = sb("kT", [P, G, NT], F32)
        vop = sb("vop", [P, QT, H, 32], F32)
        square = sb("square", [P, 4, 3 * P], F32)
        weight = sb("weight", [P, 8, 3 * P], F32)
        acc = sb("acc", [P, 2, NT], F32)
        den = sb("den", [P, QT, 4], F32)
        block = ctx.enter_context(nc.Block())

        @block.sync
        def _(sp):
            for tile, name in ((wq, "t_wq"), (wk, "t_wk"), (wv, "t_wv"), (wo, "t_wo")):
                sp.dma_start(tile[:, :, :], tiles(c.a[name])).then_inc(S("weights"), 16)
            c.ops.load_first(sp, 1)

        @block.gpsimd
        def _(pool):
            norm_pool(c, pool, S)
            pool.memset(vop[:, :, :, HD:32], 0.0).then_inc(S("vop_zero"), 1)
            pool.wait_ge(S("vop_zero"), 1)
            pool.memset(vop[:, :, :, HD:HD + 1], 1.0).then_inc(S("vop_ones"), 1)

        @block.tensor
        def _(pe):
            keep_warm(c, pe, NORM_FILL)
            pe.wait_ge(S("norm_done"), QT)
            turn_pe(c, pe, S, c.xn, 0, "turned")
            pe.wait_ge(S("xT_ready"), 1)
            pe.wait_ge(S("weights"), 64)
            for w, bank, name in ((wq, 1, "q_psum"), (wk, 3, "k_psum")):
                for m in range(G):
                    ins = by_channels_pe(c, pe, c.ps[:, bank + m // 2, (m % 2) * NT:(m % 2 + 1) * NT],
                                         lambda ct: w[:, ct, m * P:(m + 1) * P], c.xT)
                ins.then_inc(S(name), 1)
            by_tokens_pe(c, pe, halves(c, 5), c.xT, wv, None).then_inc(S("v_psum"), 1)
            pe.wait_ge(S("q_ready"), 1)
            pe.wait_ge(S("k_ready"), 1)

            def scores(g):
                for j in range(4):
                    n = 4 * g + j
                    if n >= 4:
                        pe.wait_ge(S("squared"), n - 3)
                    rows = slice(32 * j, 32 * j + HD)
                    pe.matmul(c.ps[:, 1 + j, 0:NT], kT[rows, g, 0:P], qT[rows, g, :], start=True, stop=True)
                    pe.matmul(c.ps[:, 1 + j, NT:NT + P], kT[rows, g, P:NT], qT[rows, g, P:NT],
                              start=True, stop=True).then_inc(S("s_psum"), 1)

            def values(g):
                if g >= 2:
                    pe.wait_ge(S("acc_read"), g - 1)
                for j in range(4):
                    n = 4 * g + j
                    pe.wait_ge(S("weighted"), n + 1)
                    out = c.ps[32 * j:32 * j + 32, 6 + g % 2, :]
                    pe.matmul(out[:, 0:NT], vop[:, 0, n, :], weight[:, n % 8, 0:NT], start=True, stop=False)
                    ins = pe.matmul(out[:, P:NT], vop[:, 1, n, :], weight[:, n % 8, NT:NT + P], start=False, stop=True)
                ins.then_inc(S("pv_psum"), 1)

            def turn_back(g):
                pe.wait_ge(S("acc_read"), g + 1)
                if g >= 1:
                    pe.wait_ge(S("normalised"), g)
                for t in range(QT):
                    ins = pe.transpose(c.ps[:, 5, t * P:(t + 1) * P], acc[:, g % 2, t * P:(t + 1) * P], c.ident[:, :])
                ins.then_inc(S("turned_back"), 1)

            scores(0)
            pe.wait_ge(S("v_ready"), 1)
            pe.wait_ge(S("vop_ones"), 1)
            for g in range(G):
                if g + 1 < G:
                    scores(g + 1)
                values(g)
                if g >= 1:
                    turn_back(g - 1)
            turn_back(G - 1)
            pe.wait_ge(S("normalised"), G)
            turn_pe(c, pe, S, c.att, 0, "turned")
            pe.wait_ge(S("xT_ready"), 2)
            by_tokens_pe(c, pe, halves(c, 1), c.xT, wo, None).then_inc(S("out_psum"), 1)

        def sums(act, g):
            act.wait_ge(S("pv_psum"), g + 1)
            if g >= 2:
                act.wait_ge(S("turned_back"), g - 1)
            act.activation(acc[:, g % 2, :], c.ps[:, 6 + g % 2, 0:NT], ACT.Copy).then_inc(S("acc_read"), 1)

        @block.scalar
        def _(act):
            turn_act(c, act, S)
            act.wait_ge(S("q_psum"), 1)
            act.mul(qT[:, :, :], c.ps[:, 1:3, :].rearrange("p b (m n) -> p (b m) n", n=NT), 0.25).then_inc(S("q_ready"), 1)
            act.wait_ge(S("v_psum"), 1)
            act.activation(vop[:, :, :, 0:HD].rearrange("p t h e -> p (t h) e"),
                           c.ps[:, 5, :].rearrange("p (n e) -> p n e", e=HD), ACT.Copy).then_inc(S("v_ready"), 1)
            for g in range(G):
                for j in range(4):
                    n = 4 * g + j
                    act.wait_ge(S("s_psum"), n + 1)
                    if n >= 4:
                        act.wait_ge(S("weighted"), n - 3)
                    act.activation(square[:, j, :], c.ps[:, 1 + j, 0:3 * P], ACT.Square, bias=c.ones[:, 0:1])\
                       .then_inc(S("squared"), 1)
                if g >= 1:
                    sums(act, g - 1)
            sums(act, G - 1)
            turn_act(c, act, S, n=1)

        @block.vector
        def _(dve):
            norm_dve(c, dve, S, c.x, c.xn)
            dve.wait_ge(S("k_psum"), 1)
            dve.tensor_copy(kT[:, :, :], c.ps[:, 3:5, :].rearrange("p b (m n) -> p (b m) n", n=NT)).then_inc(S("k_ready"), 1)
            link = Chain(dve, S("den_step"))

            def normalise(g):
                dve.wait_ge(S("turned_back"), g + 1)
                folded = c.ps[:, 5, 0:QT * P].rearrange("p (t j e) -> p t j e", t=QT, j=4)
                link(dve.tensor_scalar(den[:, :, :], folded[:, :, :, HD], 1e-12, None, ALU.add))
                link(dve.reciprocal(den[:, :, :], den[:, :, :]))
                dve.tensor_tensor(c.att[:, :, 64 * g:64 * g + 64].rearrange("p t (j e) -> p t j e", j=4),
                                  folded[:, :, :, 0:HD], den[:, :, :].unsqueeze(3).to_broadcast((P, QT, 4, HD)),
                                  ALU.mult).then_inc(S("normalised"), 1)

            for g in range(G):
                for j in range(4):
                    n = 4 * g + j
                    dve.wait_ge(S("squared"), n + 1)
                    if n >= 8:
                        dve.wait_ge(S("pv_psum"), g - 1)
                    dve.scalar_tensor_tensor(out=weight[:, n % 8, :], in0=square[:, j, :], scalar=1.0,
                                             in1=c.tri[:, :], op0=ALU.add, op1=ALU.mult).then_inc(S("weighted"), 1)
                if g >= 2:
                    normalise(g - 2)
            normalise(G - 2)
            normalise(G - 1)
            dve.wait_ge(S("out_psum"), 1)
            add_stream_dve(c, dve, S, 1)


def first_expert(c):
    nc = c.nc
    with ExitStack() as ctx:
        S = Sems(nc, ctx, "first")
        sb = lambda name, shape, dt: ctx.enter_context(nc.sbuf_tensor(f"f_{name}", shape, dt))
        router = sb("router", [P, CT, E], F32)
        router_b = sb("router_b", [1, E], F32)
        bias = sb("bias", [1, E, D], F32)
        w = sb("w", [P, E, CT, D], F32)
        logits = sb("logits", [P, QT, E], F32)
        top = sb("top", [P, QT, 8], F32)
        where = sb("where", [P, QT, 8], U32)
        where_f = sb("where_f", [P, QT], F32)
        ntop = sb("ntop", [P, QT], F32)
        ex = sb("ex", [P, QT, E], F32)
        total = sb("total", [P, QT], F32)
        gate = sb("gate", [P, QT], F32)
        share = sb("share", [P, QT, E], F32)
        block = ctx.enter_context(nc.Block())

        @block.sync
        def _(sp):
            sp.dma_start(router[:, :, :], tiles(c.a["f_router"])).then_inc(S("router"), 16)
            sp.dma_start(router_b[:, :], c.a["f_router_b"]).then_inc(S("router"), 16)
            sp.dma_start(bias[:, :, :], c.a["f_bias"]).then_inc(S("router"), 16)
            for e in range(E):
                sp.dma_start(w[:, e, :, :], tiles(c.a["f_w"][e, :, :])).then_inc(S(f"expert{e}"), 16)

        @block.gpsimd
        def _(pool):
            norm_pool(c, pool, S)

        @block.tensor
        def _(pe):
            keep_warm(c, pe, NORM_FILL)
            pe.wait_ge(S("norm_done"), QT)
            turn_pe(c, pe, S, c.xn, 0, "turned")
            pe.wait_ge(S("xT_ready"), 1)
            pe.wait_ge(S("router"), 48)
            by_tokens_pe(c, pe, [c.ps[:, 1, t * E:(t + 1) * E] for t in range(QT)], c.xT, router,
                         router_b[:, :]).then_inc(S("logits"), 1)
            for e in range(E):
                pe.wait_ge(S(f"expert{e}"), 16)
                if e >= 4:
                    pe.wait_ge(S("added"), QT * (e - 3))
                by_tokens_pe(c, pe, halves(c, 2 + e % 4), c.xT, w[:, e, :, :], bias[0:1, e, :]).then_inc(S("e_psum"), 1)

        @block.scalar
        def _(act):
            turn_act(c, act, S)
            act.wait_ge(S("top_found"), 1)
            for t in range(QT):
                act.activation(ex[:, t, :], logits[:, t, :], ACT.Exp, bias=ntop[:, t:t + 1],
                               accum_out=total[:, t:t + 1]).then_inc(S("exp_done"), 1)

        @block.vector
        def _(dve):
            norm_dve(c, dve, S, c.x, c.xn)
            link = Chain(dve, S("step"))
            dve.wait_ge(S("logits"), 1)
            link(dve.tensor_copy(logits[:, :, :], c.ps[:, 1, 0:QT * E].rearrange("p (t e) -> p t e", t=QT)))
            for t in range(QT):
                link(dve.max(top[:, t, :], logits[:, t, :]))
                link(dve.max_index(where[:, t, :], top[:, t, :], logits[:, t, :]))
            dve.tensor_scalar(ntop[:, :], top[:, :, 0], -1.0, None, ALU.mult).then_inc(S("top_found"), 1)
            link(dve.tensor_copy(where_f[:, :], where[:, :, 0]))
            dve.wait_ge(S("exp_done"), QT)
            link(dve.reciprocal(gate[:, :], total[:, :]))
            for t in range(QT):
                link(dve.tensor_scalar(share[:, t, :], c.count8[:, :], where_f[:, t:t + 1], gate[:, t:t + 1],
                                       ALU.is_equal, ALU.mult))
            add_experts_dve(c, dve, S, share, [2 + e % 4 for e in range(E)])


def add_experts_dve(c, dve, S, share, banks):
    for e in range(E):
        dve.wait_ge(S("e_psum"), e + 1)
        if e >= 1:
            dve.wait_ge(S("added"), QT * e)
        for t in range(QT):
            dve.scalar_tensor_tensor(out=c.x[:, t, :], in0=halves(c, banks[e])[t], scalar=share[:, t, e:e + 1],
                                     in1=c.x[:, t, :], op0=ALU.mult, op1=ALU.add).then_inc(S("added"), 1)
    dve.wait_ge(S("added"), QT * E)


def frames(c, load_next):
    nc = c.nc
    HN, DH, FR = 16, 64, 64
    INNER = HN * DH
    M = INNER // P
    with ExitStack() as ctx:
        S = Sems(nc, ctx, "frames")
        sb = lambda name, shape, dt: ctx.enter_context(nc.sbuf_tensor(f"m_{name}", shape, dt))
        w = sb("w", [P, 3, CT, INNER], F32)
        wo = sb("wo", [P, M, D], F32)
        gb = sb("gb", [P, 2, D], F32)
        bo = sb("bo", [1, D], F32)
        qT = sb("qT", [P, M, NT], F32)
        kT = sb("kT", [P, M, NT], F32)
        v = sb("v", [P, QT, INNER], F32)
        mask = sb("mask", [P, 3 * P], F32)
        s = sb("s", [P, 2, 3 * P], F32)
        top = sb("top", [P, 2, QT], F32)
        ntop = sb("ntop", [P, 2, QT], F32)
        p = sb("p", [P, 2, 3 * P], F32)
        total = sb("total", [P, 2, QT], F32)
        rden = sb("rden", [P, 2, QT], F32)
        pn = sb("pn", [P, 2, 3 * P], F32)
        pT = sb("pT", [P, 2, 3 * P], F32)
        oT = sb("oT", [P, M, NT], F32)
        block = ctx.enter_context(nc.Block())
        cols = [slice(0, P), slice(P, 3 * P)]

        @block.sync
        def _(sp):
            sp.dma_start(gb[:, 0, :], c.a["m_g"].to_broadcast((P, D))).then_inc(S("scales"), 16)
            sp.dma_start(gb[:, 1, :], c.a["m_b"].to_broadcast((P, D))).then_inc(S("scales"), 16)
            for k in range(3):
                sp.dma_start(w[:, k, :, :], tiles(c.a["m_w"])[:, :, k * INNER:(k + 1) * INNER]).then_inc(S(f"w{k}"), 16)
            sp.dma_start(wo[:, :, :], tiles(c.a["m_wo"])).then_inc(S("wo"), 16)
            sp.dma_start(bo[:, :], c.a["m_bo"]).then_inc(S("wo"), 16)
            load_next(sp)
            c.ops.load_first(sp, 2)

        @block.gpsimd
        def _(pool):
            norm_pool(c, pool, S)
            pool.memset(mask[:, :], 0.0).then_inc(S("mask"), 1)
            pool.wait_ge(S("mask"), 1)
            pool.memset(mask[0:FR, FR:2 * FR], NEG).then_inc(S("mask"), 1)
            pool.memset(mask[0:FR, P + 3 * FR:P + 4 * FR], NEG).then_inc(S("mask"), 1)
            norm_pool(c, pool, S, 1)

        @block.tensor
        def _(pe):
            keep_warm(c, pe, 2 * NORM_FILL)
            pe.wait_ge(S("scaled"), 2 * QT)
            turn_pe(c, pe, S, c.att, 0, "turned")
            pe.wait_ge(S("xT_ready"), 1)
            n = 0
            for k in range(2):
                pe.wait_ge(S(f"w{k}"), 16)
                for m in range(0, M, 2):
                    if n >= 4:
                        pe.wait_ge(S("qk_read"), n - 3)
                    for i in range(2):
                        ins = by_channels_pe(c, pe, c.ps[:, 1 + n % 4, i * NT:(i + 1) * NT],
                                             lambda ct: w[:, k, ct, (m + i) * P:(m + i + 1) * P], c.xT)
                    ins.then_inc(S("qk_psum"), 1)
                    n += 1
            pe.wait_ge(S("w2"), 16)
            for i in range(4):
                t, j = i // 2, i % 2
                if i >= 2:
                    pe.wait_ge(S("v_read"), i - 1)
                for ct in range(CT):
                    ins = pe.matmul(c.ps[:, 5 + i % 2, :], c.xT[:, ct, t * P:(t + 1) * P],
                                    w[:, 2, ct, j * 512:(j + 1) * 512], start=(ct == 0), stop=(ct == CT - 1))
                ins.then_inc(S("v_psum"), 1)

            def scores(h):
                if h >= 2:
                    pe.wait_ge(S("s_read"), QT * (h - 1))
                r, m = slice(DH * (h % 2), DH * (h % 2) + DH), h // 2
                pe.matmul(c.ps[:, 1 + h % 2, cols[0]], qT[r, m, 0:P], kT[r, m, 0:P], start=True, stop=True)
                pe.matmul(c.ps[:, 1 + h % 2, cols[1]], qT[r, m, P:NT], kT[r, m, :], start=True, stop=True)\
                  .then_inc(S("s_psum"), 1)

            def turn_p(h):
                pe.wait_ge(S("p_scaled"), QT * (h + 1))
                if h >= 2:
                    pe.wait_ge(S("pT_ready"), h - 1)
                for i in range(3):
                    ins = pe.transpose(c.ps[:, 3 + h % 2, i * P:(i + 1) * P], pn[:, h % 2, i * P:(i + 1) * P],
                                       c.ident[:, :])
                ins.then_inc(S("p_turned"), 1)

            def values(h):
                pe.wait_ge(S("pT_ready"), h + 1)
                if h >= 4 and h % 2 == 0:
                    pe.wait_ge(S("o_read"), h // 2 - 1)
                if h == 0:
                    pe.wait_ge(S("v_read"), 4)
                out = c.ps[DH * (h % 2):DH * (h % 2) + DH, 5 + (h // 2) % 2, :]
                hs = slice(h * DH, (h + 1) * DH)
                pe.matmul(out[:, 0:NT], v[:, 0, hs], pT[:, h % 2, 0:NT], start=True, stop=False)
                pe.matmul(out[:, P:NT], v[:, 1, hs], pT[:, h % 2, NT:NT + P], start=False, stop=True)\
                  .then_inc(S("pv_psum"), 1)

            pe.wait_ge(S("qk_read"), M)
            for h in range(HN + 3):
                if h < HN:
                    scores(h)
                if 2 <= h < HN + 2:
                    turn_p(h - 2)
                if h >= 3:
                    values(h - 3)
            pe.wait_ge(S("wo"), 32)
            pe.wait_ge(S("o_read"), M)
            by_tokens_pe(c, pe, halves(c, 7), oT, wo, bo[:, :], M).then_inc(S("out_psum"), 1)

        def take_out(act, m):
            act.wait_ge(S("pv_psum"), 2 * m + 2)
            act.activation(oT[:, m, :], c.ps[:, 5 + m % 2, 0:NT], ACT.Copy).then_inc(S("o_read"), 1)

        @block.scalar
        def _(act):
            turn_act(c, act, S)
            for n in range(M):
                act.wait_ge(S("qk_psum"), n + 1)
                k, m = n // (M // 2), 2 * (n % (M // 2))
                act.activation((qT, kT)[k][:, m:m + 2, :], c.ps[:, 1 + n % 4, :].rearrange("p (m n) -> p m n", n=NT),
                               ACT.Copy, scale=(DH ** -0.5, 1.0)[k]).then_inc(S("qk_read"), 1)

            def weigh(h):
                act.wait_ge(S("top_negated"), h + 1)
                if h >= 2:
                    act.wait_ge(S("p_scaled"), QT * (h - 1))
                for t in range(QT):
                    act.activation(p[:, h % 2, cols[t]], s[:, h % 2, cols[t]], ACT.Exp, bias=ntop[:, h % 2, t:t + 1],
                                   accum_out=total[:, h % 2, t:t + 1]).then_inc(S("exp_done"), 1)

            def take_turned(h):
                act.wait_ge(S("p_turned"), h + 1)
                if h >= 2:
                    act.wait_ge(S("pv_psum"), h - 1)
                act.activation(pT[:, h % 2, :], c.ps[:, 3 + h % 2, 0:3 * P], ACT.Copy).then_inc(S("pT_ready"), 1)

            for h in range(HN + 2):
                if h < HN:
                    weigh(h)
                if h >= 2:
                    take_turned(h - 2)
                if h >= 5 and h % 2 == 1:
                    take_out(act, h // 2 - 2)
            take_out(act, M - 1)

        @block.vector
        def _(dve):
            norm_dve(c, dve, S, c.x, c.xn)
            dve.wait_ge(S("norm_done"), QT)
            norm_dve(c, dve, S, c.xn, c.att, 1)
            scale_norm_dve(c, dve, S, gb)
            for i in range(4):
                t, j = i // 2, i % 2
                dve.wait_ge(S("v_psum"), i + 1)
                dve.tensor_copy(v[:, t, j * 512:(j + 1) * 512], c.ps[:, 5 + i % 2, :]).then_inc(S("v_read"), 1)
            dve.wait_ge(S("mask"), 3)

            def tops(h):
                dve.wait_ge(S("s_psum"), h + 1)
                if h >= 2:
                    dve.wait_ge(S("exp_done"), QT * (h - 1))
                for t in range(QT):
                    dve.tensor_tensor_reduce(out=s[:, h % 2, cols[t]], in0=c.ps[:, 1 + h % 2, cols[t]],
                                             in1=mask[:, cols[t]], scale=1.0, scalar=-3.0e38, op0=ALU.add,
                                             op1=ALU.max, accum_out=top[:, h % 2, t:t + 1]).then_inc(S("s_read"), 1)
                dve.wait_ge(S("s_read"), QT * (h + 1))
                dve.tensor_scalar(ntop[:, h % 2, :], top[:, h % 2, :], -1.0, None, ALU.mult).then_inc(S("top_negated"), 1)

            def divide(h):
                dve.wait_ge(S("exp_done"), QT * (h + 1))
                dve.reciprocal(rden[:, h % 2, :], total[:, h % 2, :]).then_inc(S("inverted"), 1)
                dve.wait_ge(S("inverted"), h + 1)
                if h >= 2:
                    dve.wait_ge(S("p_turned"), h - 1)
                for t in range(QT):
                    dve.tensor_scalar(pn[:, h % 2, cols[t]], p[:, h % 2, cols[t]], rden[:, h % 2, t:t + 1], None,
                                      ALU.mult).then_inc(S("p_scaled"), 1)

            for h in range(HN + 1):
                if h < HN:
                    tops(h)
                if h >= 1:
                    divide(h - 1)
            dve.wait_ge(S("out_psum"), 1)
            add_stream_dve(c, dve, S, 7)


def scale_norm_dve(c, dve, S, gb):
    dve.wait_ge(S("norm_done"), 2 * QT)
    dve.wait_ge(S("scales"), 32)
    for t in range(QT):
        dve.tensor_tensor(c.att[:, t, :], c.att[:, t, :], gb[:, 0, :], ALU.mult).then_inc(S("scaled"), 1)
    dve.wait_ge(S("scaled"), QT)
    for t in range(QT):
        dve.tensor_tensor(c.att[:, t, :], c.att[:, t, :], gb[:, 1, :], ALU.add).then_inc(S("scaled"), 1)


def experts_pe(c, pe, S, w1, w3, w2, HT):
    HB = HT // 2

    def up(e):
        pe.wait_ge(S(f"up{e}"), 32)
        for b in range(HB):
            n = HB * e + b
            if n >= 2:
                pe.wait_ge(S("gated"), n - 1)
            for w, bank, name in ((w1, 1, "gate_psum"), (w3, 3, "up_psum")):
                for i in range(2):
                    m = 2 * b + i
                    ins = by_channels_pe(c, pe, c.ps[:, bank + n % 2, i * NT:(i + 1) * NT],
                                         lambda ct: w[:, e, ct, m * P:(m + 1) * P], c.xT)
                ins.then_inc(S(name), 1)

    def down(e):
        pe.wait_ge(S(f"down{e}"), 16)
        pe.wait_ge(S("gated"), HB * (e + 1))
        if e >= 2:
            pe.wait_ge(S("added"), QT * (e - 1))
        by_tokens_pe(c, pe, halves(c, 5 + e % 2), c.hT(e), w2[:, e, :, :], None, HT).then_inc(S("e_psum"), 1)

    for e in range(E + 1):
        if e < E:
            up(e)
        if e >= 1:
            down(e - 1)


def experts_act(c, act, S, HT, silu):
    HB = HT // 2
    for n in range(HB * E):
        act.wait_ge(S("gate_psum"), n + 1)
        if n >= 2:
            act.wait_ge(S("gated"), n - 1)
        act.activation(silu[:, n % 2, :], c.ps[:, 1 + n % 2, :], ACT.Silu).then_inc(S("silu_done"), 1)


def experts_dve(c, dve, S, HT, silu, share):
    HB = HT // 2

    def add(e):
        dve.wait_ge(S("e_psum"), e + 1)
        if e >= 1:
            dve.wait_ge(S("added"), QT * e)
        for t in range(QT):
            dve.scalar_tensor_tensor(out=c.x[:, t, :], in0=halves(c, 5 + e % 2)[t], scalar=share[:, t, e:e + 1],
                                     in1=c.x[:, t, :], op0=ALU.mult, op1=ALU.add).then_inc(S("added"), 1)

    for e in range(E):
        for b in range(HB):
            n = HB * e + b
            dve.wait_ge(S("silu_done"), n + 1)
            dve.wait_ge(S("up_psum"), n + 1)
            if b == 0 and e >= 2:
                dve.wait_ge(S("e_psum"), e - 1)
            dve.tensor_tensor(c.hT(e)[:, 2 * b:2 * b + 2, :], c.ps[:, 3 + n % 2, :].rearrange("p (m n) -> p m n", n=NT),
                              silu[:, n % 2, :].rearrange("p (m n) -> p m n", n=NT), ALU.mult).then_inc(S("gated"), 1)
        if e >= 1:
            add(e - 1)
    add(E - 1)
    dve.wait_ge(S("added"), QT * E)


def load_experts(c, sp, S, prefix, w1, w3, w2):
    for e in range(E):
        sp.dma_start(w1[:, e, :, :], tiles(c.a[f"{prefix}_w1"][e, :, :])).then_inc(S(f"up{e}"), 16)
        sp.dma_start(w3[:, e, :, :], tiles(c.a[f"{prefix}_w3"][e, :, :])).then_inc(S(f"up{e}"), 16)
        sp.dma_start(w2[:, e, :, :], tiles(c.a[f"{prefix}_w2"][e, :, :])).then_inc(S(f"down{e}"), 16)


class ChosenExperts:
    HIDDEN = 512

    def __init__(self, c, ctx):
        self.c = c
        self.S = Sems(c.nc, ctx, "choose")
        sb = lambda name, shape, dt: ctx.enter_context(c.nc.sbuf_tensor(f"e_{name}", shape, dt))
        self.router = sb("router", [P, CT, E], F32)
        self.w1 = sb("w1", [P, E, CT, self.HIDDEN], F32)

    def load_group(self, sp, n, w, g, name):
        src = self.c.a[f"e_w{n}"].rearrange("e (t p) n -> p (e t) n", p=P)
        half = src.shape[1] // 2
        sp.dma_start(w[:, E // 2 * g:E // 2 * (g + 1), :, :].rearrange("p e t n -> p (e t) n"),
                     src[:, g * half:(g + 1) * half, :]).then_inc(self.S(f"{name}{g}"), 16)

    def load_first(self, sp):
        sp.dma_start(self.router[:, :, :], tiles(self.c.a["e_router"])).then_inc(self.S("router"), 16)
        for g in range(2):
            self.load_group(sp, 1, self.w1, g, "up")


def experts_choose(c, weights):
    nc = c.nc
    w1, S = weights.w1, weights.S
    HIDDEN = weights.HIDDEN
    HT = HIDDEN // P
    PLACES = NT // E
    ROUNDS = PLACES // 8
    EG = 4
    G = E // EG
    TAKEN = -3.0e38
    with ExitStack() as ctx:
        sb = lambda name, shape, dt: ctx.enter_context(nc.sbuf_tensor(f"e_{name}", shape, dt))
        w3 = sb("w3", [P, E, CT, HIDDEN], F32)
        w2 = sb("w2", [P, E, HT, D], F32)
        score = sb("score", [E, NT], F32)
        left = sb("left", [E, ROUNDS + 1, NT], F32)
        top = sb("top", [E, ROUNDS, 8], F32)
        ntop = sb("ntop", [E, 1], F32)
        ex = sb("ex", [E, NT], F32)
        taken = sb("taken", [E, NT], F32)
        taken_ex = sb("taken_ex", [E, NT], F32)
        total = sb("total", [E, 1], F32)
        rden = sb("rden", [E, 1], F32)
        share_e = sb("share_e", [E, NT], F32)
        share = sb("share", [P, QT, E], F32)
        taken_t = sb("taken_t", [P, QT, E], F32)
        place_i = sb("place_i", [P, PLACES], I32)
        place_f = sb("place_f", [P, PLACES], F32)
        place = sb("place", [P, PLACES], F32)
        here = sb("here", [P, QT, E, PLACES], F32)
        picks = sb("picks", [P, QT, E, PLACES], F32)
        shares = sb("shares", [P, QT, E, PLACES], F32)
        chosen = sb("chosen", [P, CT, E * PLACES], F32)
        spread = sb("spread", [P, G, QT, P], F32)
        silu = sb("silu", [P, G, HIDDEN], F32)
        hid = sb("hid", [P, G, HIDDEN], F32)
        hidT = sb("hidT", [P, G, HT, P], F32)
        result = sb("result", [P, G, D], F32)
        block = ctx.enter_context(nc.Block())

        @block.sync
        def _(sp):
            for g in range(G):
                weights.load_group(sp, 3, w3, g, "up")
            for g in range(G):
                weights.load_group(sp, 2, w2, g, "down")

        @block.gpsimd
        def _(pool):
            pool.iota(place_i[:, :], pattern=[[1, PLACES]], base=1, channel_multiplier=0).then_inc(S("placing"), 1)
            pool.wait_ge(S("placing"), 1)
            pool.tensor_copy(place_f[:, :], place_i[:, :]).then_inc(S("placing"), 1)
            pool.wait_ge(S("placing"), 2)
            pool.tensor_scalar(place[:, :], place_f[:, :], 0.5, None, ALU.mult).then_inc(S("place"), 1)
            pool.wait_ge(S("place"), 1)
            norm_pool(c, pool, S)

        @block.tensor
        def _(pe):
            keep_warm(c, pe, NORM_FILL)
            pe.wait_ge(S("norm_done"), QT)
            turn_pe(c, pe, S, c.xn, 0, "turned")
            pe.wait_ge(S("xT_ready"), 1)
            pe.wait_ge(S("router"), 16)
            for ct in range(CT):
                ins = pe.matmul(c.ps[0:E, 7, 0:NT], weights.router[:, ct, :], c.xT[:, ct, :],
                                start=(ct == 0), stop=(ct == CT - 1))
            ins.then_inc(S("scores"), 1)
            keep_warm(c, pe, TOP_FILL, 6)
            pe.wait_ge(S("taken_found"), 1)
            for t in range(QT):
                ins = pe.transpose(c.ps[:, 0, t * E:(t + 1) * E], taken[:, t * P:(t + 1) * P], c.ident[0:E, 0:E])
            ins.then_inc(S("taken_turned"), 1)
            pe.wait_ge(S("taken_copied"), 1)
            for t in range(QT):
                for m in range(t + 1):
                    ins = pe.matmul(c.ps[:, 1, t * E:(t + 1) * E], c.tri[:, (t + m) * P:(t + m + 1) * P], taken_t[:, m, :],
                                    start=(m == 0), stop=(m == t))
            ins.then_inc(S("counted"), 1)
            pe.wait_ge(S("share_found"), 1)
            for t in range(QT):
                ins = pe.transpose(c.ps[:, 2, t * E:(t + 1) * E], share_e[:, t * P:(t + 1) * P], c.ident[0:E, 0:E])
            ins.then_inc(S("share_turned"), 1)
            pe.wait_ge(S("picked"), 1)
            for ct in range(CT):
                for t in range(QT):
                    ins = pe.matmul(c.ps[:, 3, ct * NT:(ct + 1) * NT], c.xn[:, t, ct * P:(ct + 1) * P],
                                    picks[:, t, :, :].rearrange("p e j -> p (e j)"), start=(t == 0), stop=(t == QT - 1))
            ins.then_inc(S("chosen_psum"), 1)
            pe.wait_ge(S("shares_spread"), 1)
            for g in range(G):
                for t in range(QT):
                    ins = pe.transpose(c.ps[:, 0, (g * QT + t) * P:(g * QT + t + 1) * P],
                                       shares[:, t, g * EG:(g + 1) * EG, :].rearrange("p e j -> p (e j)"), c.ident[:, :])
            ins.then_inc(S("shares_turned"), 1)
            pe.wait_ge(S("chosen_ready"), 1)
            for g in range(G):
                pe.wait_ge(S(f"up{g}"), 32)
                for w, bank, name in ((w1, 4, "gate_psum"), (w3, 6, "up_psum")):
                    for ct in range(CT):
                        for i in range(EG):
                            e = g * EG + i
                            ins = pe.matmul(c.ps[32 * i:32 * i + 32, bank + g, :], chosen[:, ct, e * PLACES:(e + 1) * PLACES],
                                            w[:, e, ct, :], start=(ct == 0), stop=(ct == CT - 1), skip_group_check=True)
                    ins.then_inc(S(name), 1)
            for g in range(G):
                pe.wait_ge(S("gated"), g + 1)
                for m in range(HT):
                    ins = pe.transpose(c.ps[:, 1 + g, m * P:(m + 1) * P], hid[:, g, m * P:(m + 1) * P], c.ident[:, :])
                ins.then_inc(S("hid_turned"), 1)
            for g in range(G):
                pe.wait_ge(S(f"down{g}"), 16)
                pe.wait_ge(S("hidT_ready"), g + 1)
                for m in range(HT):
                    for i in range(EG):
                        ins = pe.matmul(c.ps[32 * i:32 * i + 32, 6 + g, 0:D], hidT[:, g, m, 32 * i:32 * i + 32],
                                        w2[:, g * EG + i, m, :], start=(m == 0), stop=(m == HT - 1), skip_group_check=True)
                ins.then_inc(S("down_psum"), 1)
            pe.wait_ge(S("spread_ready"), 1)
            pe.wait_ge(S("result_ready"), G)
            for t in range(QT):
                for g in range(G):
                    ins = pe.matmul(c.ps[:, 3, t * D:(t + 1) * D], spread[:, g, t, :], result[:, g, :],
                                    start=(g == 0), stop=(g == G - 1))
            ins.then_inc(S("out_psum"), 1)

        @block.scalar
        def _(act):
            turn_act(c, act, S)
            act.wait_ge(S("top_found"), 1)
            act.activation(ex[:, :], score[:, :], ACT.Exp, bias=ntop[:, :]).then_inc(S("exp_done"), 1)
            act.wait_ge(S("chosen_psum"), 1)
            act.activation(chosen[:, :, :], c.ps[:, 3, :].rearrange("p (t n) -> p t n", t=CT), ACT.Copy)\
               .then_inc(S("chosen_ready"), 1)
            act.wait_ge(S("shares_turned"), 1)
            act.activation(spread[:, :, :, :], c.ps[:, 0, :].rearrange("p (g t n) -> p g t n", g=G, t=QT), ACT.Copy)\
               .then_inc(S("spread_ready"), 1)
            for g in range(G):
                act.wait_ge(S("gate_psum"), g + 1)
                act.activation(silu[:, g, :], c.ps[:, 4 + g, :], ACT.Silu).then_inc(S("silu_done"), 1)
            for g in range(G):
                act.wait_ge(S("hid_turned"), g + 1)
                act.activation(hidT[:, g, :, :], c.ps[:, 1 + g, :].rearrange("p (m n) -> p m n", m=HT), ACT.Copy)\
                   .then_inc(S("hidT_ready"), 1)
            for g in range(G):
                act.wait_ge(S("down_psum"), g + 1)
                act.activation(result[:, g, :], c.ps[:, 6 + g, 0:D], ACT.Copy).then_inc(S("result_ready"), 1)

        @block.vector
        def _(dve):
            by_place = lambda a: a.unsqueeze(3).to_broadcast((P, QT, E, PLACES))
            two = lambda bank: c.ps[:, bank, 0:QT * E].rearrange("p (t e) -> p t e", t=QT)
            norm_dve(c, dve, S, c.x, c.xn)
            link = Chain(dve, S("step"))
            dve.wait_ge(S("scores"), 1)
            link(dve.tensor_copy(score[:, :], c.ps[0:E, 7, 0:NT]))
            link(dve.tensor_copy(left[:, 0, :], score[:, :]))
            for r in range(ROUNDS):
                link(dve.max(top[:, r, :], left[:, r, :]))
                if r == 0:
                    dve.tensor_scalar(ntop[:, :], top[:, 0, 0:1], -1.0, None, ALU.mult).then_inc(S("top_found"), 1)
                link(dve.match_replace(out=left[:, r + 1, :], in_to_replace=top[:, r, :], in_values=left[:, r, :],
                                       imm_value=TAKEN))
            dve.tensor_scalar(taken[:, :], left[:, ROUNDS, :], 0.9 * TAKEN, None, ALU.is_lt).then_inc(S("taken_found"), 1)
            dve.wait_ge(S("taken_found"), 1)
            dve.wait_ge(S("exp_done"), 1)
            link(dve.tensor_tensor(taken_ex[:, :], taken[:, :], ex[:, :], ALU.mult))
            dve.wait_ge(S("taken_turned"), 1)
            dve.tensor_copy(taken_t[:, :, :], two(0)).then_inc(S("taken_copied"), 1)
            link(dve.tensor_reduce(total[:, :], taken_ex[:, :], AX.X, ALU.add))
            link(dve.reciprocal(rden[:, :], total[:, :]))
            dve.tensor_scalar(share_e[:, :], taken_ex[:, :], rden[:, :], None, ALU.mult).then_inc(S("share_found"), 1)
            dve.wait_ge(S("counted"), 1)
            dve.wait_ge(S("place"), 1)
            link(dve.tensor_tensor(here[:, :, :, :], by_place(two(1)),
                                   place[:, :].unsqueeze(1).unsqueeze(1).to_broadcast((P, QT, E, PLACES)), ALU.is_equal))
            dve.wait_ge(S("taken_copied"), 1)
            dve.tensor_tensor(picks[:, :, :, :], here[:, :, :, :], by_place(taken_t[:, :, :]), ALU.mult)\
               .then_inc(S("picked"), 1)
            dve.wait_ge(S("share_turned"), 1)
            dve.tensor_tensor(shares[:, :, :, :], here[:, :, :, :], by_place(two(2)), ALU.mult)\
               .then_inc(S("shares_spread"), 1)
            for g in range(G):
                dve.wait_ge(S("silu_done"), g + 1)
                dve.wait_ge(S("up_psum"), g + 1)
                dve.tensor_tensor(hid[:, g, :], c.ps[:, 6 + g, :], silu[:, g, :], ALU.mult).then_inc(S("gated"), 1)
            dve.wait_ge(S("out_psum"), 1)
            add_stream_dve(c, dve, S, 3)


def plain_attention(c):
    nc = c.nc
    with ExitStack() as ctx:
        S = Sems(nc, ctx, "plain")
        sb = lambda name, shape, dt: ctx.enter_context(nc.sbuf_tensor(f"s_{name}", shape, dt))
        w = sb("w", [P, 4, CT, D], F32)
        b = sb("b", [1, 4, D], F32)
        qT = sb("qT", [P, CT, NT], F32)
        kT = sb("kT", [P, CT, NT], F32)
        v = sb("v", [P, QT, D], F32)
        ntop = sb("ntop", [P, QT], F32)
        p = sb("p", [P, QT, NT], F32)
        total = sb("total", [P, QT], F32)
        pT = sb("pT", [P, QT, NT], F32)
        oT = sb("oT", [P, CT, NT], F32)
        block = ctx.enter_context(nc.Block())

        @block.sync
        def _(sp):
            sp.dma_start(b[:, :, :], c.a["s_b"]).then_inc(S("weights"), 16)
            for k in range(4):
                sp.dma_start(w[:, k, :, :], tiles(c.a["s_w"][k, :, :])).then_inc(S("weights"), 16)
            c.ops.load_first(sp, 3)

        @block.gpsimd
        def _(pool):
            norm_pool(c, pool, S)

        @block.tensor
        def _(pe):
            keep_warm(c, pe, NORM_FILL)
            pe.wait_ge(S("norm_done"), QT)
            turn_pe(c, pe, S, c.xn, 0, "turned")
            pe.wait_ge(S("xT_ready"), 1)
            pe.wait_ge(S("weights"), 80)
            for k, name in ((0, "q_psum"), (1, "k_psum")):
                for m in range(CT):
                    ins = by_channels_pe(c, pe, c.ps[:, 1 + k, m * NT:(m + 1) * NT],
                                         lambda ct: w[:, k, ct, m * P:(m + 1) * P], c.xT, b[0:1, k, m * P:(m + 1) * P])
                ins.then_inc(S(name), 1)
            by_tokens_pe(c, pe, halves(c, 3), c.xT, w[:, 2, :, :], b[0:1, 2, :]).then_inc(S("v_psum"), 1)
            pe.wait_ge(S("q_ready"), 1)
            pe.wait_ge(S("k_ready"), 1)
            for t in range(QT):
                for ct in range(CT):
                    ins = pe.matmul(c.ps[:, 4, t * NT:(t + 1) * NT], qT[:, ct, t * P:(t + 1) * P], kT[:, ct, :],
                                    start=(ct == 0), stop=(ct == CT - 1))
            ins.then_inc(S("s_psum"), 1)
            pe.wait_ge(S("p_scaled"), QT)
            turn_pe(c, pe, S, p, 5, "p_turned")
            pe.wait_ge(S("pT_ready"), 1)
            pe.wait_ge(S("v_ready"), 1)
            for m in range(CT):
                for k in range(QT):
                    ins = pe.matmul(c.ps[:, 6, m * NT:(m + 1) * NT], v[:, k, m * P:(m + 1) * P], pT[:, k, :],
                                    start=(k == 0), stop=(k == QT - 1))
            ins.then_inc(S("o_psum"), 1)
            pe.wait_ge(S("oT_ready"), 1)
            by_tokens_pe(c, pe, halves(c, 7), oT, w[:, 3, :, :], b[0:1, 3, :]).then_inc(S("out_psum"), 1)

        @block.scalar
        def _(act):
            turn_act(c, act, S)
            act.wait_ge(S("q_psum"), 1)
            act.mul(qT[:, :, :], c.ps[:, 1, :].rearrange("p (m n) -> p m n", n=NT), D ** -0.5).then_inc(S("q_ready"), 1)
            act.wait_ge(S("v_psum"), 1)
            act.activation(v[:, :, :], c.ps[:, 3, :].rearrange("p (m n) -> p m n", n=NT), ACT.Copy).then_inc(S("v_ready"), 1)
            act.wait_ge(S("top_found"), 1)
            for t in range(QT):
                act.activation(p[:, t, :], c.ps[:, 4, t * NT:(t + 1) * NT], ACT.Exp, bias=ntop[:, t:t + 1],
                               accum_out=total[:, t:t + 1]).then_inc(S("exp_done"), 1)
            act.wait_ge(S("p_turned"), 1)
            act.activation(pT[:, :, :], c.ps[:, 5, :].rearrange("p (m n) -> p m n", n=NT), ACT.Copy)\
               .then_inc(S("pT_ready"), 1)
            act.wait_ge(S("o_psum"), 1)
            act.activation(oT[:, :, :], c.ps[:, 6, :].rearrange("p (m n) -> p m n", n=NT), ACT.Copy)\
               .then_inc(S("oT_ready"), 1)

        @block.vector
        def _(dve):
            norm_dve(c, dve, S, c.x, c.xn)
            dve.wait_ge(S("k_psum"), 1)
            dve.tensor_copy(kT[:, :, :], c.ps[:, 2, :].rearrange("p (m n) -> p m n", n=NT)).then_inc(S("k_ready"), 1)
            dve.wait_ge(S("s_psum"), 1)
            dve.tensor_reduce(ntop[:, :], c.ps[:, 4, :].rearrange("p (t k) -> p t k", t=QT), AX.X, ALU.max, negate=True)\
               .then_inc(S("top_found"), 1)
            dve.wait_ge(S("exp_done"), QT)
            link = Chain(dve, S("step"))
            link(dve.reciprocal(total[:, :], total[:, :]))
            for t in range(QT):
                dve.tensor_scalar(p[:, t, :], p[:, t, :], total[:, t:t + 1], None, ALU.mult).then_inc(S("p_scaled"), 1)
            dve.wait_ge(S("out_psum"), 1)
            add_stream_dve(c, dve, S, 7)


def zone_experts(c):
    nc = c.nc
    CENTER, LOWER, UPPER = 1.0 / math.e, 0.5 - math.log(4.0 / 3.0), 0.5
    FLOOR = 1e-8
    HIDDEN = 256
    HT = HIDDEN // P
    with ExitStack() as ctx:
        S = Sems(nc, ctx, "zone")
        sb = lambda name, shape, dt: ctx.enter_context(nc.sbuf_tensor(f"z_{name}", shape, dt))
        router = sb("router", [P, CT, E], F32)
        temp = sb("temp", [P, 1], F32)
        w1 = sb("w1", [P, E, CT, HIDDEN], F32)
        w3 = sb("w3", [P, E, CT, HIDDEN], F32)
        w2 = sb("w2", [P, E, HT, D], F32)
        hidden = sb("hidden", [P, 2, HT, NT], F32)
        silu = sb("silu", [P, 2, 2 * NT], F32)
        te = lambda name: sb(name, [P, QT, E], F32)
        inh, zone, off, dist, near, fallback = (te(n) for n in ("inh", "zone", "off", "dist", "near", "fallback"))
        picked, second, share = te("picked"), te("second"), te("share")
        total = sb("total", [P, QT], F32)
        none = sb("none", [P, QT], F32)
        some = sb("some", [P, QT], F32)
        top = sb("top", [P, QT, 8], F32)
        where = sb("where", [P, QT, 8], U32)
        where_f = sb("where_f", [P, QT, 2], F32)
        c.hT = lambda e: hidden[:, e % 2, :, :]
        block = ctx.enter_context(nc.Block())

        @block.sync
        def _(sp):
            sp.dma_start(router[:, :, :], tiles(c.a["z_router"])).then_inc(S("router"), 16)
            sp.dma_start(temp[:, :], c.a["z_temp"].to_broadcast((P, 1))).then_inc(S("router"), 16)
            load_experts(c, sp, S, "z", w1, w3, w2)

        @block.gpsimd
        def _(pool):
            norm_pool(c, pool, S)

        @block.tensor
        def _(pe):
            keep_warm(c, pe, NORM_FILL)
            pe.wait_ge(S("norm_done"), QT)
            turn_pe(c, pe, S, c.xn, 0, "turned")
            pe.wait_ge(S("xT_ready"), 1)
            pe.wait_ge(S("router"), 32)
            by_tokens_pe(c, pe, [c.ps[:, 7, t * E:(t + 1) * E] for t in range(QT)], c.xT, router, None)\
                .then_inc(S("logits"), 1)
            experts_pe(c, pe, S, w1, w3, w2, HT)

        @block.scalar
        def _(act):
            turn_act(c, act, S)
            act.wait_ge(S("logits"), 1)
            act.wait_ge(S("temp_inverted"), 1)
            act.activation(inh[:, :, :], c.ps[:, 7, 0:QT * E].rearrange("p (t e) -> p t e", t=QT), ACT.Sigmoid,
                           scale=temp[:, 0:1]).then_inc(S("inhibited"), 1)
            act.wait_ge(S("dist_found"), 1)
            act.activation(near[:, :, :], dist[:, :, :], ACT.Exp, scale=-1.0 / 0.1).then_inc(S("near_found"), 1)
            act.activation(fallback[:, :, :], dist[:, :, :], ACT.Exp, scale=-1.0 / 0.3).then_inc(S("near_found"), 1)
            experts_act(c, act, S, HT, silu)

        @block.vector
        def _(dve):
            dve.wait_ge(S("router"), 32)
            dve.reciprocal(temp[:, :], temp[:, :]).then_inc(S("temp_inverted"), 1)
            norm_dve(c, dve, S, c.x, c.xn)
            link = Chain(dve, S("step"))
            wide = lambda a: a.unsqueeze(2).to_broadcast((P, QT, E))
            dve.wait_ge(S("inhibited"), 1)
            link(dve.tensor_scalar(off[:, :, :], inh[:, :, :], CENTER, None, ALU.subtract))
            dve.scalar_tensor_tensor(out=dist[:, :, :], in0=off[:, :, :], scalar=-1.0, in1=off[:, :, :], op0=ALU.mult,
                                     op1=ALU.max).then_inc(S("dist_found"), 1)
            link(dve.tensor_scalar(zone[:, :, :], inh[:, :, :], LOWER, None, ALU.is_ge))
            link(dve.scalar_tensor_tensor(out=zone[:, :, :], in0=inh[:, :, :], scalar=UPPER, in1=zone[:, :, :],
                                          op0=ALU.is_le, op1=ALU.mult))
            dve.wait_ge(S("near_found"), 2)
            link(dve.tensor_tensor(near[:, :, :], near[:, :, :], zone[:, :, :], ALU.mult))
            link(dve.tensor_reduce(total[:, :], near[:, :, :], AX.X, ALU.add))
            link(dve.tensor_scalar(none[:, :], total[:, :], FLOOR, None, ALU.is_lt))
            link(dve.tensor_scalar(some[:, :], none[:, :], -1.0, 1.0, ALU.mult, ALU.add))
            for t in range(QT):
                link(dve.max(top[:, t, :], fallback[:, t, :]))
                link(dve.max_index(where[:, t, :], top[:, t, :], fallback[:, t, :]))
            link(dve.tensor_copy(where_f[:, :, :], where[:, :, 0:2]))
            for t in range(QT):
                link(dve.tensor_scalar(picked[:, t, :], c.count8[:, :], where_f[:, t, 0:1], None, ALU.is_equal))
                link(dve.scalar_tensor_tensor(out=second[:, t, :], in0=c.count8[:, :], scalar=where_f[:, t, 1:2],
                                              in1=picked[:, t, :], op0=ALU.is_equal, op1=ALU.add))
            link(dve.tensor_tensor(fallback[:, :, :], fallback[:, :, :], second[:, :, :], ALU.mult))
            link(dve.tensor_reduce(total[:, :], fallback[:, :, :], AX.X, ALU.add))
            link(dve.tensor_scalar(total[:, :], total[:, :], FLOOR, None, ALU.max))
            link(dve.reciprocal(total[:, :], total[:, :]))
            link(dve.tensor_tensor(total[:, :], total[:, :], none[:, :], ALU.mult))
            link(dve.tensor_tensor(fallback[:, :, :], fallback[:, :, :], wide(total[:, :]), ALU.mult))
            link(dve.tensor_tensor(near[:, :, :], near[:, :, :], wide(some[:, :]), ALU.mult))
            link(dve.tensor_tensor(near[:, :, :], near[:, :, :], fallback[:, :, :], ALU.add))
            link(dve.tensor_reduce(total[:, :], near[:, :, :], AX.X, ALU.add))
            link(dve.tensor_scalar(total[:, :], total[:, :], FLOOR, None, ALU.max))
            link(dve.reciprocal(total[:, :], total[:, :]))
            link(dve.tensor_tensor(share[:, :, :], near[:, :, :], wide(total[:, :]), ALU.mult))
            experts_dve(c, dve, S, HT, silu, share)


def recurrence(c):
    nc = c.nc
    with ExitStack() as ctx:
        S = Sems(nc, ctx, "gru")
        sb = lambda name, shape, dt: ctx.enter_context(nc.sbuf_tensor(f"r_{name}", shape, dt))
        w = sb("w", [P, 2, CT, D], F32)
        b = sb("b", [1, 2, D], F32)
        gb = sb("gb", [P, 2, D], F32)
        z = sb("z", [P, CT, NT], F32)
        keep = sb("keep", [P, CT, NT], F32)
        zc = sb("zc", [P, CT, NT], F32)
        hT = sb("hT", [P, CT, NT], F32)
        block = ctx.enter_context(nc.Block())

        @block.sync
        def _(sp):
            sp.dma_start(gb[:, 0, :], c.a["r_g"].to_broadcast((P, D))).then_inc(S("scales"), 16)
            sp.dma_start(gb[:, 1, :], c.a["r_b"].to_broadcast((P, D))).then_inc(S("scales"), 16)
            sp.dma_start(b[:, :, :], c.a["r_bias"]).then_inc(S("weights"), 16)
            for k in range(2):
                sp.dma_start(w[:, k, :, :], tiles(c.a["r_w"][k, :, :])).then_inc(S("weights"), 16)

        @block.gpsimd
        def _(pool):
            norm_pool(c, pool, S)
            norm_pool(c, pool, S, 1)

        @block.tensor
        def _(pe):
            keep_warm(c, pe, 2 * NORM_FILL)
            pe.wait_ge(S("scaled"), 2 * QT)
            turn_pe(c, pe, S, c.att, 0, "turned")
            pe.wait_ge(S("xT_ready"), 1)
            pe.wait_ge(S("weights"), 48)
            for k, name in ((0, "z_psum"), (1, "c_psum")):
                for m in range(CT):
                    ins = by_channels_pe(c, pe, c.ps[:, 1 + k, m * NT:(m + 1) * NT],
                                         lambda ct: w[:, k, ct, m * P:(m + 1) * P], c.xT, b[0:1, k, m * P:(m + 1) * P])
                ins.then_inc(S(name), 1)
            pe.wait_ge(S("scanned"), CT)
            turn_pe(c, pe, S, hT, 3, "h_turned")

        @block.scalar
        def _(act):
            turn_act(c, act, S)
            act.wait_ge(S("z_psum"), 1)
            act.activation(z[:, :, :], c.ps[:, 1, :].rearrange("p (m n) -> p m n", n=NT), ACT.Sigmoid)\
               .then_inc(S("z_ready"), 1)

        @block.vector
        def _(dve):
            norm_dve(c, dve, S, c.x, c.xn)
            dve.wait_ge(S("norm_done"), QT)
            norm_dve(c, dve, S, c.xn, c.att, 1)
            scale_norm_dve(c, dve, S, gb)
            dve.tensor_tensor(c.x[:, :, :], c.x[:, :, :], c.xn[:, :, :], ALU.add).then_inc(S("norm_added"), 1)
            dve.wait_ge(S("z_ready"), 1)
            dve.tensor_scalar(keep[:, :, :], z[:, :, :], -1.0, 1.0, ALU.mult, ALU.add).then_inc(S("gates"), 1)
            dve.wait_ge(S("c_psum"), 1)
            dve.tensor_tensor(zc[:, :, :], c.ps[:, 2, :].rearrange("p (m n) -> p m n", n=NT), z[:, :, :], ALU.mult)\
               .then_inc(S("gates"), 1)
            dve.wait_ge(S("gates"), 2)
            for m in range(CT):
                dve.tensor_tensor_scan(hT[:, m, :], keep[:, m, :], zc[:, m, :], 0.0, ALU.mult, ALU.add)\
                   .then_inc(S("scanned"), 1)
            dve.wait_ge(S("h_turned"), 1)
            dve.wait_ge(S("norm_added"), 1)
            add_stream_dve(c, dve, S, 3)


def feed_forward(c):
    nc = c.nc
    HIDDEN = 1024
    HT = HIDDEN // P
    with ExitStack() as ctx:
        S = Sems(nc, ctx, "ffn")
        sb = lambda name, shape, dt: ctx.enter_context(nc.sbuf_tensor(f"g_{name}", shape, dt))
        w1 = sb("w1", [P, CT, HIDDEN], F32)
        w2 = sb("w2", [P, HT, D], F32)
        b1 = sb("b1", [P, HT], F32)
        b2 = sb("b2", [1, D], F32)
        hT = sb("hT", [P, HT, NT], F32)
        block = ctx.enter_context(nc.Block())

        @block.sync
        def _(sp):
            sp.dma_start(b1[:, :], c.a["g_b1"]).then_inc(S("w1"), 16)
            sp.dma_start(w1[:, :, :], tiles(c.a["g_w1"])).then_inc(S("w1"), 16)
            sp.dma_start(b2[:, :], c.a["g_b2"]).then_inc(S("w2"), 16)
            sp.dma_start(w2[:, :, :], tiles(c.a["g_w2"])).then_inc(S("w2"), 16)

        @block.gpsimd
        def _(pool):
            norm_pool(c, pool, S)

        @block.tensor
        def _(pe):
            keep_warm(c, pe, NORM_FILL)
            pe.wait_ge(S("norm_done"), QT)
            turn_pe(c, pe, S, c.xn, 0, "turned")
            pe.wait_ge(S("xT_ready"), 1)
            pe.wait_ge(S("w1"), 32)
            for m in range(HT):
                if m >= 6:
                    pe.wait_ge(S("gelu_done"), m - 5)
                by_channels_pe(c, pe, c.ps[:, 1 + m % 6, 0:NT], lambda ct: w1[:, ct, m * P:(m + 1) * P], c.xT)\
                    .then_inc(S("h_psum"), 1)
            pe.wait_ge(S("w2"), 32)
            pe.wait_ge(S("gelu_done"), HT)
            by_tokens_pe(c, pe, halves(c, 7), hT, w2, b2[:, :], HT).then_inc(S("out_psum"), 1)

        @block.scalar
        def _(act):
            turn_act(c, act, S)
            for m in range(HT):
                act.wait_ge(S("h_psum"), m + 1)
                act.activation(hT[:, m, :], c.ps[:, 1 + m % 6, 0:NT], ACT.Gelu, bias=b1[:, m:m + 1])\
                   .then_inc(S("gelu_done"), 1)

        @block.vector
        def _(dve):
            norm_dve(c, dve, S, c.x, c.xn)
            dve.wait_ge(S("out_psum"), 1)
            add_stream_dve(c, dve, S, 7)


def program(nc, a, out, steps=None):
    ctx = ExitStack()
    with ctx:
        c = Core()
        c.nc, c.a = nc, a
        sb = lambda name, shape, dt: ctx.enter_context(nc.sbuf_tensor(name, shape, dt))
        c.ps = ctx.enter_context(nc.psum_tensor("ps", [P, 8, 512], F32))
        c.x = sb("x", [P, QT, D], F32)
        c.xn = sb("xn", [P, QT, D], F32)
        c.xT = sb("xT", [P, CT, NT], F32)
        c.att = sb("att", [P, QT, D], F32)
        c.rows = sb("rows", [1, len(ROWS), D], F32)
        c.row = lambda name: c.rows[0:1, ROWS.index(name), :]
        c.wq = sb("wq", [P, CT, D], F32)
        c.wo = sb("wo", [P, CT, D], F32)
        c.ident = sb("ident", [P, P], F32)
        c.identb = sb("identb", [P, P], BF16)
        c.fold = sb("fold", [P, 32], F32)
        c.idle = sb("idle", [P, CHUNK], BF16)
        c.ones = sb("ones", [P, NT], F32)
        c.minus_half = sb("minus_half", [P, QT], F32)
        c.tri = sb("tri", [P, 3 * P], F32)
        c.den16 = sb("den16", [P, 32], F32)
        c.count8 = sb("count8", [P, E], F32)
        c.count8_i = sb("count8_i", [P, E], I32)
        c.stats = sb("stats", [P, QT, 6], F32)
        c.moments = sb("moments", [P, QT, 2], F32)
        c.var = sb("var", [P, QT], F32)
        c.rstd = sb("rstd", [P, QT], F32)
        c.kparts = nc.dram_tensor("kparts", (LAYERS, 3, D, KEYS), BF16).ap()
        c.qparts = nc.dram_tensor("qparts", (3 * HD, H, NT), BF16).ap()
        c.vals = nc.dram_tensor("vals", (LAYERS, P, KT * D), F32).ap()

        c.ops = Operands(c, ctx)
        constants(c)
        steps = 12 if steps is None else steps
        with ExitStack() as masks:
            sb = lambda name, shape, dt: masks.enter_context(nc.sbuf_tensor(name, shape, dt))
            c.neg_q = sb("neg_q", [P, QT, KEYS], BF16)
            c.neg_k = sb("neg_k", [P, KT, NT], BF16)
            with nc.sbuf_tensor("gT", [P, KT, NT], F32) as c.gT:
                project_context(c)
                cross(c, 0, True, True)
            taylor(c)
            first_expert(c)
            cross(c, 1, True, False)
        with ExitStack() as beside:
            weights = ChosenExperts(c, beside)
            frames(c, weights.load_first)
            experts_choose(c, weights)
        cross(c, 2, False, False)
        plain_attention(c)
        zone_experts(c)
        cross(c, 3, False, False)
        recurrence(c)
        feed_forward(c)
        store(c, out)


def cross(c, l, by_query, weighted):
    queries(c, l)
    attend(c, l, by_query, weighted)
    project_out(c, l)


def store(c, out):
    nc = c.nc
    with ExitStack() as ctx:
        S = Sems(nc, ctx, "end")
        block = ctx.enter_context(nc.Block())

        @block.sync
        def _(sp):
            sp.dma_start(out.rearrange("(t p) d -> p t d", p=P), c.x[:, :, :]).then_inc(S("stored"), 16)
            sp.wait_ge(S("stored"), 16)


ROWS = ["bq0", "bq1", "bq2", "bq3", "bo0", "bo1", "bo2", "bo3"]


def kernel(**inputs):
    import numpy as np
    import concourse.bacc as bacc
    from concourse.bass_utils import run_bass_kernel_spmd

    arrays = lay_out(inputs, np)
    nc = bacc.Bacc("TRN2", target_bir_lowering=False, num_devices=1)
    a = {name: nc.dram_tensor(f"in_{name}", v.shape, mybir.dt.from_np(v.dtype), kind="ExternalInput").ap()
         for name, v in arrays.items()}
    out = nc.dram_tensor("out", (NT, D), F32, kind="ExternalOutput").ap()
    program(nc, a, out)
    r = run_bass_kernel_spmd(nc, [{f"in_{name}": v for name, v in arrays.items()}], core_ids=[0])
    return r.results[0]["out"].reshape(1, NT, D)


def lay_out(inputs, np):
    i = {k: np.asarray(v) for k, v in inputs.items()}
    stack = lambda names, turn=(): np.ascontiguousarray(
        np.stack([i[n].T if n in turn else i[n] for n in names]))
    names = {"q": ["L0_xattn_wq_k", "L1_xattn_wq_kernel", "L2_xattn_Wq", "L3_xattn_Wq"],
             "k": ["L0_xattn_wk_k", "L1_xattn_wk_kernel", "L2_xattn_Wk", "L3_xattn_Wk"],
             "v": ["L0_xattn_wv_k", "L1_xattn_wv_kernel", "L2_xattn_Wv", "L3_xattn_Wv"],
             "o": ["L0_xattn_wo_k", "L1_xattn_wo_kernel", "L2_xattn_Wo", "L3_xattn_Wo"]}
    bias = {w: [f"L0_xattn_w{w}_b", f"L1_xattn_w{w}_bias", f"L2_xattn_b{w}", f"L3_xattn_b{w}"] for w in "qkvo"}
    out = {f"w{w}4": stack(n, turn=n[2:]) for w, n in names.items()}
    turned_heads = lambda a: np.ascontiguousarray(a.reshape(*a.shape[:-1], H, HD).swapaxes(-1, -2).reshape(a.shape))
    out["wq4"] = turned_heads(out["wq4"])
    out["bk4"] = np.ascontiguousarray(stack(bias["k"]).reshape(LAYERS, CT, P).transpose(0, 2, 1))
    out["bv4"] = stack(bias["v"])
    out["x"] = i["x"][0]
    out["ctxT"] = np.ascontiguousarray(i["ctx_1024"][0].T)
    out["gT"] = np.ascontiguousarray(i["fside_BxSxS2_0"][0].T)
    out["mask"] = i["mask_BxSxS2_ik1"][0]
    out["maskT"] = np.ascontiguousarray(i["mask_BxSxS2_ik1"][0].T)
    out["mask_keys"] = np.ascontiguousarray(i["mask_Bx1xS2_bf1"][0]).view(np.uint8)
    for w in "qk":
        spaced = np.zeros((D, H, 32), np.float32)
        spaced[:, :, :HD] = i[f"L0_attn_W{w}"].T.reshape(D, H, HD)
        out[f"t_w{w}"] = spaced.reshape(D, H * 32)
    for w in "vo":
        out[f"t_w{w}"] = np.ascontiguousarray(i[f"L0_attn_W{w}"].T)
    out["f_router"] = i["L0_ffn_router_w"]
    out["f_router_b"] = i["L0_ffn_router_b"][None]
    out["f_bias"] = i["L0_ffn_expert_b"][None]
    out["f_w"] = i["L0_ffn_expert_w"]
    out["m_g"], out["m_b"] = i["L1_attn_g"][0], i["L1_attn_b"][0]
    out["m_w"], out["m_wo"], out["m_bo"] = i["L1_attn_w_qkv"], i["L1_attn_w_out"], i["L1_attn_b_out"][None]
    turned = lambda a: np.ascontiguousarray(a.transpose(0, 2, 1))
    out["e_router"] = np.ascontiguousarray(i["L1_ffn_Wg"].T)
    for n in "123":
        out[f"e_w{n}"] = turned(i[f"L1_ffn_W{n}"])
    out["s_w"] = np.stack([i[f"L2_attn_W{n}"] for n in "1234"])
    out["s_b"] = np.stack([i[f"L2_attn_b{n}"] for n in "1234"])[None]
    out["z_router"], out["z_temp"] = i["L2_ffn_Wr"], i["L2_ffn_temperature"][None]
    out["z_w1"], out["z_w3"], out["z_w2"] = i["L2_ffn_Wg"], i["L2_ffn_Wu"], i["L2_ffn_Wd"]
    out["r_g"], out["r_b"] = i["L3_attn_gamma"][None], i["L3_attn_beta"][None]
    out["r_w"] = np.stack([i["L3_attn_Wg"].T, i["L3_attn_Wc"].T])
    out["r_bias"] = np.stack([i["L3_attn_bg"], i["L3_attn_bc"]])[None]
    out["g_w1"], out["g_w2"], out["g_b2"] = i["L3_ffn_w1"], i["L3_ffn_w2"], i["L3_ffn_b2"][None]
    out["g_b1"] = np.ascontiguousarray(i["L3_ffn_b1"].reshape(-1, P).T)
    rows = [turned_heads(i[n]) for n in bias["q"]] + [i[n] for n in bias["o"]]
    out["rows"] = np.stack(rows)[None]
    return out
```
